# Optimizing a Trainium2 kernel written in Bass

```python
import numpy as np
import jax
import jax.numpy as jnp

def _softmax(x, axis=-1):
    return jax.nn.softmax(x, axis=axis)

def _gelu(x):
    return jax.nn.gelu(x, approximate=True)

def _silu(x):
    return jax.nn.silu(x)

def _sigmoid(x):
    return jax.nn.sigmoid(x)

def _layernorm(x, axis=-1, eps=1e-05):
    m = jnp.mean(x, axis=axis, keepdims=True)
    v = jnp.var(x, axis=axis, keepdims=True)
    return (x - m) / jnp.sqrt(v + eps)

def _scatter_add(tgt, idx, src, axis=0):
    return tgt.at[idx].add(src)

def _segment_sum(src, seg, n):
    return jax.ops.segment_sum(src, seg, n)
kernel_name = 'mk_decoder_postln_d2_seqx_r8_a964a9'

def setup_inputs(seed: int=0):
    np.random.seed(seed)
    _w = jnp.asarray

    def _rec_inputs():
        import jax
        import jax.numpy as jnp
        _rk = jax.random.key(seed)
        x = -0.0003929 + 0.9999 * jax.random.normal(jax.random.fold_in(_rk, 1), (16, 128, 128), jnp.float32)
        _lenS = 128 - jax.random.randint(jax.random.fold_in(_rk, 7), (16,), 0, max(1, 128 // 4) + 1, jnp.int32)
        _lenS2 = 128 - jax.random.randint(jax.random.fold_in(_rk, 8), (16,), 0, max(1, 128 // 4) + 1, jnp.int32)
        _ctx_1024P = jax.random.normal(jax.random.fold_in(_rk, 11), (16, 16, 128), jnp.float32)
        _ctx_1024c = jax.random.dirichlet(jax.random.fold_in(_rk, 511), 0.3 * jnp.ones((16,), jnp.float32), (16, 128))
        _ctx_1024t = jnp.einsum('bsk,bkd->bsd', _ctx_1024c, _ctx_1024P)
        _ctx_1024t = _ctx_1024t * jax.lax.rsqrt(jnp.mean(jnp.square(_ctx_1024t)) + 1e-12) * 0.953939
        ctx_1024 = 2.81802e-05 + 1.00001 * (_ctx_1024t + 0.3 * jax.random.normal(jax.random.fold_in(_rk, 611), (16, 128, 128), jnp.float32))
        _validS = jnp.arange(128)[None, :] < _lenS[:, None]
        _validS2 = jnp.arange(128)[None, :] < _lenS2[:, None]
        _causal = jnp.tril(jnp.ones((128, 128), dtype=bool))
        mask_Bx1xSxS2_if1 = jnp.where(jnp.ones((16, 1, 128, 128), dtype=bool), 1, 0).astype(jnp.int32)
        return (x, ctx_1024, mask_Bx1xSxS2_if1)
    x, ctx_1024, mask_Bx1xSxS2_if1 = _rec_inputs()

    def _L0_attn_setup():
        import jax, jax.numpy as jnp
        import numpy as np
        EMB = 128
        HEADS = 16
        HEAD_DIM = EMB // HEADS
        MAX_LEN = 125
        key = jax.random.key(seed)
        ks = jax.random.split(key, 11)
        s = 0.02
        x = jax.random.normal(ks[0], (4, 128, EMB), dtype=jnp.float32)
        Wq = jax.random.normal(ks[1], (EMB, EMB), dtype=jnp.float32) * s
        bq = jnp.zeros((EMB,), dtype=jnp.float32)
        Wk = jax.random.normal(ks[2], (EMB, EMB), dtype=jnp.float32) * s
        bk = jnp.zeros((EMB,), dtype=jnp.float32)
        Wv = jax.random.normal(ks[3], (EMB, EMB), dtype=jnp.float32) * s
        bv = jnp.zeros((EMB,), dtype=jnp.float32)
        Wp = jax.random.normal(ks[4], (EMB, EMB), dtype=jnp.float32) * s
        bp = jnp.zeros((EMB,), dtype=jnp.float32)
        bias_table = jax.random.normal(ks[5], (2 * MAX_LEN - 1, HEADS), dtype=jnp.float32) * 0.02
        temperature = jnp.ones((1,), dtype=jnp.float32)
        return {'x': x, 'Wq': Wq, 'bq': bq, 'Wk': Wk, 'bk': bk, 'Wv': Wv, 'bv': bv, 'Wp': Wp, 'bp': bp, 'bias_table': bias_table, 'temperature': temperature}
    _L0_attn_all = _L0_attn_setup()
    _L0_attn_in = {k: v for k, v in _L0_attn_all.items() if k in ('Wq', 'bq', 'Wk', 'bk', 'Wv', 'bv', 'Wp', 'bp', 'bias_table', 'temperature')}
    del _L0_attn_all

    def _L0_xattn_setup():
        import jax, jax.numpy as jnp
        import numpy as np
        import math
        B, S, D = (8, 256, 128)
        key = jax.random.key(seed)
        ks = jax.random.split(key, 8)
        s_in = 1.0 / math.sqrt(D)
        s_ent = 1.0 / math.sqrt(2 * D)
        return {'x': jax.random.normal(ks[0], (B, S, D), dtype=jnp.float32), 'context': jax.random.normal(ks[1], (B, S, D), dtype=jnp.float32), 'Wq': jax.random.normal(ks[2], (D, D), dtype=jnp.float32) * s_in, 'bq': jnp.zeros((D,), jnp.float32), 'Wk': jax.random.normal(ks[3], (D, D), dtype=jnp.float32) * s_in, 'bk': jnp.zeros((D,), jnp.float32), 'Wv': jax.random.normal(ks[4], (D, D), dtype=jnp.float32) * s_in, 'bv': jnp.zeros((D,), jnp.float32), 'We': jax.random.normal(ks[5], (D, 2 * D), dtype=jnp.float32) * s_ent, 'be': jnp.zeros((D,), jnp.float32)}
    _L0_xattn_all = _L0_xattn_setup()
    _L0_xattn_in = {k: v for k, v in _L0_xattn_all.items() if k in ('Wq', 'bq', 'Wk', 'bk', 'Wv', 'bv', 'We', 'be')}
    del _L0_xattn_all

    def _L0_ffn_setup():
        import jax, jax.numpy as jnp
        import numpy as np
        B, S, D, FF, E, L = (8, 256, 128, 512, 16, 4)

        def _unipool_layer(xt, router, W1, W2):
            logits = xt @ router
            probs = jax.nn.softmax(logits, axis=-1)
            w = jnp.max(probs, axis=-1)
            idx = jnp.argmax(probs, axis=-1)

            def body(acc, params):
                w1, w2, i = params
                h = jax.nn.silu(xt @ w1) @ w2
                sel = jnp.where(idx == i, w, 0.0)
                return (acc + sel[:, None] * h, None)
            out, _ = jax.lax.scan(body, jnp.zeros_like(xt), (W1, W2, jnp.arange(W1.shape[0])))
            return out
        key = jax.random.key(seed)
        k0, k1, k2, k3 = jax.random.split(key, 4)
        x = jax.random.normal(k0, (B, S, D), dtype=jnp.float32)
        routers = jax.random.normal(k1, (L, D, E), dtype=jnp.float32) * 0.02
        W1 = jax.random.normal(k2, (E, D, FF), dtype=jnp.float32) * 0.02
        W2 = jax.random.normal(k3, (E, FF, D), dtype=jnp.float32) * 0.02
        return {'x': x, 'routers': routers, 'W1': W1, 'W2': W2}
    _L0_ffn_all = _L0_ffn_setup()
    _L0_ffn_in = {k: v for k, v in _L0_ffn_all.items() if k in ('routers', 'W1', 'W2')}
    del _L0_ffn_all

    def _L1_attn_setup():
        import jax, jax.numpy as jnp
        import numpy as np
        DIM = 128
        NUM_HEADS = 16
        DIM_HEAD = DIM // NUM_HEADS

        def _softmax(logits, axis=-1):
            logits = logits - jnp.max(logits, axis=axis, keepdims=True)
            e = jnp.exp(logits)
            return e / jnp.sum(e, axis=axis, keepdims=True)
        key = jax.random.key(seed)
        kx, kq, kk, kv, ko = jax.random.split(key, 5)
        s = 1.0 / np.sqrt(DIM)
        return {'x': jax.random.normal(kx, (4, 256, DIM), dtype=jnp.float32), 'Wq': jax.random.uniform(kq, (DIM, DIM), jnp.float32, -s, s), 'Wk': jax.random.uniform(kk, (DIM, DIM), jnp.float32, -s, s), 'Wv': jax.random.uniform(kv, (DIM, DIM), jnp.float32, -s, s), 'Wo': jax.random.uniform(ko, (DIM, DIM), jnp.float32, -s, s)}
    _L1_attn_all = _L1_attn_setup()
    _L1_attn_in = {k: v for k, v in _L1_attn_all.items() if k in ('Wq', 'Wk', 'Wv', 'Wo')}
    del _L1_attn_all

    def _L1_xattn_setup():
        import jax, jax.numpy as jnp
        import numpy as np
        D_MODEL = 128
        HEADS = 16
        HEAD_DIM = D_MODEL // HEADS
        B, S = (2, 256)
        key0 = jax.random.key(seed)
        ks = jax.random.split(key0, 8)
        inp = {'key': jax.random.normal(ks[0], (B, S, D_MODEL), dtype=jnp.float32), 'query': jax.random.normal(ks[1], (B, S, D_MODEL), dtype=jnp.float32), 'value': jax.random.normal(ks[2], (B, S, D_MODEL), dtype=jnp.float32), 'mask': jnp.ones((B, 1, S, S), dtype=jnp.int32), 'Wq': jax.random.normal(ks[3], (D_MODEL, D_MODEL), dtype=jnp.float32) * 0.02, 'Wk': jax.random.normal(ks[4], (D_MODEL, D_MODEL), dtype=jnp.float32) * 0.02, 'Wv': jax.random.normal(ks[5], (D_MODEL, D_MODEL), dtype=jnp.float32) * 0.02, 'Wo': jax.random.normal(ks[6], (D_MODEL, D_MODEL), dtype=jnp.float32) * 0.02, 'bo': jax.random.normal(ks[7], (D_MODEL,), dtype=jnp.float32) * 0.02}
        return inp
    _L1_xattn_all = _L1_xattn_setup()
    _L1_xattn_in = {k: v for k, v in _L1_xattn_all.items() if k in ('Wq', 'Wk', 'Wv', 'Wo', 'bo')}
    del _L1_xattn_all

    def _L1_ffn_setup():
        import jax, jax.numpy as jnp
        import numpy as np
        B, S, D_MODEL, D_HIDDEN = (4, 256, 128, 512)

        def act_quant(x):
            scale = 127.0 / jnp.clip(jnp.max(jnp.abs(x), axis=-1, keepdims=True), 1e-05)
            return jnp.clip(jnp.round(x * scale), -128, 127) / scale

        def weight_quant(w):
            scale = 1.0 / jnp.clip(jnp.mean(jnp.abs(w)), 1e-05)
            return jnp.clip(jnp.round(w * scale), -1, 1) / scale

        def bit_linear(x, w):
            xq = x + jax.lax.stop_gradient(act_quant(x) - x)
            wq = w + jax.lax.stop_gradient(weight_quant(w) - w)
            return jnp.einsum('bsd,hd->bsh', xq, wq)

        def depthwise_conv1d(x_bcl, w, b):
            y = jax.lax.conv_general_dilated(x_bcl, w, window_strides=(1,), padding=[(1, 1)], dimension_numbers=('NCH', 'OIH', 'NCH'), feature_group_count=x_bcl.shape[1])
            return y + b[None, :, None]
        key = jax.random.key(seed)
        ks = jax.random.split(key, 5)
        lim1 = 1.0 / np.sqrt(D_MODEL)
        lim2 = 1.0 / np.sqrt(D_HIDDEN)
        limc = 1.0 / np.sqrt(3.0)
        return {'x': jax.random.normal(ks[0], (B, S, D_MODEL), dtype=jnp.float32), 'w1': jax.random.uniform(ks[1], (D_HIDDEN, D_MODEL), jnp.float32, -lim1, lim1), 'conv_w': jax.random.uniform(ks[2], (D_HIDDEN, 1, 3), jnp.float32, -limc, limc), 'conv_b': jax.random.uniform(ks[3], (D_HIDDEN,), jnp.float32, -limc, limc), 'w2': jax.random.uniform(ks[4], (D_MODEL, D_HIDDEN), jnp.float32, -lim2, lim2)}
    _L1_ffn_all = _L1_ffn_setup()
    _L1_ffn_in = {k: v for k, v in _L1_ffn_all.items() if k in ('w1', 'conv_w', 'conv_b', 'w2')}
    del _L1_ffn_all
    return {'x': x, 'ctx_1024': ctx_1024, 'mask_Bx1xSxS2_if1': mask_Bx1xSxS2_if1, 'L0_attn_Wq': _L0_attn_in['Wq'], 'L0_attn_bq': _L0_attn_in['bq'], 'L0_attn_Wk': _L0_attn_in['Wk'], 'L0_attn_bk': _L0_attn_in['bk'], 'L0_attn_Wv': _L0_attn_in['Wv'], 'L0_attn_bv': _L0_attn_in['bv'], 'L0_attn_Wp': _L0_attn_in['Wp'], 'L0_attn_bp': _L0_attn_in['bp'], 'L0_attn_bias_table': _L0_attn_in['bias_table'], 'L0_attn_temperature': _L0_attn_in['temperature'], 'L0_xattn_Wq': _L0_xattn_in['Wq'], 'L0_xattn_bq': _L0_xattn_in['bq'], 'L0_xattn_Wk': _L0_xattn_in['Wk'], 'L0_xattn_bk': _L0_xattn_in['bk'], 'L0_xattn_Wv': _L0_xattn_in['Wv'], 'L0_xattn_bv': _L0_xattn_in['bv'], 'L0_xattn_We': _L0_xattn_in['We'], 'L0_xattn_be': _L0_xattn_in['be'], 'L0_ffn_routers': _L0_ffn_in['routers'], 'L0_ffn_W1': _L0_ffn_in['W1'], 'L0_ffn_W2': _L0_ffn_in['W2'], 'L1_attn_Wq': _L1_attn_in['Wq'], 'L1_attn_Wk': _L1_attn_in['Wk'], 'L1_attn_Wv': _L1_attn_in['Wv'], 'L1_attn_Wo': _L1_attn_in['Wo'], 'L1_xattn_Wq': _L1_xattn_in['Wq'], 'L1_xattn_Wk': _L1_xattn_in['Wk'], 'L1_xattn_Wv': _L1_xattn_in['Wv'], 'L1_xattn_Wo': _L1_xattn_in['Wo'], 'L1_xattn_bo': _L1_xattn_in['bo'], 'L1_ffn_w1': _L1_ffn_in['w1'], 'L1_ffn_conv_w': _L1_ffn_in['conv_w'], 'L1_ffn_conv_b': _L1_ffn_in['conv_b'], 'L1_ffn_w2': _L1_ffn_in['w2']}

def reference(x, ctx_1024, mask_Bx1xSxS2_if1, L0_attn_Wq, L0_attn_bq, L0_attn_Wk, L0_attn_bk, L0_attn_Wv, L0_attn_bv, L0_attn_Wp, L0_attn_bp, L0_attn_bias_table, L0_attn_temperature, L0_xattn_Wq, L0_xattn_bq, L0_xattn_Wk, L0_xattn_bk, L0_xattn_Wv, L0_xattn_bv, L0_xattn_We, L0_xattn_be, L0_ffn_routers, L0_ffn_W1, L0_ffn_W2, L1_attn_Wq, L1_attn_Wk, L1_attn_Wv, L1_attn_Wo, L1_xattn_Wq, L1_xattn_Wk, L1_xattn_Wv, L1_xattn_Wo, L1_xattn_bo, L1_ffn_w1, L1_ffn_conv_w, L1_ffn_conv_b, L1_ffn_w2):
    import jax
    import jax.numpy as jnp

    def _L0_attn_ref(x, Wq, bq, Wk, bk, Wv, bv, Wp, bp, bias_table, temperature):
        import jax, jax.numpy as jnp
        import numpy as np
        EMB = 128
        HEADS = 16
        HEAD_DIM = EMB // HEADS
        MAX_LEN = 125
        B, N, C = x.shape
        H, D = (HEADS, C // HEADS)

        def split_heads(t):
            return t.reshape(B, N, H, D).transpose(0, 2, 1, 3)
        q = split_heads(x @ Wq + bq)
        k = split_heads(x @ Wk + bk)
        v = split_heads(x @ Wv + bv)
        energy = jnp.einsum('bhqd,bhkd->bhqk', q, k)
        pos = jnp.arange(N)
        rel = pos[:, None] - pos[None, :] + (N - 1)
        rel = jnp.clip(rel, 0, bias_table.shape[0] - 1)
        bias = bias_table[rel].transpose(2, 0, 1)
        energy = energy + bias[None]
        scaling = jnp.sqrt(jnp.float32(C))
        temp = jnp.clip(temperature[0], 0.1, 10.0)
        att = jax.nn.softmax(energy / (scaling * temp), axis=-1)
        out = jnp.einsum('bhqk,bhkd->bhqd', att, v)
        out = out.transpose(0, 2, 1, 3).reshape(B, N, C)
        return out @ Wp + bp

    def _L0_xattn_ref(x, context, Wq, bq, Wk, bk, Wv, bv, We, be):
        import jax, jax.numpy as jnp
        import numpy as np
        import math
        B, S, D = (8, 256, 128)
        q = jnp.einsum('bsd,ed->bse', x, Wq) + bq
        k = jnp.einsum('bsd,ed->bse', context, Wk) + bk
        v = jnp.einsum('bsd,ed->bse', context, Wv) + bv
        entangled = jnp.tanh(jnp.einsum('bsd,ed->bse', jnp.concatenate([q, k], axis=-1), We) + be)
        scale = 1.0 / math.sqrt(x.shape[-1])
        scores = jnp.einsum('bqd,bkd->bqk', entangled, v) * scale
        attn = jax.nn.softmax(scores, axis=-1)
        return jnp.einsum('bqk,bkd->bqd', attn, v)

    def _L0_ffn_ref(x, routers, W1, W2):
        import jax, jax.numpy as jnp
        import numpy as np
        B, S, D, FF, E, L = (8, 256, 128, 512, 16, 4)

        def _unipool_layer(xt, router, W1, W2):
            logits = xt @ router
            probs = jax.nn.softmax(logits, axis=-1)
            w = jnp.max(probs, axis=-1)
            idx = jnp.argmax(probs, axis=-1)

            def body(acc, params):
                w1, w2, i = params
                h = jax.nn.silu(xt @ w1) @ w2
                sel = jnp.where(idx == i, w, 0.0)
                return (acc + sel[:, None] * h, None)
            out, _ = jax.lax.scan(body, jnp.zeros_like(xt), (W1, W2, jnp.arange(W1.shape[0])))
            return out
        b, s, d = x.shape
        xt = x.reshape(-1, d)

        def step(carry, router):
            return (_unipool_layer(carry, router, W1, W2), None)
        xt, _ = jax.lax.scan(step, xt, routers)
        return xt.reshape(b, s, d)

    def _L1_attn_ref(x, Wq, Wk, Wv, Wo):
        import jax, jax.numpy as jnp
        import numpy as np
        DIM = 128
        NUM_HEADS = 16
        DIM_HEAD = DIM // NUM_HEADS

        def _softmax(logits, axis=-1):
            logits = logits - jnp.max(logits, axis=axis, keepdims=True)
            e = jnp.exp(logits)
            return e / jnp.sum(e, axis=axis, keepdims=True)
        B, T, D = x.shape
        H, Dh = (NUM_HEADS, DIM_HEAD)
        q = (x @ Wq.T).reshape(B, T, H, Dh).transpose(0, 2, 1, 3)
        k = (x @ Wk.T).reshape(B, T, H, Dh).transpose(0, 2, 1, 3)
        v = (x @ Wv.T).reshape(B, T, H, Dh).transpose(0, 2, 1, 3)
        scale = Dh ** (-0.5)
        logits = jnp.einsum('bhqd,bhkd->bhqk', q, k) * scale
        causal_mask = jnp.triu(jnp.ones((T, T), dtype=bool), k=1)
        neg = -jnp.finfo(logits.dtype).max
        logits = jnp.where(causal_mask, neg, logits)
        attn = _softmax(logits, axis=-1)
        out = jnp.einsum('bhqk,bhkd->bhqd', attn, v)
        out = out.transpose(0, 2, 1, 3).reshape(B, T, D)
        return out @ Wo.T

    def _L1_xattn_ref(key, query, value, mask, Wq, Wk, Wv, Wo, bo):
        import jax, jax.numpy as jnp
        import numpy as np
        D_MODEL = 128
        HEADS = 16
        HEAD_DIM = D_MODEL // HEADS
        B, S = (2, 256)
        b, q_len, d = query.shape
        k_len = key.shape[1]
        h, hd = (HEADS, HEAD_DIM)
        q = (query @ Wq.T).reshape(b, q_len, h, hd)
        k = (key @ Wk.T).reshape(b, k_len, h, hd)
        v = (value @ Wv.T).reshape(b, k_len, h, hd)
        product = jnp.einsum('bqhd,bkhd->bhqk', q, k)
        product = jnp.where(mask == 0, jnp.float32(-1e+20), product)
        product = product / jnp.sqrt(jnp.asarray(hd, product.dtype))
        scores = jax.nn.softmax(product, axis=-1)
        out = jnp.einsum('bhqk,bkhd->bqhd', scores, v).reshape(b, q_len, h * hd)
        return out @ Wo.T + bo

    def _L1_ffn_ref(x, w1, conv_w, conv_b, w2):
        import jax, jax.numpy as jnp
        import numpy as np
        B, S, D_MODEL, D_HIDDEN = (4, 256, 128, 512)

        def act_quant(x):
            scale = 127.0 / jnp.clip(jnp.max(jnp.abs(x), axis=-1, keepdims=True), 1e-05)
            return jnp.clip(jnp.round(x * scale), -128, 127) / scale

        def weight_quant(w):
            scale = 1.0 / jnp.clip(jnp.mean(jnp.abs(w)), 1e-05)
            return jnp.clip(jnp.round(w * scale), -1, 1) / scale

        def bit_linear(x, w):
            xq = x + jax.lax.stop_gradient(act_quant(x) - x)
            wq = w + jax.lax.stop_gradient(weight_quant(w) - w)
            return jnp.einsum('bsd,hd->bsh', xq, wq)

        def depthwise_conv1d(x_bcl, w, b):
            y = jax.lax.conv_general_dilated(x_bcl, w, window_strides=(1,), padding=[(1, 1)], dimension_numbers=('NCH', 'OIH', 'NCH'), feature_group_count=x_bcl.shape[1])
            return y + b[None, :, None]
        h = bit_linear(x, w1)
        h = depthwise_conv1d(h.transpose(0, 2, 1), conv_w, conv_b)
        h = h.transpose(0, 2, 1)
        h = jax.nn.silu(h)
        return bit_linear(h, w2)
    x = _layernorm(x + _L0_attn_ref(x, L0_attn_Wq, L0_attn_bq, L0_attn_Wk, L0_attn_bk, L0_attn_Wv, L0_attn_bv, L0_attn_Wp, L0_attn_bp, L0_attn_bias_table, L0_attn_temperature), axis=-1)
    x = _layernorm(x + _L0_xattn_ref(x, ctx_1024, L0_xattn_Wq, L0_xattn_bq, L0_xattn_Wk, L0_xattn_bk, L0_xattn_Wv, L0_xattn_bv, L0_xattn_We, L0_xattn_be), axis=-1)
    x = _layernorm(x + _L0_ffn_ref(x, L0_ffn_routers, L0_ffn_W1, L0_ffn_W2), axis=-1)
    x = _layernorm(x + _L1_attn_ref(x, L1_attn_Wq, L1_attn_Wk, L1_attn_Wv, L1_attn_Wo), axis=-1)
    x = _layernorm(x + _L1_xattn_ref(ctx_1024, x, ctx_1024, mask_Bx1xSxS2_if1, L1_xattn_Wq, L1_xattn_Wk, L1_xattn_Wv, L1_xattn_Wo, L1_xattn_bo), axis=-1)
    x = _layernorm(x + _L1_ffn_ref(x, L1_ffn_w1, L1_ffn_conv_w, L1_ffn_conv_b, L1_ffn_w2), axis=-1)
    return x

_drawn_inputs = setup_inputs


def setup_inputs(seed=0):
    import zlib

    import numpy as np

    out = dict(_drawn_inputs(seed))
    spreads = {'L0_attn_bq': (0.0, 0.8),
     'L0_attn_bk': (0.0, 0.8),
     'L0_attn_bv': (0.0, 0.383),
     'L0_attn_bp': (0.0, 0.1),
     'L0_xattn_bq': (0.0, 0.787),
     'L0_xattn_bk': (0.0, 0.8),
     'L0_xattn_bv': (0.0, 0.1),
     'L0_xattn_be': (0.0, 0.65)}
    factors = {'L0_attn_Wq': 8.0,
     'L0_attn_Wk': 8.0,
     'L0_attn_Wv': 8.0,
     'L0_attn_Wp': 3.041,
     'L0_attn_bias_table': 8.0,
     'L0_ffn_routers': 8.0,
     'L0_ffn_W1': 8.0,
     'L0_ffn_W2': 8.0,
     'L1_attn_Wq': 3.392,
     'L1_attn_Wk': 3.321,
     'L1_xattn_Wq': 8.0,
     'L1_xattn_Wk': 8.0,
     'L1_xattn_bo': 2.678}
    for name, (base, spread) in spreads.items():
        noise = np.random.default_rng([zlib.crc32(name.encode()), seed]).standard_normal(out[name].shape)
        drawn = base * np.exp(spread * noise) if base else spread * noise
        out[name] = jnp.asarray(drawn.astype(out[name].dtype))
    for name, factor in factors.items():
        out[name] = (out[name] * factor).astype(out[name].dtype)
    return out
```

```python
from contextlib import ExitStack

import concourse.bass as bass
from concourse import mybir

F32 = mybir.dt.float32
BF16 = mybir.dt.bfloat16
I32 = mybir.dt.int32
ALU = mybir.AluOpType
ACT = mybir.ActivationFunctionType
AX = mybir.AxisListType

P = 128
D = 128
NSEQ = 16
H = 16
HD = D // H
CB = 4
CT = CB * P
NIT = NSEQ // CB // 2
PAIR = 2 * CB
QUADS = H // 4
E = 16
FF = 512
FC = FF // P
NL = 4
NB = NSEQ + E - 1
EPS = 1e-5
MAGIC = 1.5 * 2.0 ** 23
NEG = -2.0 ** 66
RSQRT_SEED = 0x5F3759DF
Q_TERMS = (0, 0, 0, 1, 1, 2)
K_TERMS = (0, 1, 2, 0, 1, 0)


def decoder(nc, a, out):
    ctx = ExitStack()
    with ctx:
        def sb(name, shape, dt=F32):
            return ctx.enter_context(nc.sbuf_tensor(name, shape, dt))

        def sem(name):
            return ctx.enter_context(nc.semaphore(name))

        def sem2(name):
            return [sem(f"{name}{p}") for p in range(2)]

        x_stage = [a["x"].rearrange("b t d -> (b t) d")]
        for n in range(5):
            x_stage.append(nc.dram_tensor(f"x_after_{n}", [NSEQ * P, D], F32).ap())
        x_stage.append(out.rearrange("b t d -> (b t) d"))
        ctx_tok = a["ctx_1024"].rearrange("b t d -> (b t) d")
        parts_dram = [[nc.dram_tensor(f"parts_{w}{p}", [3, D, CT], BF16) for w in "qk"] for p in range(2)]
        bias_dram = nc.dram_tensor("bias_rows", [2, 3, H, 256], BF16)
        slots_x = nc.dram_tensor("slots_x", [NB * P, D], F32).ap()
        slots_y = nc.dram_tensor("slots_y", [NB * P, D], F32).ap()

        big = sb("big", [P, 16384])
        stack = big[:, :].bitcast(BF16).rearrange("p (c w h t) -> p c w h t", c=2, w=2, h=H)
        w1_sb = big[:, 0:8192]
        w2_sb = big[:, 8192:16384]
        scratch_b = sb("scratch_b", [P, 6144])
        scratch_e = sb("scratch_e", [P, 4096])
        bias_sb = scratch_b[:, :].bitcast(BF16).rearrange("p (w n m) -> p w n m", w=2, n=3)
        mask_int = scratch_b[:, 0:2048].bitcast(I32)
        mask_neg = scratch_b[:, 2048:3072].bitcast(BF16).rearrange("p (b k) -> p b k", b=NSEQ)
        tok_x = scratch_b[:, 0:2048].rearrange("p (b d) -> p b d", b=NSEQ)
        tok_in = scratch_b[:, 2048:4096].rearrange("p (b d) -> p b d", b=NSEQ)
        tok_y = scratch_b[:, 4096:6144].rearrange("p (b d) -> p b d", b=NSEQ)
        probs = [scratch_e[:, 2048 * e:2048 * e + 2048] for e in range(2)]
        wnat = scratch_e[:, 0:19 * D].rearrange("p (n d) -> p n d", n=19)
        f1nat = scratch_e[:, 19 * D:23 * D]
        f2nat = scratch_e[:, 23 * D:27 * D]
        mx = sb("mx", [P, 1024])
        mexp = mx[:, :].bitcast(BF16).rearrange("p (h q) -> p h q", h=H)
        vpad = sb("vpad", [P, 2, CB, H, 32])
        chunks = sb("chunks", [P, 8, CT])
        xc = [chunks[:, p, :].rearrange("p (b d) -> p b d", b=CB) for p in range(2)]
        xt = [chunks[:, 2 + p, :] for p in range(2)]
        cc = [chunks[:, 4 + p, :].rearrange("p (b d) -> p b d", b=CB) for p in range(2)]
        ct = [chunks[:, 6 + p, :] for p in range(2)]
        qkp_all = sb("qkp", [P, 2 * 2 * 3 * CT], BF16)
        qkp = qkp_all[:, :].rearrange("p (c w n t) -> p c w n t", c=2, w=2, n=3)
        qkp32 = qkp_all[:, :].bitcast(F32)
        rest = [[sb(f"rest{p}{w}", [P, CT]) for w in range(2)] for p in range(2)]
        vt = sb("vt", [P, CT])
        osb = [sb(f"osb{e}", [P, CT]) for e in range(2)]
        rden = sb("rden", [P, CT])
        onorm = sb("onorm", [P, CT])
        zt = [sb(f"zt{p}", [P, CB, D]) for p in range(2)]
        xo = [sb(f"xo{p}", [P, CB, D]) for p in range(2)]
        m48 = sb("m48", [P, H, P], BF16)
        wt = sb("wt", [P, 19, D])
        w0 = sb("w0", [P, 3, D])
        wo0 = sb("wo0", [P, 4, D])
        f1t = sb("f1t", [P, FF], BF16)
        f2t = sb("f2t", [P, FC, D], BF16)
        ident = sb("ident", [P, P])
        ident_b = sb("ident_b", [P, P], BF16)
        anti_b = sb("anti_b", [P, P], BF16)
        ones = sb("ones", [P, P])
        ones_b = sb("ones_b", [P, P], BF16)
        tri_b = sb("tri_b", [P, P], BF16)
        causal_b = sb("causal_b", [P, P], BF16)
        dsel = sb("dsel", [P, P])
        abias = sb("abias", [P, 9])
        xbias = sb("xbias", [P, 4])
        score_scale = sb("score_scale", [P, 3])
        router_sb = sb("router_sb", [P, NL * E])
        conv_w = sb("conv_w", [P, FC, 3])
        conv_b = sb("conv_b", [P, FC])
        wsc = sb("wsc", [P, 8])
        zero_t = sb("zero_t", [P, D])
        nmax = sb("nmax", [P, H])
        nrest = sb("nrest", [P, H])
        nparts = sb("nparts", [P, P], BF16)
        mt_sb = sb("mt_sb", [P, P], BF16)
        stats = sb("stats", [P, NSEQ, 6])
        lnv = sb("lnv", [P, 4, NSEQ])
        tab = sb("tab", [P, 2, H])
        small = sb("small", [P, 16, NSEQ])
        WT_X, WT_A1, WT_O1, WT_A2, WT_O2 = 0, 5, 8, 12, 15

        bank = [ctx.enter_context(nc.psum_tensor(f"bank{n}", [P, 1024], F32)) for n in range(4)]

        def pb(n):
            return bank[n // 2][:, 512 * (n % 2):512 * (n % 2) + 512]

        front_loaded = sem("front_loaded")
        late_loaded = sem("late_loaded")
        const_made = sem("const_made")
        table_ready = sem("table_ready")
        rows_made = sem("rows_made")
        rows_stored = sem("rows_stored")
        bias_loaded = sem("bias_loaded")
        perm_made = sem("perm_made")
        turned = sem("turned")
        wt_made = sem("wt_made")
        abs_made = sem("abs_made")
        abs_total = sem("abs_total")
        tern_made = sem("tern_made")
        tern_turned = sem("tern_turned")
        rows_added = sem("rows_added")
        slots_zero = sem("slots_zero")
        zeroed_pool = sem("zeroed_pool")
        zeroed_dve = sem("zeroed_dve")
        pool_step = sem("pool_step")
        chain = sem("dve_chain")
        prep_done = sem("prep_done")
        x_loaded = sem2("x_loaded")
        c_loaded = sem2("c_loaded")
        m_ready = [sem("bank6_ready"), sem("bank7_ready")]
        m_free = [sem("bank6_free"), sem("bank7_free")]
        part1_made = sem("part1_made")
        part2_made = sem("part2_made")
        parts_made = sem2("parts_made")
        parts_stored = [sem2(f"parts_stored{p}_") for p in range(2)]
        stacked = sem2("stacked")
        s_ready = sem("scores_ready")
        s_free = sem("scores_free")
        nm_ready = sem("nmax_ready")
        mexp_ready = sem("mexp_ready")
        st_ready = sem("scores_t_ready")
        exp_done = sem("exp_done")
        av_done = sem2("av_done")
        o_copied = sem("o_copied")
        den_ready = sem("den_ready")
        den_free = sem("den_free")
        on_ready = sem("onorm_ready")
        ln_done = sem2("ln_done")
        x_stored = sem2("x_stored")
        mask_loaded = sem("mask_loaded")
        mask_made = sem("mask_made")
        b_ready = [sem(f"bank{b}_filled") for b in range(8)]
        b_free = [sem(f"bank{b}_read") for b in range(8)]
        g_x_loaded = sem2("g_x_loaded")
        g_c_loaded = sem2("g_c_loaded")
        g_ln_done = sem2("g_ln_done")
        g_x_stored = sem2("g_x_stored")
        nbias_ready = sem("nbias_ready")
        p_made = sem("p_made")
        xq_made = sem("xq_made")
        conv_made = sem("conv_made")
        silu_made = sem("silu_made")
        qscale_made = sem("qscale_made")
        hq_made = sem("hq_made")
        moe_loaded = sem("moe_loaded")
        w1_loaded = sem("w1_loaded")
        w2_loaded = sem("w2_loaded")
        xturn_ready = sem("xturn_ready")
        xturn_a = sem("xturn_a")
        xturn_d = sem("xturn_d")
        logits_ready = sem("logits_ready")
        shifted = sem("shifted")
        expd = sem("expd")
        onehot_ready = sem("onehot_ready")
        counts_ready = sem("counts_ready")
        pos_ready = sem("pos_ready")
        block_ready = sem("block_ready")
        scattered = sem("scattered")
        xs_loaded = sem("xs_loaded")
        xsT_ready = sem("xsT_ready")
        xsT_made = sem("xsT_made")
        h_ready = sem("h_ready")
        h_made = sem("h_made")
        hT_ready = sem("hT_ready")
        hT_made = sem("hT_made")
        y_ready = sem("y_ready")
        y_made = sem("y_made")
        y_stored = sem("y_stored")
        gathered = [sem(f"gathered{g}") for g in range(4)]
        tok_made = sem("tok_made")
        moe_ln = sem("moe_ln")
        moe_stored = sem("moe_stored")

        block = ctx.enter_context(nc.Block())

        class Chain:

            def __init__(self, eng):
                self.eng, self.base, self.n = eng, 0, 0

            def __call__(self, ins):
                self.n += 1
                ins.then_inc(chain, 1)
                self.eng.wait_ge(chain, self.base + self.n)

        def looped(eng, link, body, count, steps):
            start = link.base + link.n
            with eng.Fori(0, count, 1) as i:
                link.base, link.n = start + i * steps, 0
                body(i)
                assert link.n == steps, (body, link.n, steps)
            link.base, link.n = start + count * steps, 0

        U = [3, 2]

        def use(b, s, i, p, what, j=0):
            first = [U[b] + (1 if k == 2 and b == 1 else 0) for k in range(3)]
            before = sum(NIT * 2 * (first[k] + CB) for k in range(s))
            before = before + i * (2 * (first[s] + CB))
            if what == "core":
                return before + 2 * first[s] + CB * p + j
            return before + first[s] * p + what

        UB = [[2, 2, 1, 1, 1, 1, 1, 1], [1, 1, 2, 2, 2, 2, 4, 4]]

        def ub(b, stage, i, p, k=0):
            return (2 * NIT * UB[0][b] if stage else 0) + (2 * i + p) * UB[stage][b] + k

        def heads(ap):
            return ap.rearrange("p (h q) -> p h q", q=P)

        def four(ap):
            return ap.rearrange("p (b d) -> p b d", b=4)

        def over(ap, n):
            return ap.unsqueeze(1).broadcast_to([P, n, ap.shape[1]])

        def along(ap, n):
            return ap.unsqueeze(2).broadcast_to([P, ap.shape[1], n])

        def weights_of(s):
            base = (0, WT_A1, WT_A2)[s]
            src = w0 if s == 0 else wt
            wo = wo0[:, :, :] if s == 0 else wt[:, WT_O1:WT_O1 + 4, :] if s == 1 else wt[:, WT_O2:WT_O2 + 4, :]
            return src[:, base, :], src[:, base + 1, :], src[:, base + 2, :], wo

        def attn_sp(sp, s, src, dst):
            for i in range(NIT):
                it = i + NIT * s
                for p in range(2):
                    c = 2 * i + p
                    if it:
                        sp.wait_ge(ln_done[p], it)
                    sp.dma_start(xc[p], src[CT * c:CT * c + CT, :].rearrange("(b t) d -> t b d", b=CB)).then_inc(
                        x_loaded[p], 16)
                    if s == 2:
                        sp.dma_start(cc[p], ctx_tok[CT * c:CT * c + CT, :].rearrange("(b t) d -> t b d", b=CB)).then_inc(
                            c_loaded[p], 16)
                for p in range(2):
                    if it:
                        sp.wait_ge(stacked[p], 192 * it)
                    for w in range(2):
                        sp.wait_ge(parts_made[p], 2 * it + w + 1)
                        sp.dma_start(parts_dram[p][w].ap().rearrange("n d t -> d n t"), qkp[:, p, w, :, :]).then_inc(
                            parts_stored[p][w], 16)
                    if s == 0 and i == 0:
                        sp.wait_ge(zeroed_pool, 1)
                        sp.wait_ge(zeroed_dve, 1)
                    if s == 1 and i == 0:
                        sp.wait_ge(zeroed_pool, 2)
                        sp.wait_ge(zeroed_dve, 2)
                    if it:
                        sp.wait_ge(st_ready, 2 * PAIR * (it - 1) + 2 * CB * (p + 1))
                    for w, terms in ((0, Q_TERMS), (1, K_TERMS)):
                        sp.wait_ge(parts_stored[p][w], 16 * it + 16)
                        for n, part in enumerate(terms):
                            sp.dma_start(stack[HD * n:HD * n + HD, p, w, :, :],
                                         parts_dram[p][w].ap()[part].rearrange("(h d) t -> d h t", h=H)).then_inc(
                                             stacked[p], 16)
                for p in range(2):
                    c = 2 * i + p
                    sp.wait_ge(ln_done[p], it + 1)
                    sp.dma_start(dst[CT * c:CT * c + CT, :].rearrange("(b t) d -> t b d", b=CB), xo[p][:, :, :]).then_inc(
                        x_stored[p], 16)
            for p in range(2):
                sp.wait_ge(x_stored[p], 16 * NIT * (s + 1))

        def attn_pe(pe, s, i):
            it = i + NIT * s
            wq, wk, wv, wo = weights_of(s)
            off = 1 if s == 2 else 0
            for p in range(2):
                kv = ct[p] if s == 2 else xt[p]
                pe.wait_ge(x_loaded[p], 16 * it + 16)
                pe.wait_ge(m_free[0], use(0, s, i, p, 0))
                for j in range(CB):
                    mm = pe.transpose(pb(6)[:, P * j:P * j + P], xc[p][:, j, :], ident[:, :])
                mm.then_inc(m_ready[0], 1)
                if s == 2:
                    pe.wait_ge(c_loaded[p], 16 * i + 16)
                    pe.wait_ge(m_free[1], use(1, s, i, p, 0))
                    for j in range(CB):
                        mm = pe.transpose(pb(7)[:, P * j:P * j + P], cc[p][:, j, :], ident[:, :])
                    mm.then_inc(m_ready[1], 1)
                pe.wait_ge(m_free[0], use(0, s, i, p, 1))
                pe.matmul(pb(6), wq, xt[p], start=True, stop=True).then_inc(m_ready[0], 1)
                pe.wait_ge(m_free[1], use(1, s, i, p, off))
                pe.matmul(pb(7), wk, kv, start=True, stop=True).then_inc(m_ready[1], 1)
                pe.wait_ge(m_free[0], use(0, s, i, p, 2))
                pe.matmul(pb(6), wv, kv, start=True, stop=True).then_inc(m_ready[0], 1)
                pe.wait_ge(m_free[0], use(0, s, i, p, 2) + 1)
                pe.wait_ge(m_free[1], use(1, s, i, p, off + 1))
                for j in range(CB):
                    mm = pe.transpose(pb(7)[:, P * j:P * j + P], vt[:, P * j:P * j + P], ident[:, :])
                mm.then_inc(m_ready[1], 1)

            def scores(g, half):
                p, j = g // CB, g % CB
                pe.wait_ge(s_free, 2 * PAIR * it + 2 * g + half)
                for b in range(2):
                    dst = bank[0][:, 512 * b:512 * b + 512]
                    if s == 0:
                        for n in range(3):
                            m0 = 1024 * half + 512 * b
                            pe.matmul(dst, anti_b[:, :], bias_sb[:, 0, n, m0:m0 + 512], start=(n == 0),
                                      stop=False, skip_group_check=True)
                    else:
                        row = causal_b[:, :] if s == 1 else mask_neg[:, bass.ds(PAIR * i + g, 1), :][:, 0, :]
                        pe.matmul(heads(dst), ident_b[:, :], over(row, 4), start=True, stop=False,
                                  skip_group_check=True)
                    for k in range(4):
                        h = 8 * half + 4 * b + k
                        mm = pe.matmul(dst[:, P * k:P * k + P], stack[:, p, 0, h, P * j:P * j + P],
                                       stack[:, p, 1, h, P * j:P * j + P], start=False, stop=(k == 3),
                                       skip_group_check=True)
                mm.then_inc(s_ready, 1)

            def scores_t(g, half):
                p, j = g // CB, g % CB
                pe.wait_ge(exp_done, 2 * PAIR * it + 2 * g + half)
                for b in range(2):
                    dst = bank[1][:, 512 * b:512 * b + 512]
                    m0 = 8 * half + 4 * b
                    pe.matmul(heads(dst), ones_b[:, :], mexp[:, m0:m0 + 4, :], start=True, stop=False,
                              skip_group_check=True)
                    for k in range(4):
                        h = m0 + k
                        pe.matmul(dst[:, P * k:P * k + P], stack[:, p, 1, h, P * j:P * j + P],
                                  stack[:, p, 0, h, P * j:P * j + P], start=False, stop=False,
                                  skip_group_check=True)
                    if s == 0:
                        for n in range(3):
                            mm = pe.matmul(dst, anti_b[:, :], bias_sb[:, 1, n, P * m0:P * m0 + 512], start=False,
                                           stop=(n == 2), skip_group_check=True)
                    else:
                        row = causal_b[:, :] if s == 1 else mask_neg[:, bass.ds(PAIR * i + g, 1), :][:, 0, :]
                        mm = pe.matmul(heads(dst), row, over(ident_b[:, :], 4), start=False, stop=True,
                                       skip_group_check=True)
                mm.then_inc(st_ready, 1)

            for t in range(PAIR + 3):
                if t < PAIR:
                    if t % CB == 0:
                        pe.wait_ge(stacked[t // CB], 192 * it + 192)
                    scores(t, 0)
                if 0 <= t - 1 < PAIR:
                    pe.wait_ge(mexp_ready, PAIR * it + t)
                    scores_t(t - 1, 0)
                if 0 <= t - 3 < PAIR:
                    g = t - 3
                    pe.wait_ge(o_copied, PAIR * it + g + 1)
                    pe.wait_ge(den_free, PAIR * it + g)
                    pe.matmul(pb(5), dsel[:, :], osb[g % 2][:, :], start=True, stop=True).then_inc(den_ready, 1)
                if t < PAIR:
                    scores(t, 1)
                if 0 <= t - 1 < PAIR:
                    scores_t(t - 1, 1)
                if 0 <= t - 3 < PAIR:
                    g = t - 3
                    pe.wait_ge(on_ready, PAIR * it + g + 1)
                    pe.wait_ge(m_free[0], use(0, s, i, g // CB, "core", g % CB))
                    for q in range(QUADS):
                        mm = pe.matmul(pb(6)[:, 0:D], onorm[:, P * q:P * q + P], wo[:, q, :], start=(q == 0),
                                       stop=(q == QUADS - 1))
                    mm.then_inc(m_ready[0], 1)
                if 0 <= t - 2 < PAIR:
                    g = t - 2
                    p, j = g // CB, g % CB
                    pe.wait_ge(exp_done, 2 * PAIR * it + 2 * g + 2)
                    pe.wait_ge(o_copied, PAIR * it + g)
                    pe.wait_ge(m_free[1], use(1, s, i, p, off + 1) + 1)
                    for h in range(H):
                        r, q = 32 * (h % 4), h // 4
                        mm = pe.matmul(pb(4)[r:r + 32, P * q:P * q + P], vpad[:, p, j, h, :],
                                       probs[g % 2][:, P * h:P * h + P], start=True, stop=True,
                                       skip_group_check=True)
                    mm.then_inc(av_done[g % 2], 1)
                if t < PAIR:
                    pe.wait_ge(nm_ready, PAIR * it + t + 1)
                    pe.wait_ge(m_free[1], use(1, s, i, t // CB, "core", t % CB))
                    pe.transpose(pb(7).bitcast(BF16)[:, 0:P], nparts[:, :], ident_b[:, :]).then_inc(m_ready[1], 1)

        def attn_act(act, s, i):
            it = i + NIT * s
            off = 1 if s == 2 else 0
            for p in range(2):
                act.wait_ge(m_ready[0], use(0, s, i, p, 0) + 1)
                act.copy(xt[p], pb(6)).then_inc(m_free[0], 1)
                for w in range(2):
                    act.wait_ge(parts_stored[p][w], 16 * it)
                act.wait_ge(m_ready[0], use(0, s, i, p, 1) + 1)
                act.activation(qkp[:, p, 0, 0, :], pb(6), ACT.Identity, bias=abias[:, 3 * s:3 * s + 1]).then_inc(
                    part1_made, 1)
                act.wait_ge(m_ready[1], use(1, s, i, p, off) + 1)
                act.activation(qkp[:, p, 1, 0, :], pb(7), ACT.Identity, bias=abias[:, 3 * s + 1:3 * s + 2]).then_inc(
                    part1_made, 1)
                act.wait_ge(m_ready[0], use(0, s, i, p, 2) + 1)
                act.activation(vt[:, :], pb(6), ACT.Identity, bias=abias[:, 3 * s + 2:3 * s + 3]).then_inc(m_free[0], 1)
            for t in range(PAIR + 3):
                if 0 <= t - 1 < PAIR:
                    g = t - 1
                    for half in range(2):
                        act.wait_ge(st_ready, 2 * PAIR * it + 2 * g + half + 1)
                        act.wait_ge(av_done[g % 2], CB * it + g // 2)
                        act.activation(probs[g % 2][:, 1024 * half:1024 * half + 1024], bank[1][:, :], ACT.Exp,
                                       scale=score_scale[:, s:s + 1]).then_inc(exp_done, 1)
                if 0 <= t - 2 < PAIR:
                    g = t - 2
                    act.wait_ge(av_done[g % 2], CB * it + g // 2 + 1)
                    act.wait_ge(on_ready, PAIR * it + max(g - 1, 0))
                    act.copy(osb[g % 2][:, :], pb(4)).then_inc(o_copied, 1)

        def attn_pool(pool, s, i):
            it = i + NIT * s
            off = 1 if s == 2 else 0
            for p in range(2):
                for w in range(2):
                    pool.wait_ge(m_free[w], (use(0, s, i, p, 1) if w == 0 else use(1, s, i, p, off)) + 1)
                    pool.tensor_copy(qkp[:, p, w, 1, :], rest[p][w][:, :]).then_inc(part2_made, 1)
                    pool.wait_ge(part2_made, 4 * it + 2 * p + w + 1)
                    pool.tensor_tensor(qkp[:, p, w, 2, :], rest[p][w][:, :], qkp[:, p, w, 1, :],
                                       ALU.subtract).then_inc(parts_made[p], 1)

        def layernorm(dve, link, z, n, dst):
            v, y, t, m = (lnv[:, k, 0:n] for k in range(4))
            mean_e, mean_o = stats[:, 0:n, 1], stats[:, 0:n, 4]
            link(dve.tensor_tensor(m, mean_e, mean_o, ALU.add))
            link(dve.tensor_scalar(m, m, 0.5, None, ALU.mult))
            link(dve.tensor_tensor(t, mean_e, mean_o, ALU.subtract))
            link(dve.scalar_tensor_tensor(t, t, 0.25, t, ALU.mult, ALU.mult))
            link(dve.tensor_tensor(v, stats[:, 0:n, 2], stats[:, 0:n, 5], ALU.add))
            link(dve.scalar_tensor_tensor(v, v, 1.0 / D, t, ALU.mult, ALU.add))
            link(dve.tensor_scalar(v, v, EPS, None, ALU.add))
            link(dve.tensor_scalar(y.bitcast(I32), v.bitcast(I32), 1, None, ALU.logical_shift_right))
            link(dve.tensor_scalar(y.bitcast(I32), y.bitcast(I32), -1.0, float(RSQRT_SEED), ALU.mult, ALU.add))
            link(dve.tensor_scalar(v, v, -0.5, None, ALU.mult))
            for _ in range(4):
                link(dve.tensor_tensor(t, y, y, ALU.mult))
                link(dve.tensor_tensor(t, t, v, ALU.mult))
                link(dve.scalar_tensor_tensor(y, t, 1.5, y, ALU.add, ALU.mult))
            for k in range(n):
                ins = dve.tensor_scalar(dst[:, k, :], z[:, k, :], lnv[:, 3, k:k + 1], lnv[:, 1, k:k + 1], ALU.subtract,
                                        ALU.mult)
                if k < n - 1:
                    link(ins)
            return ins

        LN_STEPS = 10 + 12

        def attn_dve(dve, link, s, i):
            it = i + NIT * s
            off = 1 if s == 2 else 0
            for p in range(2):
                if s == 2:
                    dve.wait_ge(m_ready[1], use(1, s, i, p, 0) + 1)
                    dve.tensor_copy(ct[p], pb(7)).then_inc(m_free[1], 1)
                for w in range(2):
                    dve.wait_ge(part1_made, 2 * (2 * it + p) + w + 1)
                    dve.wait_ge(parts_made[p], 2 * it)
                    dve.scalar_tensor_tensor(rest[p][w][:, :], pb(6 + w), abias[:, 3 * s + w:3 * s + w + 1],
                                             qkp[:, p, w, 0, :], ALU.add, ALU.subtract).then_inc(m_free[w], 1)
                dve.wait_ge(m_ready[1], use(1, s, i, p, off + 1) + 1)
                dve.tensor_copy(vpad[:, p, :, :, 0:HD], pb(7).rearrange("p (b h d) -> p b h d", b=CB, h=H)).then_inc(
                    m_free[1], 1)
            for t in range(PAIR + 3):
                g3 = t - 3
                if t < PAIR:
                    dve.wait_ge(s_ready, 2 * PAIR * it + 2 * t + 1)
                    dve.tensor_reduce(nmax[:, 0:8], heads(bank[0][:, :]), AX.X, ALU.max, negate=True).then_inc(s_free, 1)
                if 0 <= g3 < PAIR:
                    dve.wait_ge(den_ready, PAIR * it + g3 + 1)
                    dve.reciprocal(rden[:, :], pb(5)).then_inc(den_free, 1)
                    dve.wait_ge(den_free, PAIR * it + g3 + 1)
                    dve.tensor_tensor(onorm[:, :], osb[g3 % 2][:, :], rden[:, :], ALU.mult).then_inc(on_ready, 1)
                if t < PAIR:
                    dve.wait_ge(s_ready, 2 * PAIR * it + 2 * t + 2)
                    dve.tensor_reduce(nmax[:, 8:16], heads(bank[0][:, :]), AX.X, ALU.max, negate=True).then_inc(s_free, 1)
                    dve.wait_ge(s_free, 2 * PAIR * it + 2 * t + 2)
                    link(dve.tensor_copy(nparts[:, 0:H], nmax[:, :]))
                    link(dve.tensor_tensor(nrest[:, :], nmax[:, :], nparts[:, 0:H], ALU.subtract))
                    link(dve.tensor_copy(nparts[:, H:2 * H], nrest[:, :]))
                    dve.tensor_tensor(nparts[:, 2 * H:3 * H], nrest[:, :], nparts[:, H:2 * H],
                                      ALU.subtract).then_inc(nm_ready, 1)
                if 0 <= g3 < PAIR:
                    p, j = g3 // CB, g3 % CB
                    dve.wait_ge(m_ready[0], use(0, s, i, p, "core", j) + 1)
                    dve.tensor_tensor(zt[p][:, j, :], pb(6)[:, 0:D], xc[p][:, j, :], ALU.add).then_inc(m_free[0], 1)
                    dve.wait_ge(m_free[0], use(0, s, i, p, "core", j) + 1)
                    link(dve.bn_stats(stats[:, j, :], zt[p][:, j, :]))
                if t < PAIR:
                    dve.wait_ge(m_ready[1], use(1, s, i, t // CB, "core", t % CB) + 1)
                    dve.tensor_copy(mt_sb[:, :], pb(7).bitcast(BF16)[:, 0:P]).then_inc(m_free[1], 1)
                    dve.wait_ge(m_free[1], use(1, s, i, t // CB, "core", t % CB) + 1)
                    dve.wait_ge(st_ready, 2 * (PAIR * it + t))
                    dve.tensor_tensor(mexp, over(mt_sb[:, :], H), m48[:, :, :], ALU.mult).then_inc(mexp_ready, 1)
                if 0 <= g3 < PAIR and g3 % CB == CB - 1:
                    p = g3 // CB
                    dve.wait_ge(x_stored[p], 16 * it)
                    layernorm(dve, link, zt[p], CB, xo[p]).then_inc(ln_done[p], 1)

        ATTN_STEPS = 3 * PAIR + PAIR + 2 * (LN_STEPS + CB - 1)

        sel = mx[:, :].rearrange("p (w n j) -> p w n j", w=2, n=2)
        rows32 = rden[0:H, :].rearrange("h (w j) -> h w j", w=2)
        rowsr = onorm[0:H, :].rearrange("h (w j) -> h w j", w=2)
        rows_b = qkp_all[0:H, 0:1536].rearrange("h (n w j) -> h n w j", n=3, w=2)
        tern1 = qkp_all[:, 2048:2560]
        tern2 = qkp_all[:, 2560:3072]
        TABLE = 2 * P - 1
        TR = 249

        def prep_sp(sp):
            def load(dst, src):
                sp.dma_start(dst, src).then_inc(front_loaded, 16)

            sp.wait_ge(const_made, 3)
            table = a["L0_attn_bias_table"]
            load(tab[:, 0, :], table[0:P, :])
            load(tab[0:TR - P, 1, :], table[P:TR, :])
            for n, name in enumerate(("Wq", "Wk", "Wv")):
                load(w0[:, n, :], a["L0_attn_" + name])
            for g in range(4):
                load(wo0[32 * g:32 * g + HD, :, :],
                     a["L0_attn_Wp"].rearrange("(i g d) n -> g d i n", i=4, g=4)[g])
            load(wo0[HD:HD + 1, 0, :], a["L0_attn_bp"].rearrange("(o d) -> o d", o=1))
            for n, name in enumerate(("bq", "bk", "bv")):
                load(abias[:, n:n + 1], a["L0_attn_" + name].rearrange("(d o) -> d o", o=1))
            load(score_scale[:, 0:1], bass.AP(a["L0_attn_temperature"].tensor, 0, [[0, P], [1, 1]]))
            late_n = [0]

            def late(dst, src):
                late_n[0] += 1
                sp.dma_start(dst, src).then_inc(late_loaded, 16)

            for n, name in enumerate(("L0_xattn_Wq", "L0_xattn_Wk", "L0_xattn_Wv")):
                late(wnat[:, WT_X + n, :], a[name])
            late(wnat[:, WT_X + 3:WT_X + 5, :], a["L0_xattn_We"].rearrange("e (n d) -> e n d", n=2))
            for n, name in enumerate(("L1_attn_Wq", "L1_attn_Wk", "L1_attn_Wv")):
                late(wnat[:, WT_A1 + n, :], a[name])
            for n, name in enumerate(("L1_xattn_Wq", "L1_xattn_Wk", "L1_xattn_Wv")):
                late(wnat[:, WT_A2 + n, :], a[name])
            late(zt[0][:, 0, :], a["L1_attn_Wo"])
            late(zt[0][:, 1, :], a["L1_xattn_Wo"])
            for n, name in enumerate(("bq", "bk", "bv", "be")):
                late(xbias[:, n:n + 1], a["L0_xattn_" + name].rearrange("(d o) -> d o", o=1))
            late(router_sb[:, :].rearrange("d (l e) -> d l e", l=NL), a["L0_ffn_routers"].rearrange("l d e -> d l e"))
            late(conv_w[:, :, :], a["L1_ffn_conv_w"].rearrange("(c p) o k -> p c (o k)", p=P))
            for c in range(FC):
                late(conv_b[:, c:c + 1], a["L1_ffn_conv_b"][P * c:P * c + P].rearrange("(p o) -> p o", o=1))
            late(f1nat.rearrange("p (c d) -> p c d", c=FC), a["L1_ffn_w1"].rearrange("(c p) d -> p c d", p=P))
            late(f2nat, a["L1_ffn_w2"])
            assert late_n[0] == LATE
            for n in range(3):
                sp.wait_ge(rows_made, n + 1)
                sp.dma_start(bias_dram.ap()[:, n, :, :].rearrange("w h j -> h w j"), rows_b[:, n, :, :]).then_inc(
                    rows_stored, 16)
            for n in range(3):
                sp.wait_ge(rows_stored, 16 * 3)
                for w in range(2):
                    sp.dma_start(bias_sb[:, w, n, :].rearrange("p (h k) -> p h k", h=H),
                                 bass.AP(bias_dram, (w * 3 + n) * H * 256, [[1, P], [256, H], [1, P]])).then_inc(
                                     bias_loaded, 16)
            sp.wait_ge(const_made, 17)
            sp.wait_ge(wt_made, 5)
            sp.dma_start(wt[HD:HD + 1, WT_O2, :], a["L1_xattn_bo"].rearrange("(o d) -> o d", o=1)).then_inc(rows_added, 16)
            sp.dma_start(slots_x.rearrange("(b p) d -> p b d", p=P), over(zero_t[:, :], NB)).then_inc(slots_zero, 16)

        LATE = 3 + 1 + 3 + 3 + 2 + 4 + 1 + 1 + FC + 2
        FRONT = 2 + 3 + 4 + 1 + 3 + 1

        def prep_pool(pool):
            made = [0]

            def step(ins):
                made[0] += 1
                ins.then_inc(pool_step, 1)
                pool.wait_ge(pool_step, made[0])

            pool.memset(abias[:, :], 0.0).then_inc(const_made, 1)
            pool.memset(wo0[:, :, :], 0.0).then_inc(const_made, 1)
            pool.memset(tab[:, :, :], 0.0).then_inc(const_made, 1)

            def diagonal(t, pattern, base, cm, fill=1.0, cmp=ALU.not_equal, first=0.0):
                step(pool.memset(t, first))
                return pool.affine_select(out=t, in_=t, compare_op=cmp, fill=fill, base=base, pattern=pattern,
                                          channel_multiplier=cm)

            for n in range(2):
                diagonal(sel[:, 0, n, :], [[1, 256]], P * n - (TABLE - 1), 1).then_inc(const_made, 1)
                diagonal(sel[:, 1, n, :], [[-1, 256]], P * n, 1).then_inc(const_made, 1)
            diagonal(ident[:, :], [[-1, P]], 0, 1).then_inc(const_made, 1)
            pool.memset(ones[:, :], 1.0).then_inc(const_made, 1)
            diagonal(ident_b[:, :], [[-1, P]], 0, 1).then_inc(const_made, 1)
            diagonal(anti_b[:, :], [[1, P]], -(P - 1), 1).then_inc(const_made, 1)
            pool.memset(ones_b[:, :], 1.0).then_inc(const_made, 1)
            diagonal(dsel[:, :].rearrange("p (g c) -> p g c", g=4), [[-32, 4], [0, 32]], -HD, 1).then_inc(const_made, 1)
            step(pool.memset(m48[:, :, :], 0.0))
            for n in range(3):
                step(pool.affine_select(out=m48[:, :, :], in_=m48[:, :, :], compare_op=ALU.not_equal, fill=1.0,
                                        base=-H * n, pattern=[[-1, H], [0, P]], channel_multiplier=1))
            pool.memset(big[:, 0:8192], 0.0).then_inc(zeroed_pool, 1)
            diagonal(causal_b[:, :], [[-1, P]], 0, 1, NEG, ALU.is_ge).then_inc(const_made, 1)
            diagonal(tri_b[:, :], [[1, P]], 0, -1, 0.0, ALU.is_gt, 1.0).then_inc(const_made, 1)
            pool.memset(score_scale[:, 1:3], HD ** -0.5).then_inc(const_made, 1)
            pool.memset(zero_t[:, :], 0.0).then_inc(const_made, 1)

        def prep_pe(pe):
            pe.wait_ge(const_made, 7)
            pe.wait_ge(front_loaded, 16 * FRONT)
            for w in range(2):
                for n in range(2):
                    mm = pe.matmul(pb(0)[0:H, 256 * w:256 * w + 256], tab[:, n, :], sel[:, w, n, :], start=(n == 0),
                                   stop=(n == 1), skip_group_check=True)
            mm.then_inc(table_ready, 1)
            pe.wait_ge(const_made, 12)
            pe.wait_ge(late_loaded, 16 * LATE)
            pe.wait_ge(perm_made, 3)
            for n in range(19):
                mm = pe.transpose(pb(1 + n // 4)[:, P * (n % 4):P * (n % 4) + P], wnat[:, n, :], ident[:, :])
                if n % 4 == 3 or n == 18:
                    mm.then_inc(turned, 1)
            pe.wait_ge(abs_made, 2)
            pe.matmul(pb(6)[:, 0:2], ones[:, :], wsc[:, 0:2], start=True, stop=True).then_inc(abs_total, 1)
            pe.wait_ge(tern_made, 2)
            for n in range(8):
                src = (tern1 if n < 4 else tern2)[:, P * (n % 4):P * (n % 4) + P]
                mm = pe.transpose(pb(7).bitcast(BF16)[:, P * n:P * n + P], src, ident_b[:, :])
            mm.then_inc(tern_turned, 1)

        def prep_dve(dve, link):
            dve.memset(big[:, 8192:16384], 0.0).then_inc(zeroed_dve, 1)
            link(dve.memset(nparts[:, :], 0.0))
            link(dve.memset(vpad[:, :, :, :, :], 0.0))
            link(dve.memset(vpad[:, :, :, :, HD:HD + 1], 1.0))
            dve.wait_ge(table_ready, 1)
            link(dve.tensor_copy(rows32, pb(0)[0:H, :].rearrange("h (w j) -> h w j", w=2)))
            link(dve.tensor_copy(rows32[:, 0, 0:TABLE - TR], rows32[:, 0, TABLE - TR:TABLE - TR + 1].broadcast_to(
                [H, TABLE - TR])))
            link(dve.tensor_copy(rows32[:, 1, TR:TABLE], rows32[:, 1, TR - 1:TR].broadcast_to([H, TABLE - TR])))
            dve.tensor_copy(rows_b[:, 0, :, :], rows32).then_inc(rows_made, 1)
            dve.wait_ge(rows_made, 1)
            link(dve.tensor_tensor(rowsr, rows32, rows_b[:, 0, :, :], ALU.subtract))
            dve.tensor_copy(rows_b[:, 1, :, :], rowsr).then_inc(rows_made, 1)
            dve.wait_ge(rows_made, 2)
            dve.tensor_tensor(rows_b[:, 2, :, :], rowsr, rows_b[:, 1, :, :], ALU.subtract).then_inc(rows_made, 1)
            dve.wait_ge(front_loaded, 16 * FRONT)
            link(dve.tensor_scalar(score_scale[:, 0:1], score_scale[:, 0:1], 0.1, 10.0, ALU.max, ALU.min))
            link(dve.tensor_scalar(score_scale[:, 0:1], score_scale[:, 0:1], float(D) ** 0.5, None, ALU.mult))
            link(dve.reciprocal(score_scale[:, 0:1], score_scale[:, 0:1]))
            dve.wait_ge(late_loaded, 16 * LATE)
            dve.memset(wnat[:, WT_O1:WT_O1 + 4, :], 0.0).then_inc(perm_made, 1)
            dve.wait_ge(perm_made, 1)
            link(dve.memset(wnat[:, WT_O2:WT_O2 + 4, :], 0.0))
            for n, o in ((0, WT_O1), (1, WT_O2)):
                dve.tensor_copy(wnat[:, o:o + 4, :].rearrange("p i (g d) -> p i g d", g=4)[:, :, :, 0:HD],
                                zt[0][:, n, :].rearrange("p (i g d) -> p i g d", i=4, g=4)).then_inc(perm_made, 1)
            for n, f in enumerate((f1nat, f2nat)):
                dve.tensor_reduce(wsc[:, n:n + 1], f, AX.X, ALU.add, apply_absolute_value=True).then_inc(abs_made, 1)
            dve.wait_ge(abs_total, 1)
            link(dve.tensor_scalar(wsc[:, 2:4], pb(6)[:, 0:2], 1.0 / (D * FF), 1e-5, ALU.mult, ALU.max))
            link(dve.reciprocal(wsc[:, 4:6], wsc[:, 2:4]))
            for n, (f, t) in enumerate(((f1nat, tern1), (f2nat, tern2))):
                link(dve.tensor_scalar(f, f, wsc[:, 4 + n:5 + n], MAGIC, ALU.mult, ALU.add))
                link(dve.tensor_scalar(f, f, MAGIC, 1.0, ALU.subtract, ALU.min))
                dve.tensor_scalar(t, f, -1.0, None, ALU.max).then_inc(tern_made, 1)
            for n in range(5):
                m = min(4, 19 - 4 * n)
                dve.wait_ge(turned, n + 1)
                dve.tensor_copy(wt[:, 4 * n:4 * n + m, :].rearrange("p n d -> p (n d)"), pb(1 + n)[:, 0:P * m]).then_inc(
                    wt_made, 1)
            dve.wait_ge(tern_turned, 1)
            link(dve.tensor_copy(f1t[:, :], pb(7).bitcast(BF16)[:, 0:FF]))
            dve.tensor_copy(f2t[:, :, :].rearrange("p c d -> p (c d)"), pb(7).bitcast(BF16)[:, FF:2 * FF]).then_inc(
                prep_done, 1)

        q_t, k_t, v_t, ent_t = rest[0][0][:, :], rest[0][1][:, :], rest[1][1][:, :], rest[1][0][:, :]
        v_tok, p_tok, p_t = osb[0][:, :], osb[1][:, :], onorm[:, :]
        XSCALE = float(D) ** -0.5

        def xattn_sp(sp, src, dst):
            for i in range(NIT):
                for p in range(2):
                    c = 2 * i + p
                    if i:
                        sp.wait_ge(g_ln_done[p], i)
                    sp.dma_start(xc[p], src[CT * c:CT * c + CT, :].rearrange("(b t) d -> t b d", b=CB)).then_inc(
                        g_x_loaded[p], 16)
                    sp.dma_start(cc[p], ctx_tok[CT * c:CT * c + CT, :].rearrange("(b t) d -> t b d", b=CB)).then_inc(
                        g_c_loaded[p], 16)
                for p in range(2):
                    c = 2 * i + p
                    sp.wait_ge(g_ln_done[p], i + 1)
                    sp.dma_start(dst[CT * c:CT * c + CT, :].rearrange("(b t) d -> t b d", b=CB), xo[p][:, :, :]).then_inc(
                        g_x_stored[p], 16)
            for p in range(2):
                sp.wait_ge(g_x_stored[p], 16 * NIT)

        def xattn_pe(pe, i):
            for p in range(2):
                def fill(b, k=0):
                    pe.wait_ge(b_free[b], ub(b, 0, i, p, k))

                pe.wait_ge(g_x_loaded[p], 16 * i + 16)
                fill(0)
                for j in range(CB):
                    mm = pe.transpose(pb(0)[:, P * j:P * j + P], xc[p][:, j, :], ident[:, :])
                mm.then_inc(b_ready[0], 1)
                pe.wait_ge(g_c_loaded[p], 16 * i + 16)
                fill(1)
                for j in range(CB):
                    mm = pe.transpose(pb(1)[:, P * j:P * j + P], cc[p][:, j, :], ident[:, :])
                mm.then_inc(b_ready[1], 1)
                pe.wait_ge(b_free[0], ub(0, 0, i, p) + 1)
                fill(2)
                pe.matmul(pb(2), wt[:, WT_X, :], xt[p], start=True, stop=True).then_inc(b_ready[2], 1)
                pe.wait_ge(b_free[1], ub(1, 0, i, p) + 1)
                fill(3)
                pe.matmul(pb(3), wt[:, WT_X + 1, :], ct[p], start=True, stop=True).then_inc(b_ready[3], 1)
                fill(4)
                pe.matmul(pb(4), wt[:, WT_X + 2, :], ct[p], start=True, stop=True).then_inc(b_ready[4], 1)
                pe.wait_ge(b_free[2], ub(2, 0, i, p) + 1)
                fill(5)
                pe.matmul(pb(5), wt[:, WT_X + 3, :], q_t, start=True, stop=False)
                pe.wait_ge(b_free[3], ub(3, 0, i, p) + 1)
                pe.matmul(pb(5), wt[:, WT_X + 4, :], k_t, start=False, stop=True).then_inc(b_ready[5], 1)
                pe.wait_ge(b_free[4], ub(4, 0, i, p) + 1)
                fill(6)
                for j in range(CB):
                    mm = pe.transpose(pb(6)[:, P * j:P * j + P], v_t[:, P * j:P * j + P], ident[:, :])
                mm.then_inc(b_ready[6], 1)
                pe.wait_ge(b_free[5], ub(5, 0, i, p) + 1)
                fill(7)
                for j in range(CB):
                    mm = pe.matmul(pb(7)[:, P * j:P * j + P], ent_t[:, P * j:P * j + P], v_t[:, P * j:P * j + P],
                                   start=True, stop=True, skip_group_check=True)
                mm.then_inc(b_ready[7], 1)
                pe.wait_ge(b_free[7], ub(7, 0, i, p) + 1)
                for j in range(CB):
                    mm = pe.transpose(pb(0)[:, P * j:P * j + P], p_tok[:, P * j:P * j + P], ident[:, :])
                mm.then_inc(b_ready[0], 1)
                pe.wait_ge(b_free[0], ub(0, 0, i, p, 1) + 1)
                pe.wait_ge(b_free[6], ub(6, 0, i, p) + 1)
                for j in range(CB):
                    mm = pe.matmul(pb(1)[:, P * j:P * j + P], p_t[:, P * j:P * j + P], v_tok[:, P * j:P * j + P],
                                   start=True, stop=True, skip_group_check=True)
                mm.then_inc(b_ready[1], 1)

        def xattn_act(act, i):
            for p in range(2):
                act.wait_ge(b_ready[0], ub(0, 0, i, p) + 1)
                act.copy(xt[p], pb(0)).then_inc(b_free[0], 1)
                act.wait_ge(b_ready[2], ub(2, 0, i, p) + 1)
                act.activation(q_t, pb(2), ACT.Identity, bias=xbias[:, 0:1]).then_inc(b_free[2], 1)
                act.wait_ge(b_ready[4], ub(4, 0, i, p) + 1)
                act.activation(v_t, pb(4), ACT.Identity, bias=xbias[:, 2:3]).then_inc(b_free[4], 1)
                act.wait_ge(b_ready[5], ub(5, 0, i, p) + 1)
                act.activation(ent_t, pb(5), ACT.Tanh, bias=xbias[:, 3:4]).then_inc(b_free[5], 1)
                act.wait_ge(nbias_ready, 2 * i + p + 1)
                for j in range(CB):
                    ins = act.activation(p_tok[:, P * j:P * j + P], pb(7)[:, P * j:P * j + P], ACT.Exp,
                                         bias=small[:, 0, j:j + 1], scale=XSCALE, accum_out=small[:, 1, j:j + 1])
                ins.then_inc(b_free[7], 1)

        def xattn_dve(dve, link, i):
            for p in range(2):
                dve.wait_ge(b_ready[1], ub(1, 0, i, p) + 1)
                dve.tensor_copy(ct[p], pb(1)).then_inc(b_free[1], 1)
                dve.wait_ge(b_ready[3], ub(3, 0, i, p) + 1)
                dve.tensor_scalar(k_t, pb(3), xbias[:, 1:2], None, ALU.add).then_inc(b_free[3], 1)
                dve.wait_ge(b_ready[6], ub(6, 0, i, p) + 1)
                dve.tensor_copy(v_tok, pb(6)).then_inc(b_free[6], 1)
                dve.wait_ge(b_ready[7], ub(7, 0, i, p) + 1)
                link(dve.tensor_reduce(small[:, 0, 0:CB], four(pb(7)), AX.X, ALU.max, negate=True))
                dve.tensor_scalar(small[:, 0, 0:CB], small[:, 0, 0:CB], XSCALE, None, ALU.mult).then_inc(nbias_ready, 1)
                dve.wait_ge(b_ready[0], ub(0, 0, i, p, 1) + 1)
                dve.tensor_copy(p_t, pb(0)).then_inc(b_free[0], 1)
                link(dve.reciprocal(small[:, 2, 0:CB], small[:, 1, 0:CB]))
                dve.wait_ge(b_ready[1], ub(1, 0, i, p, 1) + 1)
                for j in range(CB):
                    ins = dve.scalar_tensor_tensor(zt[p][:, j, :], pb(1)[:, P * j:P * j + P], small[:, 2, j:j + 1],
                                                   xc[p][:, j, :], ALU.mult, ALU.add)
                    if j < CB - 1:
                        link(ins)
                ins.then_inc(b_free[1], 1)
                dve.wait_ge(b_free[1], ub(1, 0, i, p, 1) + 1)
                for j in range(CB):
                    link(dve.bn_stats(stats[:, j, :], zt[p][:, j, :]))
                dve.wait_ge(g_x_stored[p], 16 * i)
                layernorm(dve, link, zt[p], CB, xo[p]).then_inc(g_ln_done[p], 1)

        XATTN_STEPS = 2 * (1 + 1 + CB - 1 + CB + LN_STEPS + CB - 1)

        xt_all = scratch_e[:, 0:2048]
        tmps = scratch_e[:, 2048:4096].rearrange("p (n m) -> p n m", n=8)
        shift_sb, exp_sb, cand_sb, cnt_sb, cum_sb, base_sb, rank_sb = (tmps[:, n, :] for n in range(7))
        onehot_b = tmps[:, 7, 0:P].bitcast(BF16)
        consts = mx[:, :].rearrange("p (n m) -> p n m", n=4)
        iota_e, iota_e64, seg, iota_i = (consts[:, n, :] for n in range(4))
        h_sb = [qkp32[:, FF * u:FF * u + FF] for u in range(2)]
        hT_sb = [qkp32[:, 2 * FF + FF * u:2 * FF + FF * u + FF] for u in range(2)]
        xs_sb = [rest[g][0][:, :] for g in range(2)]
        ys_sb = chunks[:, :, :].rearrange("p a b -> p (a b)")
        xsT_sb = [qkp32[:, 4 * FF + 2 * D + D * u:4 * FF + 2 * D + D * u + D] for u in range(2)]

        def te(ap):
            return ap.rearrange("p (t e) -> p t e", e=E)

        def et(ap):
            return ap.rearrange("p (e t) -> p e t", e=E)

        (LMAX, EMAX, ESUM, EREC, WSEL, IDX, NEXP, BLK, BEND, BSTART, POS, POSI) = range(12)
        SEG1 = 12
        GRP = 4
        GROUPS = [(j, min(j + GRP, NB)) for j in range(0, NB, GRP)]
        TURNS = (NB - GRP) // (2 * GRP)

        def moe_sp(sp, src, dst):
            sp.dma_start(tok_x, src.rearrange("(b t) d -> t b d", b=NSEQ)).then_inc(moe_loaded, 16)
            sp.dma_start(w1_sb.rearrange("p (e f) -> p e f", e=E), a["L0_ffn_W1"].rearrange("e d f -> d e f")).then_inc(w1_loaded, 16)
            sp.dma_start(w2_sb.rearrange("p (e c d) -> p e c d", e=E, c=FC),
                         a["L0_ffn_W2"].rearrange("e (c p) d -> p e c d", p=P)).then_inc(w2_loaded, 16)

            def store(l, j0, j1):
                sp.wait_ge(y_made, NB * l + j1)
                sp.dma_start(slots_y[P * j0:P * j1, :].rearrange("(b p) d -> p b d", p=P),
                             ys_sb[:, D * j0:D * j1].rearrange("p (b d) -> p b d", d=D)).then_inc(y_stored, 16)

            for l in range(NL):
                sp.wait_ge(scattered, 16 * NSEQ * (l + 1))
                for g, (j0, j1) in enumerate(GROUPS):
                    if g >= 2:
                        sp.wait_ge(xsT_ready, NB * l + GRP * (g - 1))
                    sp.dma_start(xs_sb[g % 2][:, 0:D * (j1 - j0)].rearrange("p (b d) -> p b d", d=D),
                                 slots_x[P * j0:P * j1, :].rearrange("(b p) d -> p b d", p=P)).then_inc(xs_loaded, 16)
                    sp.wait_ge(xs_loaded, 16 * (len(GROUPS) * l + g + 1))
                    if g >= 2:
                        store(l, *GROUPS[g - 2])
                for g in (-2, -1):
                    store(l, *GROUPS[g])
            sp.wait_ge(moe_ln, 1)
            sp.dma_start(dst.rearrange("(b t) d -> t b d", b=NSEQ), tok_x).then_inc(moe_stored, 16)
            sp.wait_ge(moe_stored, 16)

        def moe_pool(pool):
            pool.wait_ge(moe_loaded, 16)
            ii = iota_i.bitcast(I32)
            base = pool_steps[0]
            pool.iota(ii, pattern=[[0, NSEQ], [1, E]], base=0, channel_multiplier=0).then_inc(pool_step, 1)
            pool.wait_ge(pool_step, base + 1)
            pool.tensor_copy(iota_e, ii).then_inc(pool_step, 1)
            pool.wait_ge(pool_step, base + 2)
            pool.tensor_scalar(iota_e64, iota_e, 64.0, None, ALU.add).then_inc(pool_step, 1)
            pool.memset(seg, 1.0).then_inc(pool_step, 1)
            pool.wait_ge(pool_step, base + 4)
            pool.memset(et(seg)[:, :, 0:1], 0.0).then_inc(pool_step, 1)
            pool.memset(small[:, SEG1, :], 1.0).then_inc(pool_step, 1)
            pool.wait_ge(pool_step, base + 6)
            pool.iota(blocks_i, pattern=[[1, NB]], base=0, channel_multiplier=0).then_inc(pool_step, 1)
            pool.wait_ge(pool_step, base + 7)
            pool.tensor_copy(blocks_f, blocks_i).then_inc(pool_step, 1)
            for l in range(NL):
                pool.wait_ge(pos_ready, l + 1)
                if l == 0:
                    pool.wait_ge(slots_zero, 16)
                for t in range(NSEQ):
                    pool.indirect_dma_start(out=slots_x, out_offset=bass.IndirectOffsetOnAxis(
                        ap=posi[:, t:t + 1], axis=0), in_=tok_x[:, t, :], in_offset=None).then_inc(scattered, 16)
                pool.wait_ge(y_stored, 16 * len(GROUPS) * (l + 1))
                for t in range(NSEQ):
                    pool.indirect_dma_start(out=tok_y[:, t, :], out_offset=None, in_=slots_y,
                                            in_offset=bass.IndirectOffsetOnAxis(ap=posi[:, t:t + 1], axis=0)).then_inc(
                                                gathered[t // 4], 16)

        posi = small[:, POSI, :].bitcast(I32)
        blk_tab = sb("blk_tab", [P, 4, NB])
        blocks_i = blk_tab[:, 0, :].bitcast(I32)
        blocks_f = blk_tab[:, 1, :]
        bexp = blk_tab[:, 2, :]
        boff = blk_tab[:, 3, :].bitcast(I32)
        cmp_sb = sb("cmp_sb", [P, NB * E])
        pool_steps = [8 + 4 + 2]

        def block_steps(eng, step):
            for j in range(GRP):
                step(j, j, 0 if j == 0 else None)
            with eng.Fori(0, TURNS, 1) as k:
                for m in range(GRP, 3 * GRP):
                    step(2 * GRP * k + m, m % (2 * GRP), 2 * k + m // GRP if m % GRP == 0 else None)
            for j in range(GRP + 2 * GRP * TURNS, NB + 3):
                step(j, j % (2 * GRP), j // GRP if j % GRP == 0 and j < NB else None)

        def moe_pe(pe, l):
            for g in range(4):
                if g == 0:
                    pe.wait_ge(tok_made, l)
                for j in range(4):
                    mm = pe.transpose(pb(g)[:, P * j:P * j + P], tok_x[:, 4 * g + j, :], ident[:, :])
                mm.then_inc(xturn_ready, 1)
            for g in range(4):
                pe.wait_ge(xturn_a if g % 2 == 0 else xturn_d, 2 * l + g // 2 + 1)
                for j in range(4):
                    t = 4 * g + j
                    mm = pe.matmul(pb(4)[:, E * t:E * t + E], xt_all[:, P * t:P * t + P],
                                   router_sb[:, bass.ds(E * l, E)], start=True, stop=True, skip_group_check=True)
            mm.then_inc(logits_ready, 1)
            pe.wait_ge(onehot_ready, l + 1)
            pe.matmul(pb(5)[:, 0:NSEQ * E], tri_b[:, :], onehot_b, start=True, stop=True, skip_group_check=True)
            pe.matmul(pb(5)[:, NSEQ * E:2 * NSEQ * E], ones_b[:, :], onehot_b, start=True, stop=True,
                      skip_group_check=True).then_inc(counts_ready, 1)
            pe.wait_ge(block_ready, l + 1)

            def offset(j):
                return pe.value_load(boff[0:1, bass.ds(j, 1)], min_val=0, max_val=(E - 1) * FF)

            def turn_x(j, m, u, k):
                if k is not None:
                    pe.wait_ge(xs_loaded, 16 * (len(GROUPS) * l + k + 1))
                pe.wait_ge(xsT_made, NB * l + j - 1 if not isinstance(j, int) or j > 0 else NB * l)
                pe.transpose(pb(u)[:, 0:P], xs_sb[m // GRP][:, D * (m % GRP):D * (m % GRP) + D], ident[:, :]).then_inc(xsT_ready, 1)

            def hidden(j, u):
                e = offset(j)
                pe.wait_ge(xsT_made, NB * l + j + 1)
                pe.wait_ge(h_made, NB * l + j - 1 if not isinstance(j, int) or j > 0 else NB * l)
                pe.matmul(pb(2 + u), xsT_sb[u], w1_sb[:, bass.ds(e, FF)], start=True, stop=True).then_inc(h_ready, 1)

            def turn_h(j, u):
                pe.wait_ge(h_made, NB * l + j + 1)
                pe.wait_ge(hT_made, NB * l + j - 1 if not isinstance(j, int) or j > 0 else NB * l)
                for c in range(FC):
                    mm = pe.transpose(pb(4 + u)[:, P * c:P * c + P], h_sb[u][:, P * c:P * c + P], ident[:, :])
                mm.then_inc(hT_ready, 1)

            def out_rows(j, u):
                e = offset(j)
                pe.wait_ge(hT_made, NB * l + j + 1)
                pe.wait_ge(y_made, NB * l + j - 1 if not isinstance(j, int) or j > 0 else NB * l)
                for c in range(FC):
                    mm = pe.matmul(pb(6 + u)[:, 0:D], hT_sb[u][:, P * c:P * c + P], w2_sb[:, bass.ds(e + P * c, D)],
                                   start=(c == 0), stop=(c == FC - 1))
                mm.then_inc(y_ready, 1)

            def step(j, m, k=None):
                u = m % 2
                known = isinstance(j, int)
                if not known or j < NB:
                    turn_x(j, m, u, k)
                if not known or 0 <= j - 1 < NB:
                    hidden(j - 1, 1 - u)
                if not known or 0 <= j - 2 < NB:
                    turn_h(j - 2, u)
                if not known or 0 <= j - 3 < NB:
                    out_rows(j - 3, 1 - u)

            pe.wait_ge(w1_loaded, 16)
            pe.wait_ge(w2_loaded, 16)
            block_steps(pe, step)

        def moe_act(act, l):
            for g in (0, 2):
                act.wait_ge(xturn_ready, 4 * l + g + 1)
                act.copy(xt_all[:, 512 * g:512 * g + 512], pb(g)).then_inc(xturn_a, 1)
            act.wait_ge(shifted, l + 1)
            act.activation(exp_sb, shift_sb, ACT.Exp).then_inc(expd, 1)

            def step(j, m, k=None):
                u = m % 2
                known = isinstance(j, int)
                if not known or 0 <= j - 1 < NB:
                    act.wait_ge(h_ready, NB * l + j)
                    act.activation(h_sb[1 - u], pb(2 + 1 - u), ACT.Silu).then_inc(h_made, 1)
                if not known or 0 <= j - 3 < NB:
                    act.wait_ge(y_ready, NB * l + j - 2)
                    act.copy(ys_sb[:, bass.ds((j - 3) * D, D)], pb(6 + 1 - u)[:, 0:D]).then_inc(y_made, 1)

            block_steps(act, step)

        def moe_dve(dve, link, l):
            sm = small
            for g in (1, 3):
                dve.wait_ge(xturn_ready, 4 * l + g + 1)
                dve.tensor_copy(xt_all[:, 512 * g:512 * g + 512], pb(g)).then_inc(xturn_d, 1)
            dve.wait_ge(logits_ready, l + 1)
            logits = te(pb(4)[:, 0:NSEQ * E])
            link(dve.tensor_reduce(sm[:, LMAX, :], logits, AX.X, ALU.max))
            dve.tensor_tensor(te(shift_sb), logits, along(sm[:, LMAX, :], E), ALU.subtract).then_inc(shifted, 1)
            dve.wait_ge(expd, l + 1)
            link(dve.tensor_reduce(sm[:, EMAX, :], te(exp_sb), AX.X, ALU.max))
            link(dve.tensor_reduce(sm[:, ESUM, :], te(exp_sb), AX.X, ALU.add))
            link(dve.reciprocal(sm[:, EREC, :], sm[:, ESUM, :]))
            link(dve.tensor_tensor(sm[:, WSEL, :], sm[:, EMAX, :], sm[:, EREC, :], ALU.mult))
            link(dve.tensor_tensor(te(cand_sb), te(exp_sb), along(sm[:, EMAX, :], E), ALU.is_equal))
            link(dve.scalar_tensor_tensor(cand_sb, cand_sb, -64.0, iota_e64, ALU.mult, ALU.add))
            link(dve.tensor_reduce(sm[:, IDX, :], te(cand_sb), AX.X, ALU.min))
            dve.tensor_tensor(te(onehot_b), te(iota_e), along(sm[:, IDX, :], E), ALU.is_equal).then_inc(onehot_ready, 1)
            dve.wait_ge(counts_ready, l + 1)
            link(dve.tensor_copy(et(cnt_sb), te(pb(5)[:, NSEQ * E:2 * NSEQ * E]).rearrange("p t e -> p e t")))
            link(dve.tensor_tensor_scan(cum_sb, seg, cnt_sb, 0.0, ALU.mult, ALU.add))
            link(dve.tensor_scalar(sm[:, NEXP, :], et(cum_sb)[:, :, NSEQ - 1], 1.0 / P,
                                   (P - 1) / P - 0.5 + 0.5 / P, ALU.mult, ALU.add))
            link(dve.tensor_scalar(sm[:, NEXP, :], sm[:, NEXP, :], MAGIC, None, ALU.add))
            link(dve.tensor_scalar(sm[:, BLK, :], sm[:, NEXP, :], MAGIC, None, ALU.subtract))
            link(dve.tensor_tensor_scan(sm[:, BEND, :], sm[:, SEG1, :], sm[:, BLK, :], 0.0, ALU.mult, ALU.add))
            link(dve.tensor_tensor(sm[:, BSTART, :], sm[:, BEND, :], sm[:, BLK, :], ALU.subtract))
            link(dve.tensor_tensor(base_sb, cum_sb, cnt_sb, ALU.subtract))
            link(dve.scalar_tensor_tensor(et(base_sb), along(sm[:, BSTART, :], NSEQ), float(P), et(base_sb),
                                          ALU.mult, ALU.add))
            link(dve.tensor_tensor(te(rank_sb), te(pb(5)[:, 0:NSEQ * E]), et(base_sb).rearrange("p e t -> p t e"),
                                   ALU.add))
            link(dve.tensor_tensor(rank_sb, rank_sb, onehot_b, ALU.mult))
            link(dve.tensor_reduce(sm[:, POS, :], te(rank_sb), AX.X, ALU.add))
            dve.tensor_copy(posi, sm[:, POS, :]).then_inc(pos_ready, 1)
            link(dve.tensor_tensor(te(cmp_sb[:, :]), over(sm[:, BEND, :], NB), along(blocks_f, E), ALU.is_le))
            link(dve.tensor_reduce(bexp, te(cmp_sb[:, :]), AX.X, ALU.add))
            link(dve.tensor_scalar(bexp, bexp, float(E - 1), float(FF), ALU.min, ALU.mult))
            dve.tensor_copy(boff, bexp).then_inc(block_ready, 1)

            def step(j, m, k=None):
                u = m % 2
                known = isinstance(j, int)
                if not known or j < NB:
                    dve.wait_ge(xsT_ready, NB * l + j + 1)
                    dve.tensor_copy(xsT_sb[u], pb(u)[:, 0:P]).then_inc(xsT_made, 1)
                if not known or 0 <= j - 2 < NB:
                    dve.wait_ge(hT_ready, NB * l + j - 1)
                    dve.tensor_copy(hT_sb[u], pb(4 + u)).then_inc(hT_made, 1)

            block_steps(dve, step)
            for g in range(4):
                dve.wait_ge(gathered[g], 16 * 4 * (l + 1))
                ins = dve.tensor_tensor(tok_x[:, 4 * g:4 * g + 4, :], tok_y[:, 4 * g:4 * g + 4, :],
                                        along(sm[:, WSEL, 4 * g:4 * g + 4], D), ALU.mult)
            ins.then_inc(tok_made, 1)

        MOE_STEPS = 8 + 12 + 3

        def moe_end_dve(dve, link):
            link(dve.tensor_tensor(tok_in, tok_in, tok_x, ALU.add))
            for t in range(NSEQ):
                link(dve.bn_stats(stats[:, t, :], tok_in[:, t, :]))
            layernorm(dve, link, tok_in, NSEQ, tok_x).then_inc(moe_ln, 1)

        hp = [scratch_b[:, 528 * c:528 * c + 520].rearrange("p (b t) -> p b t", b=CB) for c in range(FC)]
        xq_f = scratch_b[:, 2112:2624]
        diag = scratch_b[:, 2624:3136]
        inv_rows = scratch_b[:, 3136:3648]
        hc = [scratch_b[:, 3648 + 512 * n:4160 + 512 * n] for n in range(2)]
        q_f = [scratch_b[:, 4672 + 512 * n:5184 + 512 * n] for n in range(2)]
        magic_t = scratch_b[:, 5700:5701]
        hs = scratch_e[:, 0:2048].rearrange("p (c t) -> p c t", c=FC)
        xq_b = scratch_e[:, 2048:2304].bitcast(BF16)
        xqT_b = scratch_e[:, 2304:2560].bitcast(BF16)
        hq_b = [scratch_e[:, 2560 + 256 * n:2816 + 256 * n].bitcast(BF16) for n in range(2)]
        hqT_b = [scratch_e[:, 3072 + 256 * n:3328 + 256 * n].bitcast(BF16) for n in range(2)]

        def ffn_sp(sp, src, dst):
            for i in range(NIT):
                for p in range(2):
                    c = 2 * i + p
                    if i:
                        sp.wait_ge(g_ln_done[p], NIT + i)
                    sp.dma_start(xc[p], src[CT * c:CT * c + CT, :].rearrange("(b t) d -> t b d", b=CB)).then_inc(
                        g_x_loaded[p], 16)
                for p in range(2):
                    c = 2 * i + p
                    sp.wait_ge(g_ln_done[p], NIT + i + 1)
                    sp.dma_start(dst[CT * c:CT * c + CT, :].rearrange("(b t) d -> t b d", b=CB), xo[p][:, :, :]).then_inc(
                        g_x_stored[p], 16)
            for p in range(2):
                sp.wait_ge(g_x_stored[p], 16 * 2 * NIT)

        def ffn_pe(pe, i):
            for p in range(2):
                n = 2 * i + p

                def fill(b, k=0):
                    pe.wait_ge(b_free[b], ub(b, 1, i, p, k))

                pe.wait_ge(xq_made, n + 1)
                fill(0)
                for j in range(CB):
                    mm = pe.transpose(pb(0).bitcast(BF16)[:, P * j:P * j + P], xq_b[:, P * j:P * j + P], ident_b[:, :])
                mm.then_inc(b_ready[0], 1)
                fill(1)
                pe.matmul(pb(1), ones[:, :], diag, start=True, stop=True).then_inc(b_ready[1], 1)
                pe.wait_ge(b_free[0], ub(0, 1, i, p) + 1)
                for c in range(FC):
                    fill(2 + c % 2, c // 2)
                    pe.matmul(pb(2 + c % 2), f1t[:, P * c:P * c + P], xqT_b, start=True, stop=True).then_inc(
                        b_ready[2 + c % 2], 1)

                def turn(j):
                    fill(4 + j % 2, j // 2)
                    for c in range(FC):
                        mm = pe.transpose(pb(4 + j % 2)[:, P * c:P * c + P], hs[:, c, P * j:P * j + P], ident[:, :])
                    mm.then_inc(b_ready[4 + j % 2], 1)

                def down(j):
                    pe.wait_ge(hq_made, CB * n + j + 1)
                    fill(6, j)
                    for c in range(FC):
                        mm = pe.transpose(pb(6).bitcast(BF16)[:, P * c:P * c + P], hq_b[j % 2][:, P * c:P * c + P],
                                          ident_b[:, :])
                    mm.then_inc(b_ready[6], 1)
                    pe.wait_ge(b_free[6], ub(6, 1, i, p, j) + 1)
                    fill(7, j)
                    for c in range(FC):
                        mm = pe.matmul(pb(7)[:, 0:D], hqT_b[j % 2][:, P * c:P * c + P], f2t[:, c, :], start=(c == 0),
                                       stop=(c == FC - 1))
                    mm.then_inc(b_ready[7], 1)

                pe.wait_ge(silu_made, FC * n + FC)
                turn(0)
                for j in range(CB):
                    if j + 1 < CB:
                        turn(j + 1)
                    down(j)

        def ffn_act(act, i):
            for p in range(2):
                n = 2 * i + p
                act.wait_ge(b_ready[0], ub(0, 1, i, p) + 1)
                act.copy(xqT_b, pb(0).bitcast(BF16)[:, 0:512]).then_inc(b_free[0], 1)
                act.wait_ge(b_ready[1], ub(1, 1, i, p) + 1)
                act.copy(inv_rows, pb(1)).then_inc(b_free[1], 1)
                for c in range(FC):
                    act.wait_ge(conv_made, FC * n + c + 1)
                    act.activation(hs[:, c, :], hc[c % 2], ACT.Silu).then_inc(silu_made, 1)
                for j in range(CB):
                    act.wait_ge(qscale_made, CB * n + j + 1)
                    act.activation(q_f[j % 2], pb(4 + j % 2), ACT.Identity, bias=magic_t,
                                   scale=small[:, 4 + j, 0:1]).then_inc(b_free[4 + j % 2], 1)
                    act.wait_ge(b_ready[6], ub(6, 1, i, p, j) + 1)
                    act.copy(hqT_b[j % 2], pb(6).bitcast(BF16)[:, 0:512]).then_inc(b_free[6], 1)

        def ffn_dve(dve, link, i):
            for p in range(2):
                n = 2 * i + p
                dve.wait_ge(g_x_loaded[p], 16 * (NIT + i + 1))
                am, sc, inv = small[:, 0, 0:CB], small[:, 1, 0:CB], small[:, 2, 0:CB]
                link(dve.tensor_reduce(am, xc[p], AX.X, ALU.max, apply_absolute_value=True))
                link(dve.tensor_scalar(am, am, 1e-5, None, ALU.max))
                link(dve.reciprocal(sc, am))
                link(dve.tensor_scalar(sc, sc, 127.0, None, ALU.mult))
                link(dve.tensor_scalar(inv, am, 1.0 / 127.0, wsc[:, 2:3], ALU.mult, ALU.mult))
                for j in range(CB):
                    link(dve.tensor_scalar(xq_f[:, P * j:P * j + P], xc[p][:, j, :], sc[:, j:j + 1], MAGIC, ALU.mult,
                                           ALU.add))
                for j in range(CB):
                    link(dve.tensor_scalar(diag[:, P * j:P * j + P], ident[:, :], inv[:, j:j + 1], None, ALU.mult))
                dve.tensor_scalar(xq_b, xq_f, MAGIC, 127.0, ALU.subtract, ALU.min).then_inc(xq_made, 1)
                dve.wait_ge(b_free[1], ub(1, 1, i, p) + 1)
                for c in range(FC):
                    b = 2 + c % 2
                    dve.wait_ge(b_ready[b], ub(b, 1, i, p, c // 2) + 1)
                    dve.tensor_tensor(hp[c][:, :, 1:P + 1], four(pb(b)), four(inv_rows), ALU.mult).then_inc(b_free[b], 1)
                    dve.wait_ge(b_free[b], ub(b, 1, i, p, c // 2) + 1)
                    dve.wait_ge(silu_made, max(FC * n + c - 1, 0) if isinstance(i, int) else FC * n + max(c - 1, 0))
                    t = four(hc[c % 2])
                    link(dve.tensor_scalar(t, hp[c][:, :, 0:P], conv_w[:, c, 0:1], conv_b[:, c:c + 1], ALU.mult, ALU.add))
                    link(dve.scalar_tensor_tensor(t, hp[c][:, :, 1:P + 1], conv_w[:, c, 1:2], t, ALU.mult, ALU.add))
                    dve.scalar_tensor_tensor(t, hp[c][:, :, 2:P + 2], conv_w[:, c, 2:3], t, ALU.mult, ALU.add).then_inc(
                        conv_made, 1)

                def out_row(j):
                    dve.wait_ge(b_ready[7], ub(7, 1, i, p, j) + 1)
                    dve.scalar_tensor_tensor(zt[p][:, j, :], pb(7)[:, 0:D], small[:, 4 + j, 1:2], xc[p][:, j, :],
                                             ALU.mult, ALU.add).then_inc(b_free[7], 1)
                    dve.wait_ge(b_free[7], ub(7, 1, i, p, j) + 1)
                    link(dve.bn_stats(stats[:, j, :], zt[p][:, j, :]))

                for j in range(CB):
                    b = 4 + j % 2
                    q = small[:, 4 + j, :]
                    dve.wait_ge(b_ready[b], ub(b, 1, i, p, j // 2) + 1)
                    link(dve.tensor_reduce(q[:, 2:3], pb(b), AX.X, ALU.max, apply_absolute_value=True))
                    link(dve.tensor_scalar(q[:, 2:3], q[:, 2:3], 1e-5, None, ALU.max))
                    link(dve.reciprocal(q[:, 3:4], q[:, 2:3]))
                    link(dve.tensor_scalar(q[:, 1:2], q[:, 2:3], 1.0 / 127.0, wsc[:, 3:4], ALU.mult, ALU.mult))
                    dve.tensor_scalar(q[:, 0:1], q[:, 3:4], 127.0, None, ALU.mult).then_inc(qscale_made, 1)
                    if j:
                        out_row(j - 1)
                    dve.wait_ge(b_free[b], ub(b, 1, i, p, j // 2) + 1)
                    dve.tensor_scalar(hq_b[j % 2], q_f[j % 2], MAGIC, 127.0, ALU.subtract, ALU.min).then_inc(hq_made, 1)
                out_row(CB - 1)
                dve.wait_ge(g_x_stored[p], 16 * (NIT + i))
                layernorm(dve, link, zt[p], CB, xo[p]).then_inc(g_ln_done[p], 1)

        FFN_STEPS = 2 * (5 + 2 * CB + 2 * FC + CB + 4 * CB + LN_STEPS + CB - 1)

        @block.sync
        def _(sp):
            prep_sp(sp)
            attn_sp(sp, 0, x_stage[0], x_stage[1])
            xattn_sp(sp, x_stage[1], x_stage[2])
            moe_sp(sp, x_stage[2], x_stage[3])
            attn_sp(sp, 1, x_stage[3], x_stage[4])
            sp.dma_start(mask_int.rearrange("q (b k) -> q b k", b=NSEQ),
                         a["mask_Bx1xSxS2_if1"].rearrange("b o q k -> q (b o) k")).then_inc(mask_loaded, 16)
            attn_sp(sp, 2, x_stage[4], x_stage[5])
            ffn_sp(sp, x_stage[5], x_stage[6])

        @block.tensor
        def _(pe):
            prep_pe(pe)
            pe.wait_ge(const_made, 17)
            pe.wait_ge(prep_done, 1)
            pe.wait_ge(bias_loaded, 16 * 6)
            with pe.Fori(0, NIT, 1) as i:
                attn_pe(pe, 0, i)
            with pe.Fori(0, NIT, 1) as i:
                xattn_pe(pe, i)
            pe.wait_ge(moe_loaded, 16)
            with pe.Fori(0, NL, 1) as l:
                moe_pe(pe, l)
            with pe.Fori(0, NIT, 1) as i:
                attn_pe(pe, 1, i)
            pe.wait_ge(mask_made, 1)
            pe.wait_ge(rows_added, 16)
            with pe.Fori(0, NIT, 1) as i:
                attn_pe(pe, 2, i)
            with pe.Fori(0, NIT, 1) as i:
                ffn_pe(pe, i)

        @block.scalar
        def _(act):
            act.wait_ge(prep_done, 1)
            act.wait_ge(rows_stored, 16 * 3)
            act.wait_ge(const_made, 17)
            with act.Fori(0, NIT, 1) as i:
                attn_act(act, 0, i)
            with act.Fori(0, NIT, 1) as i:
                xattn_act(act, i)
            with act.Fori(0, NL, 1) as l:
                moe_act(act, l)
            with act.Fori(0, NIT, 1) as i:
                attn_act(act, 1, i)
            with act.Fori(0, NIT, 1) as i:
                attn_act(act, 2, i)
            with act.Fori(0, NIT, 1) as i:
                ffn_act(act, i)

        @block.gpsimd
        def _(pool):
            prep_pool(pool)
            for i in range(NIT):
                attn_pool(pool, 0, i)
            moe_pool(pool)
            pool.wait_ge(moe_ln, 1)
            pool.memset(big[:, 0:8192], 0.0).then_inc(zeroed_pool, 1)
            for i in range(NIT):
                attn_pool(pool, 1, i)
            for i in range(NIT):
                attn_pool(pool, 2, i)

        @block.vector
        def _(dve):
            link = Chain(dve)
            prep_dve(dve, link)
            dve.wait_ge(const_made, 17)
            looped(dve, link, lambda i: attn_dve(dve, link, 0, i), NIT, ATTN_STEPS)
            looped(dve, link, lambda i: xattn_dve(dve, link, i), NIT, XATTN_STEPS)
            dve.wait_ge(moe_loaded, 16)
            dve.wait_ge(pool_step, pool_steps[0] + 8)
            link(dve.tensor_copy(tok_in, tok_x))
            looped(dve, link, lambda l: moe_dve(dve, link, l), NL, MOE_STEPS)
            dve.wait_ge(tok_made, NL)
            moe_end_dve(dve, link)
            dve.memset(big[:, 8192:16384], 0.0).then_inc(zeroed_dve, 1)
            looped(dve, link, lambda i: attn_dve(dve, link, 1, i), NIT, ATTN_STEPS)
            dve.wait_ge(mask_loaded, 16)
            dve.tensor_scalar(mask_neg.rearrange("p b k -> p (b k)"), mask_int, 0.0, NEG, ALU.is_equal,
                              ALU.mult).then_inc(mask_made, 1)
            looped(dve, link, lambda i: attn_dve(dve, link, 2, i), NIT, ATTN_STEPS)
            link(dve.memset(scratch_b[:, 0:2112], 0.0))
            link(dve.memset(magic_t, MAGIC))
            looped(dve, link, lambda i: ffn_dve(dve, link, i), NIT, FFN_STEPS)


_INS = ["x", "ctx_1024", "mask_Bx1xSxS2_if1",
        "L0_attn_Wq", "L0_attn_bq", "L0_attn_Wk", "L0_attn_bk", "L0_attn_Wv", "L0_attn_bv", "L0_attn_Wp", "L0_attn_bp",
        "L0_attn_bias_table", "L0_attn_temperature",
        "L0_xattn_Wq", "L0_xattn_bq", "L0_xattn_Wk", "L0_xattn_bk", "L0_xattn_Wv", "L0_xattn_bv", "L0_xattn_We",
        "L0_xattn_be", "L0_ffn_routers", "L0_ffn_W1", "L0_ffn_W2",
        "L1_attn_Wq", "L1_attn_Wk", "L1_attn_Wv", "L1_attn_Wo",
        "L1_xattn_Wq", "L1_xattn_Wk", "L1_xattn_Wv", "L1_xattn_Wo", "L1_xattn_bo",
        "L1_ffn_w1", "L1_ffn_conv_w", "L1_ffn_conv_b", "L1_ffn_w2"]


def kernel(**inputs):
    import numpy as _np
    import concourse.bacc as _bacc
    from concourse import mybir as _mybir
    from concourse.bass_utils import run_bass_kernel_spmd as _run

    nc = _bacc.Bacc("TRN2", target_bir_lowering=False, num_devices=1)
    arrays, args = {}, {}
    for name in _INS:
        arr = _np.ascontiguousarray(inputs[name])
        arrays[f"in_{name}"] = arr
        args[name] = nc.dram_tensor(f"in_{name}", arr.shape, _mybir.dt.from_np(arr.dtype), kind="ExternalInput").ap()
    out = nc.dram_tensor("out_0", (NSEQ, P, D), F32, kind="ExternalOutput").ap()
    decoder(nc, args, out)
    r = _run(nc, [arrays], core_ids=[0])
    return r.results[0]["out_0"]
```

```python
from contextlib import ExitStack

import concourse.bass as bass
from concourse import mybir

F32 = mybir.dt.float32
BF16 = mybir.dt.bfloat16
I32 = mybir.dt.int32
ALU = mybir.AluOpType
ACT = mybir.ActivationFunctionType
AX = mybir.AxisListType

P = 128
D = 128
NSEQ = 16
H = 16
HD = D // H
CB = 4
CT = CB * P
NCH = NSEQ // CB
NIT = NCH // 2
QUADS = H // 4
E = 16
FF = 512
FC = FF // P
NL = 4
NB = NSEQ + E - 1
EPS = 1e-5
MAGIC = 1.5 * 2.0 ** 23
NEG = -2.0 ** 66
RSQRT_SEED = 0x5F3759DF
Q_TERMS = (0, 0, 0, 1, 1, 2)
K_TERMS = (0, 1, 2, 0, 1, 0)


def decoder(nc, a, out):
    ctx = ExitStack()
    with ctx:
        def sb(name, shape, dt=F32):
            return ctx.enter_context(nc.sbuf_tensor(name, shape, dt))

        def sem(name):
            return ctx.enter_context(nc.semaphore(name))

        def sem2(name):
            return [sem(f"{name}{p}") for p in range(2)]

        parts_dram = [[nc.dram_tensor(f"parts_{w}{p}", [3, D, CT], BF16) for w in "qk"] for p in range(2)]
        bias_dram = nc.dram_tensor("bias_rows", [2, 3, 2 * P, H], BF16)
        slots_x = nc.dram_tensor("slots_x", [NB * P, D], F32).ap()
        slots_y = nc.dram_tensor("slots_y", [NB * P, D], F32).ap()

        big = sb("big", [P, 16384])
        stack = big[:, :].bitcast(BF16).rearrange("p (c w h t) -> p c w h t", c=2, w=2, h=H)
        w1_sb = big[:, 0:8192]
        w2_sb = big[:, 8192:16384]
        scratch_b = sb("scratch_b", [P, 6144])
        scratch_e = sb("scratch_e", [P, 4096])
        bias_sb = scratch_b[:, :].bitcast(BF16).rearrange("p (w n k h) -> p w n h k", w=2, n=3, k=P)
        mask_int = scratch_b[:, 0:2048].bitcast(I32)
        mask_neg = scratch_b[:, 2048:3072].bitcast(BF16).rearrange("p (b k) -> p b k", b=NSEQ)
        tok_x = scratch_b[:, 0:2048].rearrange("p (b d) -> p b d", b=NSEQ)
        tok_y = scratch_b[:, 4096:6144].rearrange("p (b d) -> p b d", b=NSEQ)
        probs = [scratch_e[:, 2048 * e:2048 * e + 2048] for e in range(2)]
        f1nat = scratch_e[:, 0:FF]
        f2nat = scratch_e[:, FF:2 * FF]
        mx = sb("mx", [P, 1024])
        mexp = mx[:, :].bitcast(BF16).rearrange("p (h q) -> p h q", h=H)
        vpad = sb("vpad", [P, 2, CB, H, 32])
        chunks = sb("chunks", [P, 8, CT])
        x_all = sb("x_all", [P, NSEQ, D])
        xc = [x_all[:, CB * c:CB * c + CB, :] for c in range(NCH)]
        xt = [chunks[:, p, :] for p in range(2)]
        ct = [chunks[:, 2 + p, :] for p in range(2)]
        qkp_all = sb("qkp", [P, 2 * 2 * 3 * CT], BF16)
        qkp = qkp_all[:, :].rearrange("p (c w n t) -> p c w n t", c=2, w=2, n=3)
        qkp32 = qkp_all[:, :].bitcast(F32)
        rest = [[sb(f"rest{p}{w}", [P, CT]) for w in range(2)] for p in range(2)]
        osb = [sb(f"osb{e}", [P, CT]) for e in range(2)]
        rden = sb("rden", [P, H])
        onorm = sb("onorm", [P, D])
        oh = sb("oh", [P, D])
        p_t = sb("p_t", [P, CT])
        m_rows = sb("m_rows", [P, H, P], BF16)
        wt = sb("wt", [P, 13, D])
        w0 = sb("w0", [P, 4, D])
        row_bias = sb("row_bias", [P, 3, D])
        f1t = sb("f1t", [P, FF], BF16)
        f2t = sb("f2t", [P, FC, D], BF16)
        ident = sb("ident", [P, P])
        ident_b = sb("ident_b", [P, P], BF16)
        anti_b = sb("anti_b", [P, P], BF16)
        ones = sb("ones", [P, P])
        ones_b = sb("ones_b", [P, P], BF16)
        tri_b = sb("tri_b", [P, P], BF16)
        causal_b = sb("causal_b", [P, P], BF16)
        abias = sb("abias", [P, 6])
        xbias = sb("xbias", [P, 4])
        score_scale = sb("score_scale", [P, 3])
        router_sb = sb("router_sb", [P, NL * E])
        conv_w = sb("conv_w", [P, FC, 3])
        conv_b = sb("conv_b", [P, FC])
        wsc = sb("wsc", [P, 8])
        zero_t = sb("zero_t", [P, D])
        nmax = sb("nmax", [P, H])
        nparts = sb("nparts", [P, P], BF16)
        mt_sb = sb("mt_sb", [P, P], BF16)
        stats = sb("stats", [P, NSEQ, 6])
        lnv = sb("lnv", [P, 4, NSEQ])
        tab = sb("tab", [P, 2, H])
        small = sb("small", [P, 16, NSEQ])
        WT_X, WT_A1, WT_O1, WT_A2, WT_O2 = 0, 5, 8, 9, 12

        bank = [ctx.enter_context(nc.psum_tensor(f"bank{n}", [P, 1024], F32)) for n in range(4)]

        def pb(n):
            return bank[n // 2][:, 512 * (n % 2):512 * (n % 2) + 512]

        table_loaded = sem("table_loaded")
        front_loaded = sem("front_loaded")
        late_loaded = sem("late_loaded")
        const_made = sem("const_made")
        table_ready = sem("table_ready")
        rows_made = sem("rows_made")
        rows_stored = sem("rows_stored")
        bias_loaded = sem("bias_loaded")
        abs_made = sem("abs_made")
        abs_total = sem("abs_total")
        slots_zero = sem("slots_zero")
        zeroed_0 = sem("zeroed_0")
        zeroed_1 = sem("zeroed_1")
        pool_step = sem("pool_step")
        chain = sem("dve_chain")
        prep_done = sem("prep_done")
        x_loaded = sem("x_loaded")
        x_normed = sem("x_normed")
        t_loaded = sem2("t_loaded")
        build_ready = sem("build_ready")
        build_free = sem("build_free")
        part1_made = sem("part1_made")
        part2_made = sem("part2_made")
        parts_made = sem2("parts_made")
        parts_stored = [sem2(f"parts_stored{p}_") for p in range(2)]
        stacked = sem2("stacked")
        bias_added = sem("bias_added")
        s_ready = sem("scores_ready")
        s_free = sem("scores_free")
        nm_ready = sem("nmax_ready")
        mt_ready = sem("mt_ready")
        mt_free = sem("mt_free")
        mexp_ready = sem("mexp_ready")
        st_ready = sem("scores_t_ready")
        exp_done = sem("exp_done")
        av_done = sem("av_done")
        o_copied = sem("o_copied")
        ot_ready = sem("o_turned")
        on_ready = sem("onorm_ready")
        oh_ready = sem("oh_ready")
        oh_made = sem("oh_made")
        proj_ready = sem("proj_ready")
        z_made = sem("z_made")
        mask_loaded = sem("mask_loaded")
        mask_made = sem("mask_made")
        b_ready = [sem(f"bank{b}_filled") for b in range(8)]
        b_free = [sem(f"bank{b}_read") for b in range(8)]
        g_c_loaded = sem2("g_c_loaded")
        out_stored = sem("out_stored")
        nbias_ready = sem("nbias_ready")
        p_made = sem("p_made")
        xscale_made = sem("xscale_made")
        xq_scaled = sem("xq_scaled")
        diag_made = sem("diag_made")
        xq_made = sem("xq_made")
        tap_made = sem("tap_made")
        conv_made = sem("conv_made")
        silu_made = sem("silu_made")
        qscale_made = sem("qscale_made")
        hq_made = sem("hq_made")
        w1_loaded = sem("w1_loaded")
        w2_loaded = sem("w2_loaded")
        xturn_ready = sem("xturn_ready")
        xturn_a = sem("xturn_a")
        xturn_d = sem("xturn_d")
        logits_ready = sem("logits_ready")
        shifted = sem("shifted")
        expd = sem("expd")
        onehot_ready = sem("onehot_ready")
        counts_ready = sem("counts_ready")
        pos_ready = sem("pos_ready")
        block_ready = sem("block_ready")
        scattered = sem("scattered")
        xs_loaded = sem("xs_loaded")
        xsT_ready = sem("xsT_ready")
        xsT_made = sem("xsT_made")
        h_ready = sem("h_ready")
        h_made = sem("h_made")
        w1_copied = sem("w1_copied")
        y_ready = sem("y_ready")
        y_made = sem("y_made")
        y_stored = sem("y_stored")
        gathered = [sem(f"gathered{g}") for g in range(4)]
        tok_made = sem("tok_made")

        block = ctx.enter_context(nc.Block())

        class Chain:

            def __init__(self, eng):
                self.eng, self.base, self.n = eng, 0, 0

            def __call__(self, ins):
                self.n += 1
                ins.then_inc(chain, 1)
                self.eng.wait_ge(chain, self.base + self.n)

        def looped(eng, link, body, count, steps):
            start = link.base + link.n
            with eng.Fori(0, count, 1) as i:
                link.base, link.n = start + i * steps, 0
                body(i)
                assert link.n == steps, (body, link.n, steps)
            link.base, link.n = start + count * steps, 0

        UB = [[1, 1, 2, 1, 1, 1, 1, 1], [1, 1, 2, 2, 2, 2, 4, 4]]

        def ub(b, n, k=0):
            return n * UB[0][b] + k

        def heads(ap):
            return ap.rearrange("p (h q) -> p h q", q=P)

        def four(ap):
            return ap.rearrange("p (b d) -> p b d", b=4)

        def over(ap, n):
            return ap.unsqueeze(1).broadcast_to([P, n, ap.shape[1]])

        def along(ap, n):
            return ap.unsqueeze(2).broadcast_to([P, ap.shape[1], n])

        def weights_of(s):
            base = (0, WT_A1, WT_A2)[s]
            src = w0 if s == 0 else wt
            return [src[:, base + n, :] for n in range(4)]

        BUILD = (("q", "k", "v"), ("x", "q", "k", "v"), ("x", "q", "k", "v"))
        WHEN = {"x": (0, 1), "q": (1, 0), "k": (1, 1), "v": (2, 0)}
        NORMED = (0, 2 * NCH, 3 * NCH)

        def nbuild(n, what):
            s = n // NCH
            return sum(NCH * len(BUILD[k]) for k in range(s)) + len(BUILD[s]) * (n % NCH) + BUILD[s].index(what)

        def build_at(last, g, half, build):
            n, m = g // CB + 1, g % CB
            if n < last:
                for what in BUILD[n // NCH]:
                    if WHEN[what] == (m, half):
                        build(n, what)

        def build_first(n, build):
            for what in BUILD[n // NCH]:
                build(n, what)

        def attn_sp(sp, first, last):
            def load(n):
                s, c, p = n // NCH, n % NCH, n % 2
                if n < last and s != 1:
                    if c >= 2:
                        sp.wait_ge(build_ready, nbuild(n - 2, "v") + 1)
                    sp.dma_start((xt if s == 0 else ct)[p],
                                 a["x_T" if s == 0 else "ctx_T"][:, CT * c:CT * c + CT]).then_inc(t_loaded[p], 16)

            def restack(n):
                p = n % 2
                if n >= 2:
                    sp.wait_ge(stacked[p], 192 * (n // 2))
                for w in range(2):
                    sp.wait_ge(parts_made[p], 2 * (n // 2) + w + 1)
                    sp.dma_start(parts_dram[p][w].ap().rearrange("n d t -> d n t"), qkp[:, p, w, :, :]).then_inc(
                        parts_stored[p][w], 16)
                if n in (0, 1, NCH, NCH + 1):
                    sp.wait_ge((zeroed_0, zeroed_1)[p], n // NCH + 1)
                if n >= 2:
                    sp.wait_ge(st_ready, 2 * CB * (n - 1))
                for w, terms in ((0, Q_TERMS), (1, K_TERMS)):
                    sp.wait_ge(parts_stored[p][w], 16 * (n // 2) + 16)
                    for r, part in enumerate(terms):
                        sp.dma_start(stack[HD * r:HD * r + HD, p, w, :, :],
                                     parts_dram[p][w].ap()[part].rearrange("(h d) t -> d h t", h=H)).then_inc(
                                         stacked[p], 16)

            if first:
                load(first)
                load(first + 1)
            restack(first)
            if not first:
                sp.dma_start(xt[1], a["x_T"][:, CT:2 * CT]).then_inc(t_loaded[1], 16)
                sp.dma_start(x_all[:, :, :], a["x"].rearrange("b t d -> t b d")).then_inc(x_loaded, 16)
            for n in range(first + 1, last):
                restack(n)
                load(n + 1)

        def build_pe(pe, n, what):
            s, c, p = n // NCH, n % NCH, n % 2
            wq, wk, wv, _ = weights_of(s)
            if nbuild(n, what):
                pe.wait_ge(build_free, nbuild(n, what))
            if what == "x":
                pe.wait_ge(x_normed, NORMED[s] + c + 1)
                for j in range(CB):
                    mm = pe.transpose(pb(6)[:, P * j:P * j + P], xc[c][:, j, :], ident[:, :])
            elif what == "q":
                if s == 0:
                    pe.wait_ge(t_loaded[p], 16 * (c // 2) + 16)
                mm = pe.matmul(pb(6), wq, xt[p], start=True, stop=True)
            elif what == "k":
                if s == 2:
                    pe.wait_ge(t_loaded[p], 16 * (NIT + c // 2) + 16)
                mm = pe.matmul(pb(6), wk, ct[p] if s == 2 else xt[p], start=True, stop=True)
            else:
                for j in range(CB):
                    mm = pe.matmul(pb(6)[:, P * j:P * j + P], (ct[p] if s == 2 else xt[p])[:, P * j:P * j + P], wv,
                                   start=True, stop=True, skip_group_check=True)
            mm.then_inc(build_ready, 1)

        def build_act(act, n, what):
            s, p = n // NCH, n % 2
            if what == "x":
                act.wait_ge(build_ready, nbuild(n, what) + 1)
                act.copy(xt[p], pb(6)).then_inc(build_free, 1)
            elif what != "v":
                w = "qk".index(what)
                if n >= 2:
                    act.wait_ge(parts_stored[p][w], 16 * (n // 2))
                act.wait_ge(build_ready, nbuild(n, what) + 1)
                act.activation(qkp[:, p, w, 0, :], pb(6), ACT.Identity, bias=abias[:, 2 * s + w:2 * s + w + 1]).then_inc(
                    part1_made, 1)

        def build_dve(dve, n, what):
            s, p = n // NCH, n % 2
            if what == "v":
                dve.wait_ge(build_ready, nbuild(n, what) + 1)
                v = pb(6).rearrange("p (b h d) -> p b h d", b=CB, h=H)
                if n >= 2:
                    dve.wait_ge(av_done, CB * (n - 1))
                if s == 0:
                    for j in range(CB):
                        ins = dve.tensor_tensor(vpad[:, p, j, :, 0:HD], v[:, j],
                                                row_bias[:, 1, :].rearrange("p (h d) -> p h d", h=H), ALU.add)
                else:
                    ins = dve.tensor_copy(vpad[:, p, :, :, 0:HD], v)
                ins.then_inc(build_free, 1)
            elif what != "x":
                w = "qk".index(what)
                dve.wait_ge(part1_made, 2 * n + w + 1)
                if n >= 2:
                    dve.wait_ge(parts_made[p], 2 * (n // 2))
                dve.scalar_tensor_tensor(rest[p][w][:, :], pb(6), abias[:, 2 * s + w:2 * s + w + 1],
                                         qkp[:, p, w, 0, :], ALU.add, ALU.subtract).then_inc(build_free, 1)

        def attn_pool(pool, first, last):
            for n in range(first, last):
                s, c, p = n // NCH, n % NCH, n % 2
                for w in range(2):
                    pool.wait_ge(build_free, nbuild(n, "qk"[w]) + 1)
                    if n >= 2:
                        pool.wait_ge(parts_stored[p][w], 16 * (n // 2))
                    pool.tensor_copy(qkp[:, p, w, 1, :], rest[p][w][:, :]).then_inc(part2_made, 1)
                    pool.wait_ge(part2_made, 2 * n + w + 1)
                    pool.tensor_tensor(qkp[:, p, w, 2, :], rest[p][w][:, :], qkp[:, p, w, 1, :],
                                       ALU.subtract).then_inc(parts_made[p], 1)
                if s != 1:
                    if n == 0:
                        pool.wait_ge(x_loaded, 16)
                    pool.tensor_tensor(xc[c], xc[c], over(row_bias[:, s, :], CB), ALU.add).then_inc(bias_added, 1)

        def attn_pe(pe, first, last):
            g0, g1 = CB * first, CB * last

            def scores(g, half):
                s, p, j = g // NSEQ, g // CB % 2, g % CB
                if g + half:
                    pe.wait_ge(s_free, 2 * g + half)
                for b in range(2):
                    dst = bank[0][:, 512 * b:512 * b + 512]
                    if s == 0:
                        for n in range(2):
                            m0 = 8 * half + 4 * b
                            pe.matmul(heads(dst), anti_b[:, :], bias_sb[:, 0, n, m0:m0 + 4, :], start=(n == 0),
                                      stop=False, skip_group_check=True)
                    else:
                        row = causal_b[:, :] if s == 1 else mask_neg[:, g % NSEQ, :]
                        pe.matmul(heads(dst), ident_b[:, :], over(row, 4), start=True, stop=False,
                                  skip_group_check=True)
                    for k in range(4):
                        h = 8 * half + 4 * b + k
                        mm = pe.matmul(dst[:, P * k:P * k + P], stack[:, p, 0, h, P * j:P * j + P],
                                       stack[:, p, 1, h, P * j:P * j + P], start=False, stop=(k == 3),
                                       skip_group_check=True)
                mm.then_inc(s_ready, 1)

            def scores_t(g, half):
                s, p, j = g // NSEQ, g // CB % 2, g % CB
                if g + half:
                    pe.wait_ge(exp_done, 2 * g + half)
                for b in range(2):
                    dst = bank[1][:, 512 * b:512 * b + 512]
                    m0 = 8 * half + 4 * b
                    pe.matmul(heads(dst), ones_b[:, :], mexp[:, m0:m0 + 4, :], start=True, stop=False,
                              skip_group_check=True)
                    for k in range(4):
                        h = m0 + k
                        pe.matmul(dst[:, P * k:P * k + P], stack[:, p, 1, h, P * j:P * j + P],
                                  stack[:, p, 0, h, P * j:P * j + P], start=False, stop=False,
                                  skip_group_check=True)
                    if s == 0:
                        for n in range(3):
                            mm = pe.matmul(heads(dst), anti_b[:, :], bias_sb[:, 1, n, m0:m0 + 4, :], start=False,
                                           stop=(n == 2), skip_group_check=True)
                    else:
                        row = causal_b[:, :] if s == 1 else mask_neg[:, g % NSEQ, :]
                        mm = pe.matmul(heads(dst), row, over(ident_b[:, :], 4), start=False, stop=True,
                                       skip_group_check=True)
                mm.then_inc(st_ready, 1)

            for t in range(g0, g1 + 4):
                if t < g1:
                    if t % CB == 0:
                        n = t // CB
                        pe.wait_ge(stacked[n % 2], 192 * (n // 2) + 192)
                        if n == 2 * NCH:
                            pe.wait_ge(mask_made, 1)
                    scores(t, 0)
                if g0 <= t - 1 < g1:
                    pe.wait_ge(mexp_ready, t)
                    scores_t(t - 1, 0)
                build_at(last, t, 0, lambda *b: build_pe(pe, *b))
                if g0 <= t - 4 < g1:
                    g = t - 4
                    pe.wait_ge(on_ready, g + 1)
                    pe.wait_ge(mt_free, min(t, g1))
                    if g:
                        pe.wait_ge(z_made, g)
                    pe.transpose(pb(7)[:, 0:P], onorm[:, :], ident[:, :]).then_inc(oh_ready, 1)
                if t < g1:
                    scores(t, 1)
                if g0 <= t - 1 < g1:
                    scores_t(t - 1, 1)
                if g0 <= t - 4 < g1:
                    g = t - 4
                    pe.wait_ge(oh_made, g + 1)
                    pe.matmul(pb(7)[:, 0:D], oh[:, :], weights_of(g // NSEQ)[3], start=True, stop=True).then_inc(
                        proj_ready, 1)
                if g0 <= t - 3 < g1:
                    g = t - 3
                    pe.wait_ge(o_copied, g + 1)
                    if g:
                        pe.wait_ge(on_ready, g)
                    for q in range(QUADS):
                        mm = pe.transpose(pb(5)[:, P * q:P * q + P], osb[g % 2][:, P * q:P * q + P], ident[:, :])
                    mm.then_inc(ot_ready, 1)
                build_at(last, t, 1, lambda *b: build_pe(pe, *b))
                if t < g1:
                    pe.wait_ge(nm_ready, t + 1)
                    if t >= g0 + 4:
                        pe.wait_ge(z_made, t - 3)
                    elif t:
                        pe.wait_ge(mt_free, t)
                    pe.transpose(pb(7).bitcast(BF16)[:, 0:P], nparts[:, :], ident_b[:, :]).then_inc(mt_ready, 1)
                if g0 <= t - 2 < g1:
                    g = t - 2
                    p, j = g // CB % 2, g % CB
                    pe.wait_ge(exp_done, 2 * g + 2)
                    if g:
                        pe.wait_ge(o_copied, g)
                    pe.wait_ge(build_free, nbuild(g // CB, "v") + 1)
                    for h in range(H):
                        r, q = 32 * (h % 4), h // 4
                        mm = pe.matmul(pb(4)[r:r + 32, P * q:P * q + P], vpad[:, p, j, h, :],
                                       probs[g % 2][:, P * h:P * h + P], start=True, stop=True,
                                       skip_group_check=True)
                    mm.then_inc(av_done, 1)

        def attn_act(act, first, last):
            g0, g1 = CB * first, CB * last

            def exp_of(g, half):
                s = g // NSEQ
                act.wait_ge(st_ready, 2 * g + half + 1)
                if g >= 2:
                    act.wait_ge(av_done, g - 1)
                act.activation(probs[g % 2][:, 1024 * half:1024 * half + 1024], bank[1][:, :], ACT.Exp,
                               scale=score_scale[:, s:s + 1]).then_inc(exp_done, 1)

            for t in range(g0, g1 + 4):
                if g0 <= t - 1 < g1:
                    exp_of(t - 1, 0)
                build_at(last, t, 0, lambda *b: build_act(act, *b))
                if g0 <= t - 4 < g1:
                    g = t - 4
                    act.wait_ge(oh_ready, g + 1)
                    if g:
                        act.wait_ge(proj_ready, g)
                    act.copy(oh[:, :], pb(7)[:, 0:P]).then_inc(oh_made, 1)
                if g0 <= t - 1 < g1:
                    exp_of(t - 1, 1)
                build_at(last, t, 1, lambda *b: build_act(act, *b))
                if g0 <= t - 2 < g1:
                    g = t - 2
                    act.wait_ge(av_done, g + 1)
                    if g >= 2:
                        act.wait_ge(ot_ready, g - 1)
                    act.copy(osb[g % 2][:, :], pb(4)).then_inc(o_copied, 1)

        def ln_begin(dve, link, n):
            v, y, t, m = (lnv[:, k, 0:n] for k in range(4))
            mean_e, mean_o = stats[:, 0:n, 1], stats[:, 0:n, 4]
            link(dve.tensor_tensor(m, mean_e, mean_o, ALU.add))
            link(dve.tensor_scalar(m, m, 0.5, None, ALU.mult))
            link(dve.tensor_tensor(t, mean_e, mean_o, ALU.subtract))
            link(dve.scalar_tensor_tensor(t, t, 0.25, t, ALU.mult, ALU.mult))
            link(dve.tensor_tensor(v, stats[:, 0:n, 2], stats[:, 0:n, 5], ALU.add))
            link(dve.scalar_tensor_tensor(v, v, 1.0 / D, t, ALU.mult, ALU.add))
            link(dve.tensor_scalar(v, v, EPS, None, ALU.add))
            link(dve.tensor_scalar(y.bitcast(I32), v.bitcast(I32), 1, None, ALU.logical_shift_right))
            link(dve.tensor_scalar(y.bitcast(I32), y.bitcast(I32), -1.0, float(RSQRT_SEED), ALU.mult, ALU.add))
            link(dve.tensor_scalar(v, v, -0.5, None, ALU.mult))

        def ln_newton(dve, link, n):
            v, y, t = (lnv[:, k, 0:n] for k in range(3))
            for _ in range(3):
                link(dve.tensor_tensor(t, y, y, ALU.mult))
                link(dve.tensor_tensor(t, t, v, ALU.mult))
                link(dve.scalar_tensor_tensor(y, t, 1.5, y, ALU.add, ALU.mult))

        def ln_scale(dve, link, z, n, dst, m=0):
            for k in range(n):
                ins = dve.tensor_scalar(dst[:, k, :], z[:, k, :], lnv[:, 3, m + k:m + k + 1],
                                        lnv[:, 1, m + k:m + k + 1], ALU.subtract, ALU.mult)
                if k < n - 1:
                    link(ins)
            return ins

        def layernorm(dve, link, z, n, dst):
            ln_begin(dve, link, n)
            ln_newton(dve, link, n)
            return ln_scale(dve, link, z, n, dst)

        LN_STEPS = 10 + 9

        def attn_dve(dve, link, first, last):
            g0, g1 = CB * first, CB * last

            def maximum(g, half):
                dve.wait_ge(s_ready, 2 * g + half + 1)
                dve.tensor_reduce(nmax[:, 8 * half:8 * half + 8], heads(bank[0][:, :]), AX.X, ALU.max,
                                  negate=True).then_inc(s_free, 1)

            def scale_chunk(c):
                ln_scale(dve, link, xc[c], CB, xc[c]).then_inc(x_normed, 1)

            for t in range(g0, g1 + 4):
                if t < g1:
                    maximum(t, 0)
                build_at(last, t, 0, lambda *b: build_dve(dve, *b))
                if t >= g0 + 2 * CB and t % CB == 0:
                    ln_newton(dve, link, CB)
                if t < g1:
                    maximum(t, 1)
                    dve.wait_ge(s_free, 2 * t + 2)
                    link(dve.tensor_copy(nparts[:, 0:H], nmax[:, :]))
                    dve.tensor_tensor(nparts[:, H:2 * H], nmax[:, :], nparts[:, 0:H], ALU.subtract).then_inc(
                        nm_ready, 1)
                if g0 <= t - 4 < g1:
                    g, s, c, j = t - 4, (t - 4) // NSEQ, (t - 4) // CB % NCH, (t - 4) % CB
                    dve.wait_ge(proj_ready, g + 1)
                    if s != 1 and j == 0:
                        dve.wait_ge(bias_added, NCH * (1 if s == 2 else 0) + c + 1)
                    dve.tensor_tensor(xc[c][:, j, :], pb(7)[:, 0:D], xc[c][:, j, :], ALU.add).then_inc(z_made, 1)
                    dve.wait_ge(z_made, g + 1)
                    link(dve.bn_stats(stats[:, j, :], xc[c][:, j, :]))
                if g0 <= t - 3 < g1:
                    g = t - 3
                    ot = pb(5).rearrange("p (h d) -> p h d", d=32)
                    dve.wait_ge(ot_ready, g + 1)
                    link(dve.reciprocal(rden[:, :], ot[:, :, HD]))
                    if g:
                        dve.wait_ge(oh_ready, g)
                    dve.tensor_tensor(onorm[:, :].rearrange("p (h d) -> p h d", h=H), ot[:, :, 0:HD],
                                      along(rden[:, :], HD), ALU.mult).then_inc(on_ready, 1)
                build_at(last, t, 1, lambda *b: build_dve(dve, *b))
                if t < g1:
                    dve.wait_ge(mt_ready, t + 1)
                    dve.tensor_copy(mt_sb[:, :], pb(7).bitcast(BF16)[:, 0:P]).then_inc(mt_free, 1)
                    dve.wait_ge(mt_free, t + 1)
                    if t:
                        dve.wait_ge(st_ready, 2 * t)
                    dve.tensor_tensor(mexp, over(mt_sb[:, :], H), m_rows[:, :, :], ALU.mult).then_inc(mexp_ready, 1)
                if t >= g0 + CB + 3 and (t - 4) % CB == CB - 1:
                    ln_begin(dve, link, CB)
                if t >= g0 + 2 * CB and t % CB == 0:
                    scale_chunk((t // CB - 2) % NCH)
            ln_newton(dve, link, CB)
            scale_chunk(NCH - 1)

        sel = mx[:, :].rearrange("p (w n j) -> p w n j", w=2, n=2)
        rows32 = p_t[:, 0:4 * H].rearrange("p (w n h) -> p w n h", w=2, n=2)
        rowsr = osb[0][:, 0:4 * H].rearrange("p (w n h) -> p w n h", w=2, n=2)
        rows_b = [p_t[:, 64 + 32 * k:96 + 32 * k].bitcast(BF16).rearrange("p (w n h) -> p w n h", w=2, n=2)
                  for k in range(3)]
        TABLE = 2 * P - 1
        TR = 249

        def prep_sp(sp):
            def load(dst, src, arrived=front_loaded):
                sp.dma_start(dst, src).then_inc(arrived, 16)

            sp.wait_ge(const_made, 2)
            table = a["L0_attn_bias_table"]
            load(tab[:, 0, :], table[0:P, :], table_loaded)
            load(tab[0:TR - P, 1, :], table[P:TR, :], table_loaded)
            load(tab[TR - P:TABLE - P, 1, :], bass.AP(table.tensor, (TR - 1) * H, [[0, TABLE - TR], [1, H]]),
                 table_loaded)
            sp.dma_start(xt[0], a["x_T"][:, 0:CT]).then_inc(t_loaded[0], 16)
            for n, name in enumerate(("Wq", "Wk", "Wv", "Wp")):
                load(w0[:, n, :], a["L0_attn_" + name])
            for n, name in enumerate(("bq", "bk")):
                load(abias[:, n:n + 1], a["L0_attn_" + name].rearrange("(d o) -> d o", o=1))
            for n, name in enumerate(("L0_attn_bp", "L0_attn_bv", "L1_xattn_bo")):
                load(row_bias[:, n, :], bass.AP(a[name].tensor, 0, [[0, P], [1, D]]))
            load(score_scale[:, 0:1], bass.AP(a["L0_attn_temperature"].tensor, 0, [[0, P], [1, 1]]))
            for k in range(3):
                sp.wait_ge(rows_made, k + 1)
                for w in range(2):
                    sp.dma_start(bias_dram.ap()[w, k].rearrange("(n p) h -> p n h", p=P), rows_b[k][:, w]).then_inc(
                        rows_stored, 16)
            sp.wait_ge(rows_stored, 16 * 6)
            for k in range(3):
                for w in range(2):
                    sp.dma_start(scratch_b[:, :].bitcast(BF16)[:, P * H * (3 * w + k):P * H * (3 * w + k + 1)],
                                 bass.AP(bias_dram, (w * 3 + k) * 2 * P * H, [[H, P], [1, P * H]])).then_inc(
                                     bias_loaded, 16)

        def prep_act(act):
            act.wait_ge(front_loaded, 16 * FRONT)
            late_n = [0]

            def late(dst, src):
                late_n[0] += 1
                act.dma_start(dst, src).then_inc(late_loaded, 16)

            late(f1nat, a["L1_ffn_w1_T"])
            late(f2nat.rearrange("p (c d) -> p c d", c=FC), a["L1_ffn_w2_T"].rearrange("(c p) d -> p c d", p=P))
            for n, name in enumerate(("L0_xattn_Wq", "L0_xattn_Wk", "L0_xattn_Wv")):
                late(wt[:, WT_X + n, :], a[name + "_T"])
            late(wt[:, WT_X + 3:WT_X + 5, :], a["L0_xattn_We_T"].rearrange("(n e) d -> e n d", n=2))
            for n, name in enumerate(("L1_attn_Wq", "L1_attn_Wk", "L1_attn_Wv", "L1_attn_Wo")):
                late(wt[:, WT_A1 + n, :], a[name + "_T"])
            for n, name in enumerate(("L1_xattn_Wq", "L1_xattn_Wk", "L1_xattn_Wv", "L1_xattn_Wo")):
                late(wt[:, WT_A2 + n, :], a[name + "_T"])
            for n, name in enumerate(("bq", "bk", "bv", "be")):
                late(xbias[:, n:n + 1], a["L0_xattn_" + name].rearrange("(d o) -> d o", o=1))
            late(router_sb[:, :].rearrange("d (l e) -> d l e", l=NL), a["L0_ffn_routers"].rearrange("l d e -> d l e"))
            late(conv_w[:, :, :], a["L1_ffn_conv_w"].rearrange("(c p) o k -> p c (o k)", p=P))
            for c in range(FC):
                late(conv_b[:, c:c + 1], a["L1_ffn_conv_b"][P * c:P * c + P].rearrange("(p o) -> p o", o=1))
            assert late_n[0] == LATE
            build_first(0, lambda *b: build_act(act, *b))
            act.wait_ge(const_made, CONSTS)
            act.copy(big[:, 8192:16384].rearrange("p (n d) -> p n d", d=D), over(zero_t[:, :], 64)).then_inc(
                zeroed_1, 1)

        LATE = 2 + 3 + 1 + 4 + 4 + 4 + 1 + 1 + FC
        FRONT = 4 + 2 + 3 + 1
        CONSTS = 2 + 4 + 4 + 1 + 4

        def prep_pool(pool):
            made = [0]

            def step(ins):
                made[0] += 1
                ins.then_inc(pool_step, 1)
                pool.wait_ge(pool_step, made[0])

            pool.memset(abias[:, :], 0.0).then_inc(const_made, 1)
            pool.memset(tab[:, :, :], 0.0).then_inc(const_made, 1)

            def diagonal(t, pattern, base, cm, fill=1.0, cmp=ALU.not_equal, first=0.0):
                step(pool.memset(t, first))
                return pool.affine_select(out=t, in_=t, compare_op=cmp, fill=fill, base=base, pattern=pattern,
                                          channel_multiplier=cm)

            for n in range(2):
                diagonal(sel[:, 0, n, :], [[1, 256]], P * n - (TABLE - 1), 1).then_inc(const_made, 1)
                diagonal(sel[:, 1, n, :], [[-1, 256]], P * n, 1).then_inc(const_made, 1)
            diagonal(ident[:, :], [[-1, P]], 0, 1).then_inc(const_made, 1)
            pool.memset(ones[:, :], 1.0).then_inc(const_made, 1)
            diagonal(ident_b[:, :], [[-1, P]], 0, 1).then_inc(const_made, 1)
            diagonal(anti_b[:, :], [[1, P]], -(P - 1), 1).then_inc(const_made, 1)
            pool.memset(ones_b[:, :], 1.0).then_inc(const_made, 1)
            step(pool.memset(m_rows[:, :, :], 0.0))
            for n in range(2):
                step(pool.affine_select(out=m_rows[:, :, :], in_=m_rows[:, :, :], compare_op=ALU.not_equal, fill=1.0,
                                        base=-H * n, pattern=[[-1, H], [0, P]], channel_multiplier=1))
            pool.memset(big[:, 0:8192], 0.0).then_inc(zeroed_0, 1)
            diagonal(causal_b[:, :], [[-1, P]], 0, 1, NEG, ALU.is_ge).then_inc(const_made, 1)
            diagonal(tri_b[:, :], [[1, P]], 0, -1, 0.0, ALU.is_gt, 1.0).then_inc(const_made, 1)
            pool.memset(score_scale[:, 1:3], HD ** -0.5).then_inc(const_made, 1)
            pool.memset(zero_t[:, :], 0.0).then_inc(const_made, 1)

        def prep_pe(pe):
            pe.wait_ge(const_made, 6)
            pe.wait_ge(table_loaded, 16 * 3)
            for w in range(2):
                for b in range(2):
                    for n in range(2):
                        m0 = H * (2 * w + b)
                        mm = pe.matmul(pb(0)[:, m0:m0 + H], sel[:, w, n, P * b:P * b + P], tab[:, n, :],
                                       start=(n == 0), stop=(n == 1), skip_group_check=True)
            mm.then_inc(table_ready, 1)
            pe.wait_ge(front_loaded, 16 * FRONT)
            build_first(0, lambda *b: build_pe(pe, *b))
            pe.wait_ge(const_made, 8)
            pe.wait_ge(abs_made, 2)
            pe.matmul(pb(6)[:, 0:2], ones[:, :], wsc[:, 0:2], start=True, stop=True).then_inc(abs_total, 1)
        def prep_dve(dve, link):
            link(dve.memset(nparts[:, :], 0.0))
            link(dve.memset(vpad[:, :, :, :, :], 0.0))
            link(dve.memset(vpad[:, :, :, :, HD:HD + 1], 1.0))
            dve.wait_ge(table_ready, 1)
            link(dve.tensor_copy(rows32, pb(0)[:, 0:4 * H].rearrange("p (w n h) -> p w n h", w=2, n=2)))
            dve.tensor_copy(rows_b[0], rows32).then_inc(rows_made, 1)
            dve.wait_ge(rows_made, 1)
            link(dve.tensor_tensor(rowsr, rows32, rows_b[0], ALU.subtract))
            dve.tensor_copy(rows_b[1], rowsr).then_inc(rows_made, 1)
            dve.wait_ge(rows_made, 2)
            dve.tensor_tensor(rows_b[2], rowsr, rows_b[1], ALU.subtract).then_inc(rows_made, 1)
            dve.wait_ge(front_loaded, 16 * FRONT)
            build_first(0, lambda *b: build_dve(dve, *b))
            link(dve.tensor_scalar(score_scale[:, 0:1], score_scale[:, 0:1], 0.1, 10.0, ALU.max, ALU.min))
            link(dve.tensor_scalar(score_scale[:, 0:1], score_scale[:, 0:1], float(D) ** 0.5, None, ALU.mult))
            link(dve.reciprocal(score_scale[:, 0:1], score_scale[:, 0:1]))
            dve.wait_ge(late_loaded, 16 * LATE)
            for n, f in enumerate((f1nat, f2nat)):
                dve.tensor_reduce(wsc[:, n:n + 1], f, AX.X, ALU.add, apply_absolute_value=True).then_inc(abs_made, 1)
            dve.wait_ge(abs_total, 1)
            link(dve.tensor_scalar(wsc[:, 2:4], pb(6)[:, 0:2], 1.0 / (D * FF), 1e-5, ALU.mult, ALU.max))
            link(dve.reciprocal(wsc[:, 4:6], wsc[:, 2:4]))
            for n, (f, t) in enumerate(((f1nat, f1t[:, :]), (f2nat, f2t[:, :, :].rearrange("p c d -> p (c d)")))):
                link(dve.tensor_scalar(f, f, wsc[:, 4 + n:5 + n], MAGIC, ALU.mult, ALU.add))
                link(dve.tensor_scalar(f, f, MAGIC, 1.0, ALU.subtract, ALU.min))
                dve.tensor_scalar(t, f, -1.0, None, ALU.max).then_inc(prep_done, 1)

        q_t, k_t, v_t, ent_t = rest[0][0][:, :], rest[0][1][:, :], rest[1][1][:, :], rest[1][0][:, :]
        v_tok = [osb[p][:, :] for p in range(2)]
        p_tok, p_turned = p_t[:, :], scratch_e[:, 0:512]
        XSCALE = float(D) ** -0.5

        def xattn_sp(sp):
            for n in range(NCH):
                if n >= 2:
                    sp.wait_ge(b_ready[6], ub(6, n - 2) + 1)
                sp.dma_start(ct[n % 2], a["ctx_T"][:, CT * n:CT * n + CT]).then_inc(g_c_loaded[n % 2], 16)
            sp.dma_start(slots_x.rearrange("(b p) d -> p b d", p=P), over(zero_t[:, :], NB)).then_inc(slots_zero, 16)

        def xattn_pe(pe):
            def fill(b, n, k=0):
                if ub(b, n, k):
                    pe.wait_ge(b_free[b], ub(b, n, k))

            def tokens(n):
                p = n % 2
                pe.wait_ge(x_normed, n + 1)
                fill(2, n)
                for j in range(CB):
                    mm = pe.transpose(pb(2)[:, P * j:P * j + P], xc[n][:, j, :], ident[:, :])
                mm.then_inc(b_ready[2], 1)
                pe.wait_ge(g_c_loaded[p], 16 * (n // 2) + 16)
                fill(3, n)
                pe.matmul(pb(3), wt[:, WT_X + 1, :], ct[p], start=True, stop=True).then_inc(b_ready[3], 1)
                pe.wait_ge(b_free[2], ub(2, n) + 1)
                pe.matmul(pb(2), wt[:, WT_X, :], xt[p], start=True, stop=True).then_inc(b_ready[2], 1)

            def values(n):
                p = n % 2
                fill(4, n)
                pe.matmul(pb(4), wt[:, WT_X + 2, :], ct[p], start=True, stop=True).then_inc(b_ready[4], 1)
                fill(6, n)
                pe.wait_ge(b_free[4], ub(4, n) + 1)
                for j in range(CB):
                    mm = pe.transpose(pb(6)[:, P * j:P * j + P], v_t[:, P * j:P * j + P], ident[:, :])
                mm.then_inc(b_ready[6], 1)

            def entangle(n):
                pe.wait_ge(b_free[3], ub(3, n) + 1)
                fill(5, n)
                pe.matmul(pb(5), wt[:, WT_X + 4, :], k_t, start=True, stop=False)
                pe.wait_ge(b_free[2], ub(2, n, 1) + 1)
                pe.matmul(pb(5), wt[:, WT_X + 3, :], q_t, start=False, stop=True).then_inc(b_ready[5], 1)

            def scores(n):
                pe.wait_ge(b_free[5], ub(5, n) + 1)
                fill(7, n)
                for j in range(CB):
                    mm = pe.matmul(pb(7)[:, P * j:P * j + P], ent_t[:, P * j:P * j + P], v_t[:, P * j:P * j + P],
                                   start=True, stop=True, skip_group_check=True)
                mm.then_inc(b_ready[7], 1)

            def turn_probs(n):
                pe.wait_ge(b_free[7], ub(7, n) + 1)
                fill(1, n)
                for j in range(CB):
                    mm = pe.transpose(pb(1)[:, P * j:P * j + P], p_tok[:, P * j:P * j + P], ident[:, :])
                mm.then_inc(b_ready[1], 1)

            def weigh(n):
                pe.wait_ge(b_free[1], ub(1, n) + 1)
                pe.wait_ge(b_free[6], ub(6, n) + 1)
                fill(0, n)
                for j in range(CB):
                    mm = pe.matmul(pb(0)[:, P * j:P * j + P], p_turned[:, P * j:P * j + P],
                                   v_tok[n % 2][:, P * j:P * j + P], start=True, stop=True, skip_group_check=True)
                mm.then_inc(b_ready[0], 1)

            pe.wait_ge(x_normed, NCH)
            for n in range(NCH + 1):
                if n < NCH:
                    tokens(n)
                if n >= 1:
                    turn_probs(n - 1)
                if n < NCH:
                    values(n)
                if n >= 1:
                    weigh(n - 1)
                if n < NCH:
                    entangle(n)
                    scores(n)

        def xattn_act(act):
            for n in range(NCH + 1):
                if n < NCH:
                    act.wait_ge(b_ready[2], ub(2, n) + 1)
                    act.copy(xt[n % 2], pb(2)).then_inc(b_free[2], 1)
                if n >= 1:
                    act.wait_ge(nbias_ready, n)
                    for j in range(CB):
                        ins = act.activation(p_tok[:, P * j:P * j + P], pb(7)[:, P * j:P * j + P], ACT.Exp,
                                             bias=small[:, 0, j:j + 1], scale=XSCALE, accum_out=small[:, 1, j:j + 1])
                    ins.then_inc(b_free[7], 1)
                if n < NCH:
                    act.wait_ge(b_ready[2], ub(2, n, 1) + 1)
                    act.activation(q_t, pb(2), ACT.Identity, bias=xbias[:, 0:1]).then_inc(b_free[2], 1)
                    act.wait_ge(b_ready[4], ub(4, n) + 1)
                    act.activation(v_t, pb(4), ACT.Identity, bias=xbias[:, 2:3]).then_inc(b_free[4], 1)
                    act.wait_ge(b_ready[5], ub(5, n) + 1)
                    act.activation(ent_t, pb(5), ACT.Tanh, bias=xbias[:, 3:4]).then_inc(b_free[5], 1)

        def xattn_dve(dve, link):
            for n in range(NCH + 1):
                if n < NCH:
                    dve.wait_ge(b_ready[3], ub(3, n) + 1)
                    dve.tensor_scalar(k_t, pb(3), xbias[:, 1:2], None, ALU.add).then_inc(b_free[3], 1)
                if n >= 1:
                    dve.wait_ge(b_ready[1], ub(1, n - 1) + 1)
                    dve.tensor_copy(p_turned, pb(1)).then_inc(b_free[1], 1)
                    link(dve.reciprocal(small[:, 2, 0:CB], small[:, 1, 0:CB]))
                if n < NCH:
                    dve.wait_ge(b_ready[6], ub(6, n) + 1)
                    dve.tensor_copy(v_tok[n % 2], pb(6)).then_inc(b_free[6], 1)
                if n >= 1:
                    dve.wait_ge(b_ready[0], ub(0, n - 1) + 1)
                    for j in range(CB):
                        ins = dve.scalar_tensor_tensor(xc[n - 1][:, j, :], pb(0)[:, P * j:P * j + P],
                                                       small[:, 2, j:j + 1], xc[n - 1][:, j, :], ALU.mult, ALU.add)
                        if j < CB - 1:
                            link(ins)
                    ins.then_inc(b_free[0], 1)
                if n < NCH:
                    dve.wait_ge(b_ready[7], ub(7, n) + 1)
                    link(dve.tensor_reduce(small[:, 0, 0:CB], four(pb(7)), AX.X, ALU.max, negate=True))
                    dve.tensor_scalar(small[:, 0, 0:CB], small[:, 0, 0:CB], XSCALE, None, ALU.mult).then_inc(
                        nbias_ready, 1)
                if n >= 1:
                    dve.wait_ge(b_free[0], ub(0, n - 1) + 1)
                    for j in range(CB):
                        link(dve.bn_stats(stats[:, j, :], xc[n - 1][:, j, :]))
                    layernorm(dve, link, xc[n - 1], CB, xc[n - 1]).then_inc(x_normed, 1)

        xt_all = scratch_e[:, 0:2048]
        tmps = scratch_e[:, 2048:4096].rearrange("p (n m) -> p n m", n=8)
        shift_sb, exp_sb, cand_sb, cnt_sb, cum_sb, base_sb, rank_sb = (tmps[:, n, :] for n in range(7))
        onehot_b = tmps[:, 7, 0:P].bitcast(BF16)
        consts = mx[:, :].rearrange("p (n m) -> p n m", n=4)
        iota_e, iota_e64, seg, iota_i = (consts[:, n, :] for n in range(4))
        w1_block = [qkp32[:, FF * u:FF * u + FF] for u in range(2)]
        hT_sb = [qkp32[:, 2 * FF + FF * u:2 * FF + FF * u + FF] for u in range(2)]
        xs_sb = [rest[g][0][:, :] for g in range(2)]
        ys_sb = chunks[:, :, :].rearrange("p a b -> p (a b)")
        xsT_sb = [qkp32[:, 4 * FF + 2 * D + D * u:4 * FF + 2 * D + D * u + D] for u in range(2)]

        def te(ap):
            return ap.rearrange("p (t e) -> p t e", e=E)

        def et(ap):
            return ap.rearrange("p (e t) -> p e t", e=E)

        (LMAX, EMAX, ESUM, EREC, WSEL, IDX, NEXP, BLK, BEND, BSTART, POS, POSI) = range(12)
        SEG1 = 12
        GRP = 4
        GROUPS = [(j, min(j + GRP, NB)) for j in range(0, NB, GRP)]
        TURNS = (NB - GRP) // (2 * GRP)

        def moe_sp(sp):
            sp.wait_ge(st_ready, 2 * NSEQ)
            sp.dma_start(w1_sb.rearrange("p (e f) -> p e f", e=E), a["L0_ffn_W1"].rearrange("e d f -> d e f")).then_inc(w1_loaded, 16)
            sp.dma_start(w2_sb.rearrange("p (e c d) -> p e c d", e=E, c=FC),
                         a["L0_ffn_W2"].rearrange("e (c p) d -> p e c d", p=P)).then_inc(w2_loaded, 16)

            def store(l, j0, j1):
                sp.wait_ge(y_made, NB * l + j1)
                sp.dma_start(slots_y[P * j0:P * j1, :].rearrange("(b p) d -> p b d", p=P),
                             ys_sb[:, D * j0:D * j1].rearrange("p (b d) -> p b d", d=D)).then_inc(y_stored, 16)

            for l in range(NL):
                sp.wait_ge(scattered, 16 * NSEQ * (l + 1))
                for g, (j0, j1) in enumerate(GROUPS):
                    if g >= 2:
                        sp.wait_ge(xsT_ready, NB * l + GRP * (g - 1))
                    sp.dma_start(xs_sb[g % 2][:, 0:D * (j1 - j0)].rearrange("p (b d) -> p b d", d=D),
                                 slots_x[P * j0:P * j1, :].rearrange("(b p) d -> p b d", p=P)).then_inc(xs_loaded, 16)
                    sp.wait_ge(xs_loaded, 16 * (len(GROUPS) * l + g + 1))
                    if g >= 2:
                        store(l, *GROUPS[g - 2])
                for g in (-2, -1):
                    store(l, *GROUPS[g])

        def moe_pool(pool):
            for g in range(4):
                pool.wait_ge(x_normed, NCH + g + 1)
                pool.dma_start(tok_y[:, 4 * g:4 * g + 4, :], xc[g]).then_inc(gathered[g], 16)
            ii = iota_i.bitcast(I32)
            base = pool_steps[0]
            pool.iota(ii, pattern=[[0, NSEQ], [1, E]], base=0, channel_multiplier=0).then_inc(pool_step, 1)
            pool.wait_ge(pool_step, base + 1)
            pool.tensor_copy(iota_e, ii).then_inc(pool_step, 1)
            pool.wait_ge(pool_step, base + 2)
            pool.tensor_scalar(iota_e64, iota_e, 64.0, None, ALU.add).then_inc(pool_step, 1)
            pool.memset(seg, 1.0).then_inc(pool_step, 1)
            pool.wait_ge(pool_step, base + 4)
            pool.memset(et(seg)[:, :, 0:1], 0.0).then_inc(pool_step, 1)
            pool.memset(small[:, SEG1, :], 1.0).then_inc(pool_step, 1)
            pool.wait_ge(pool_step, base + 6)
            pool.iota(blocks_i, pattern=[[1, NB]], base=0, channel_multiplier=0).then_inc(pool_step, 1)
            pool.wait_ge(pool_step, base + 7)
            pool.tensor_copy(blocks_f, blocks_i).then_inc(pool_step, 1)
            for l in range(NL):
                pool.wait_ge(pos_ready, l + 1)
                if l == 0:
                    pool.wait_ge(slots_zero, 16)
                for t in range(NSEQ):
                    pool.indirect_dma_start(out=slots_x, out_offset=bass.IndirectOffsetOnAxis(
                        ap=posi[:, t:t + 1], axis=0), in_=tok_x[:, t, :], in_offset=None).then_inc(scattered, 16)
                pool.wait_ge(y_stored, 16 * len(GROUPS) * (l + 1))
                for t in range(NSEQ):
                    pool.indirect_dma_start(out=tok_y[:, t, :], out_offset=None, in_=slots_y,
                                            in_offset=bass.IndirectOffsetOnAxis(ap=posi[:, t:t + 1], axis=0)).then_inc(
                                                gathered[t // 4], 16)

        posi = small[:, POSI, :].bitcast(I32)
        blk_tab = sb("blk_tab", [P, 4, NB])
        blocks_i = blk_tab[:, 0, :].bitcast(I32)
        blocks_f = blk_tab[:, 1, :]
        bexp = blk_tab[:, 2, :]
        boff = blk_tab[:, 3, :].bitcast(I32)
        cmp_sb = sb("cmp_sb", [P, NB * E])
        pool_steps = [8 + 2 + 2]

        def block_steps(eng, step):
            for j in range(GRP):
                step(j, j, 0 if j == 0 else None)
            with eng.Fori(0, TURNS, 1) as k:
                for m in range(GRP, 3 * GRP):
                    step(2 * GRP * k + m, m % (2 * GRP), 2 * k + m // GRP if m % GRP == 0 else None)
            for j in range(GRP + 2 * GRP * TURNS, NB + 2):
                step(j, j % (2 * GRP), j // GRP if j % GRP == 0 and j < NB else None)

        def moe_pe(pe, l):
            for g in range(4):
                pe.wait_ge(tok_made, 4 * l + g + 1)
                for j in range(4):
                    mm = pe.transpose(pb(g)[:, P * j:P * j + P], tok_x[:, 4 * g + j, :], ident[:, :])
                mm.then_inc(xturn_ready, 1)
            for g in range(4):
                pe.wait_ge(xturn_a if g % 2 == 0 else xturn_d, 2 * l + g // 2 + 1)
                for j in range(4):
                    t = 4 * g + j
                    mm = pe.matmul(pb(4)[:, E * t:E * t + E], xt_all[:, P * t:P * t + P],
                                   router_sb[:, bass.ds(E * l, E)], start=True, stop=True, skip_group_check=True)
            mm.then_inc(logits_ready, 1)
            pe.wait_ge(onehot_ready, l + 1)
            pe.matmul(pb(5)[:, 0:NSEQ * E], tri_b[:, :], onehot_b, start=True, stop=True, skip_group_check=True)
            pe.matmul(pb(5)[:, NSEQ * E:2 * NSEQ * E], ones_b[:, :], onehot_b, start=True, stop=True,
                      skip_group_check=True).then_inc(counts_ready, 1)
            pe.wait_ge(block_ready, l + 1)

            def offset(j):
                return pe.value_load(boff[0:1, bass.ds(j, 1)], min_val=0, max_val=(E - 1) * FF)

            def turn_x(j, m, u, k):
                if k is not None:
                    pe.wait_ge(xs_loaded, 16 * (len(GROUPS) * l + k + 1))
                pe.wait_ge(xsT_made, NB * l + j - 1 if not isinstance(j, int) or j > 0 else NB * l)
                pe.transpose(pb(u)[:, 0:P], xs_sb[m // GRP][:, D * (m % GRP):D * (m % GRP) + D], ident[:, :]).then_inc(xsT_ready, 1)

            def up(j, u):
                pe.wait_ge(w1_copied, NB * l + j + 1)
                pe.wait_ge(xsT_made, NB * l + j + 1)
                pe.wait_ge(h_made, NB * l + j - 1 if not isinstance(j, int) or j > 0 else NB * l)
                for c in range(FC):
                    mm = pe.matmul(pb(2 + u)[:, P * c:P * c + P], w1_block[u][:, P * c:P * c + P], xsT_sb[u],
                                   start=True, stop=True, skip_group_check=True)
                mm.then_inc(h_ready, 1)

            def out_rows(j, u):
                e = offset(j)
                pe.wait_ge(h_made, NB * l + j + 1)
                pe.wait_ge(y_made, NB * l + j - 1 if not isinstance(j, int) or j > 0 else NB * l)
                for c in range(FC):
                    mm = pe.matmul(pb(6 + u)[:, 0:D], hT_sb[u][:, P * c:P * c + P], w2_sb[:, bass.ds(e + P * c, D)],
                                   start=(c == 0), stop=(c == FC - 1))
                mm.then_inc(y_ready, 1)

            def step(j, m, k=None):
                u = m % 2
                known = isinstance(j, int)
                if not known or j < NB:
                    turn_x(j, m, u, k)
                if not known or 0 <= j - 1 < NB:
                    up(j - 1, 1 - u)
                if not known or 0 <= j - 2 < NB:
                    out_rows(j - 2, u)

            pe.wait_ge(w1_loaded, 16)
            pe.wait_ge(w2_loaded, 16)
            block_steps(pe, step)

        def moe_act(act, l):
            for g in (0, 2):
                act.wait_ge(xturn_ready, 4 * l + g + 1)
                act.copy(xt_all[:, 512 * g:512 * g + 512], pb(g)).then_inc(xturn_a, 1)
            act.wait_ge(shifted, l + 1)
            act.activation(exp_sb, shift_sb, ACT.Exp).then_inc(expd, 1)

            def step(j, m, k=None):
                u = m % 2
                known = isinstance(j, int)
                if not known or 0 <= j - 1 < NB:
                    act.wait_ge(h_ready, NB * l + j)
                    act.activation(hT_sb[1 - u], pb(2 + 1 - u), ACT.Silu).then_inc(h_made, 1)
                if not known or 0 <= j - 2 < NB:
                    act.wait_ge(y_ready, NB * l + j - 1)
                    act.copy(ys_sb[:, bass.ds((j - 2) * D, D)], pb(6 + u)[:, 0:D]).then_inc(y_made, 1)

            block_steps(act, step)

        def moe_dve(dve, link, l):
            sm = small
            for g in range(4):
                dve.wait_ge(gathered[g], l * (16 * 4) + 16)
                dve.tensor_tensor(tok_x[:, 4 * g:4 * g + 4, :], tok_y[:, 4 * g:4 * g + 4, :],
                                  along(sm[:, WSEL, 4 * g:4 * g + 4], D), ALU.mult).then_inc(tok_made, 1)
            for g in (1, 3):
                dve.wait_ge(xturn_ready, 4 * l + g + 1)
                dve.tensor_copy(xt_all[:, 512 * g:512 * g + 512], pb(g)).then_inc(xturn_d, 1)
            dve.wait_ge(logits_ready, l + 1)
            logits = te(pb(4)[:, 0:NSEQ * E])
            link(dve.tensor_reduce(sm[:, LMAX, :], logits, AX.X, ALU.max))
            dve.tensor_tensor(te(shift_sb), logits, along(sm[:, LMAX, :], E), ALU.subtract).then_inc(shifted, 1)
            dve.wait_ge(expd, l + 1)
            link(dve.tensor_reduce(sm[:, EMAX, :], te(exp_sb), AX.X, ALU.max))
            link(dve.tensor_tensor(te(cand_sb), te(exp_sb), along(sm[:, EMAX, :], E), ALU.is_equal))
            link(dve.scalar_tensor_tensor(cand_sb, cand_sb, -64.0, iota_e64, ALU.mult, ALU.add))
            link(dve.tensor_reduce(sm[:, IDX, :], te(cand_sb), AX.X, ALU.min))
            dve.tensor_tensor(te(onehot_b), te(iota_e), along(sm[:, IDX, :], E), ALU.is_equal).then_inc(onehot_ready, 1)
            dve.wait_ge(counts_ready, l + 1)
            link(dve.tensor_copy(et(cnt_sb), te(pb(5)[:, NSEQ * E:2 * NSEQ * E]).rearrange("p t e -> p e t")))
            link(dve.tensor_tensor_scan(cum_sb, seg, cnt_sb, 0.0, ALU.mult, ALU.add))
            link(dve.tensor_scalar(sm[:, NEXP, :], et(cum_sb)[:, :, NSEQ - 1], 1.0 / P,
                                   (P - 1) / P - 0.5 + 0.5 / P, ALU.mult, ALU.add))
            link(dve.tensor_scalar(sm[:, NEXP, :], sm[:, NEXP, :], MAGIC, None, ALU.add))
            link(dve.tensor_scalar(sm[:, BLK, :], sm[:, NEXP, :], MAGIC, None, ALU.subtract))
            link(dve.tensor_tensor_scan(sm[:, BEND, :], sm[:, SEG1, :], sm[:, BLK, :], 0.0, ALU.mult, ALU.add))
            link(dve.tensor_tensor(sm[:, BSTART, :], sm[:, BEND, :], sm[:, BLK, :], ALU.subtract))
            link(dve.tensor_tensor(base_sb, cum_sb, cnt_sb, ALU.subtract))
            link(dve.scalar_tensor_tensor(et(base_sb), along(sm[:, BSTART, :], NSEQ), float(P), et(base_sb),
                                          ALU.mult, ALU.add))
            link(dve.tensor_tensor(te(rank_sb), te(pb(5)[:, 0:NSEQ * E]), et(base_sb).rearrange("p e t -> p t e"),
                                   ALU.add))
            link(dve.tensor_tensor(rank_sb, rank_sb, onehot_b, ALU.mult))
            link(dve.tensor_reduce(sm[:, POS, :], te(rank_sb), AX.X, ALU.add))
            dve.tensor_copy(posi, sm[:, POS, :]).then_inc(pos_ready, 1)
            link(dve.tensor_tensor(te(cmp_sb[:, :]), over(sm[:, BEND, :], NB), along(blocks_f, E), ALU.is_le))
            link(dve.tensor_reduce(bexp, te(cmp_sb[:, :]), AX.X, ALU.add))
            link(dve.tensor_scalar(bexp, bexp, float(E - 1), float(FF), ALU.min, ALU.mult))
            dve.tensor_copy(boff, bexp).then_inc(block_ready, 1)
            link(dve.tensor_reduce(sm[:, ESUM, :], te(exp_sb), AX.X, ALU.add))
            link(dve.reciprocal(sm[:, EREC, :], sm[:, ESUM, :]))
            link(dve.tensor_tensor(sm[:, WSEL, :], sm[:, EMAX, :], sm[:, EREC, :], ALU.mult))

            def step(j, m, k=None):
                u = m % 2
                known = isinstance(j, int)
                if not known or j < NB:
                    dve.wait_ge(xsT_ready, NB * l + j + 1)
                    dve.tensor_copy(xsT_sb[u], pb(u)[:, 0:P]).then_inc(xsT_made, 1)
                    e = dve.value_load(boff[0:1, bass.ds(j, 1)], min_val=0, max_val=(E - 1) * FF)
                    dve.wait_ge(h_ready, NB * l + j - 1 if not known or j > 0 else NB * l)
                    dve.tensor_copy(w1_block[u], w1_sb[:, bass.ds(e, FF)]).then_inc(w1_copied, 1)
            dve.wait_ge(block_ready, l + 1)
            dve.wait_ge(w1_loaded, 16)
            block_steps(dve, step)

        MOE_STEPS = 8 + 12 + 3

        def moe_end_dve(dve, link):
            for c in range(NCH):
                dve.wait_ge(gathered[c], 16 * 4 * NL + 16)
                for j in range(CB):
                    link(dve.scalar_tensor_tensor(xc[c][:, j, :], tok_y[:, CB * c + j, :],
                                                  small[:, WSEL, CB * c + j:CB * c + j + 1], xc[c][:, j, :],
                                                  ALU.mult, ALU.add))
                for j in range(CB):
                    link(dve.bn_stats(stats[:, CB * c + j, :], xc[c][:, j, :]))
            ln_begin(dve, link, NSEQ)
            ln_newton(dve, link, NSEQ)
            for c in range(NCH):
                ln_scale(dve, link, xc[c], CB, xc[c], CB * c).then_inc(x_normed, 1)

        hp = [scratch_b[:, 528 * c:528 * c + 520].rearrange("p (b t) -> p b t", b=CB) for c in range(FC)]
        xq_f = scratch_b[:, 2112:2624]
        diag = scratch_b[:, 2624:3136]
        inv_rows = scratch_b[:, 3136:3648]
        hc = [scratch_b[:, 3648 + 512 * n:4160 + 512 * n] for n in range(2)]
        q_f = [scratch_b[:, 4672 + 512 * n:5184 + 512 * n] for n in range(2)]
        magic_t = scratch_b[:, 5700:5701]
        hs = [big[:, 2048 * n:2048 * n + 2048].rearrange("p (c t) -> p c t", c=FC) for n in range(2)]
        xq_b = scratch_e[:, 2048:2304].bitcast(BF16)
        xqT_b = scratch_e[:, 2304:2560].bitcast(BF16)
        hq_b = [scratch_e[:, 2560 + 256 * n:2816 + 256 * n].bitcast(BF16) for n in range(2)]
        hqT_b = [scratch_e[:, 3072 + 256 * n:3328 + 256 * n].bitcast(BF16) for n in range(2)]

        def fb(b, n, k=0):
            return NCH * UB[0][b] + n * UB[1][b] + k

        def ffn_sp(sp):
            for c in range(NCH):
                sp.wait_ge(x_normed, 5 * NCH + c + 1)
                sp.dma_start(out.rearrange("b t d -> t b d")[:, CB * c:CB * c + CB, :], xc[c]).then_inc(out_stored, 16)
            sp.wait_ge(out_stored, 16 * NCH)

        def ffn_pe(pe):
            def turn(k):
                n, j = k // CB, k % CB
                b = 4 + j % 2
                pe.wait_ge(silu_made, FC * n + FC)
                pe.wait_ge(b_free[b], fb(b, n, j // 2))
                for c in range(FC):
                    mm = pe.transpose(pb(b)[:, P * c:P * c + P], hs[n % 2][:, c, P * j:P * j + P], ident[:, :])
                mm.then_inc(b_ready[b], 1)

            def turn_rounded(k):
                n, j = k // CB, k % CB
                pe.wait_ge(hq_made, k + 1)
                pe.wait_ge(b_free[6], fb(6, n, j))
                for c in range(FC):
                    mm = pe.transpose(pb(6).bitcast(BF16)[:, P * c:P * c + P], hq_b[j % 2][:, P * c:P * c + P],
                                      ident_b[:, :])
                mm.then_inc(b_ready[6], 1)

            def bring_down(k):
                n, j = k // CB, k % CB
                pe.wait_ge(b_free[6], fb(6, n, j) + 1)
                pe.wait_ge(b_free[7], fb(7, n, j))
                for c in range(FC):
                    mm = pe.matmul(pb(7)[:, 0:D], hqT_b[j % 2][:, P * c:P * c + P], f2t[:, c, :], start=(c == 0),
                                   stop=(c == FC - 1))
                mm.then_inc(b_ready[7], 1)

            def up_first(n):
                pe.wait_ge(xq_made, n + 1)
                pe.wait_ge(b_free[0], fb(0, n))
                for j in range(CB):
                    mm = pe.transpose(pb(0).bitcast(BF16)[:, P * j:P * j + P], xq_b[:, P * j:P * j + P], ident_b[:, :])
                mm.then_inc(b_ready[0], 1)
                pe.wait_ge(diag_made, n + 1)
                pe.wait_ge(b_free[1], fb(1, n))
                pe.matmul(pb(1), ones[:, :], diag, start=True, stop=True).then_inc(b_ready[1], 1)
                pe.wait_ge(b_free[0], fb(0, n) + 1)

            def up(n, c):
                b = 2 + c % 2
                pe.wait_ge(b_free[b], fb(b, n, c // 2))
                pe.matmul(pb(b), f1t[:, P * c:P * c + P], xqT_b, start=True, stop=True).then_inc(b_ready[b], 1)

            for k in range(-CB - 1, NSEQ + 1):
                n, c = (k + CB + 1) // CB, (k + CB + 1) % CB
                if 0 <= k - 1 < NSEQ:
                    turn_rounded(k - 1)
                if n < NCH and c == 0:
                    up_first(n)
                if n < NCH:
                    up(n, c)
                if 0 <= k + 1 < NSEQ:
                    turn(k + 1)
                if 0 <= k - 1 < NSEQ:
                    bring_down(k - 1)

        def ffn_act(act):
            def scaled(k):
                b = 4 + k % 2
                act.wait_ge(qscale_made, k + 1)
                act.activation(q_f[k % 2], pb(b), ACT.Identity, bias=magic_t, scale=small[:, 4 + k % CB, 0:1]).then_inc(
                    b_free[b], 1)

            def turned(k):
                act.wait_ge(b_ready[6], fb(6, 0, k) + 1)
                act.copy(hqT_b[k % 2], pb(6).bitcast(BF16)[:, 0:512]).then_inc(b_free[6], 1)

            def quantise(n):
                act.wait_ge(xscale_made, n + 1)
                for j in range(CB):
                    ins = act.activation(xq_f[:, P * j:P * j + P], xc[n][:, j, :], ACT.Identity, bias=magic_t,
                                         scale=small[:, 1, j:j + 1])
                ins.then_inc(xq_scaled, 1)
                if n:
                    act.wait_ge(b_ready[1], fb(1, n))
                for j in range(CB):
                    ins = act.activation(diag[:, P * j:P * j + P], ident[:, :], ACT.Copy, scale=small[:, 2, j:j + 1])
                ins.then_inc(diag_made, 1)

            quantise(0)
            for k in range(-CB - 1, NSEQ + 1):
                n, c = (k + CB + 1) // CB, (k + CB + 1) % CB
                if n < NCH and c == 0:
                    act.wait_ge(b_ready[0], fb(0, n) + 1)
                    act.copy(xqT_b, pb(0).bitcast(BF16)[:, 0:512]).then_inc(b_free[0], 1)
                    act.wait_ge(b_ready[1], fb(1, n) + 1)
                    for b in (2, 3):
                        act.wait_ge(b_free[b], fb(b, n))
                    act.copy(inv_rows, pb(1)).then_inc(b_free[1], 1)
                if 0 <= k < NSEQ:
                    scaled(k)
                if 0 <= k - 1 < NSEQ:
                    turned(k - 1)
                if n < NCH:
                    act.wait_ge(b_free[2 + c % 2], fb(2 + c % 2, n, c // 2) + 1)
                    if FC * n + c >= 2:
                        act.wait_ge(silu_made, FC * n + c - 1)
                    act.activation(four(hc[c % 2]), hp[c][:, :, 0:P], ACT.Identity, bias=conv_b[:, c:c + 1],
                                   scale=conv_w[:, c, 0:1]).then_inc(tap_made, 1)
                if 0 <= k + CB < NSEQ:
                    n1, c1 = (k + CB) // CB, (k + CB) % CB
                    act.wait_ge(conv_made, FC * n1 + c1 + 1)
                    act.activation(hs[n1 % 2][:, c1, :], hc[c1 % 2], ACT.Silu).then_inc(silu_made, 1)
                if c == CB - 2 and n + 1 < NCH:
                    quantise(n + 1)

        def ffn_dve(dve, link):
            def quantise(n):
                am, sc, inv = small[:, 0, 0:CB], small[:, 1, 0:CB], small[:, 2, 0:CB]
                x = xc[n]
                if n == 0:
                    dve.wait_ge(x_normed, 5 * NCH)
                link(dve.tensor_reduce(am, x, AX.X, ALU.max, apply_absolute_value=True))
                link(dve.tensor_scalar(am, am, 1e-5, None, ALU.max))
                link(dve.reciprocal(sc, am))
                link(dve.tensor_scalar(sc, sc, 127.0, None, ALU.mult))
                dve.tensor_scalar(inv, am, 1.0 / 127.0, wsc[:, 2:3], ALU.mult, ALU.mult).then_inc(xscale_made, 1)

            def rounded(n):
                dve.wait_ge(xq_scaled, n + 1)
                if n:
                    dve.wait_ge(b_ready[0], fb(0, n))
                dve.tensor_scalar(xq_b, xq_f, MAGIC, 127.0, ALU.subtract, ALU.min).then_inc(xq_made, 1)

            def residual(k):
                n, j = k // CB, k % CB
                dve.wait_ge(b_ready[7], fb(7, n, j) + 1)
                dve.scalar_tensor_tensor(xc[n][:, j, :], pb(7)[:, 0:D], small[:, 4 + j, 1:2], xc[n][:, j, :],
                                         ALU.mult, ALU.add).then_inc(b_free[7], 1)
                dve.wait_ge(b_free[7], fb(7, n, j) + 1)
                link(dve.bn_stats(stats[:, j, :], xc[n][:, j, :]))
                if j == CB - 1:
                    layernorm(dve, link, xc[n], CB, xc[n]).then_inc(x_normed, 1)

            quantise(0)
            rounded(0)
            for k in range(-CB - 1, NSEQ + 2):
                n, c = (k + CB + 1) // CB, (k + CB + 1) % CB
                if 0 <= k - 2 < NSEQ:
                    residual(k - 2)
                if 0 <= k < NSEQ:
                    b = 4 + k % 2
                    q = small[:, 4 + k % CB, :]
                    dve.wait_ge(b_ready[b], fb(b, k // CB, k % CB // 2) + 1)
                    link(dve.tensor_reduce(q[:, 2:3], pb(b), AX.X, ALU.max, apply_absolute_value=True))
                    link(dve.tensor_scalar(q[:, 2:3], q[:, 2:3], 1e-5, None, ALU.max))
                    link(dve.reciprocal(q[:, 3:4], q[:, 2:3]))
                    link(dve.tensor_scalar(q[:, 1:2], q[:, 2:3], 1.0 / 127.0, wsc[:, 3:4], ALU.mult, ALU.mult))
                    dve.tensor_scalar(q[:, 0:1], q[:, 3:4], 127.0, None, ALU.mult).then_inc(qscale_made, 1)
                if n < NCH:
                    b = 2 + c % 2
                    if c == 0:
                        dve.wait_ge(b_free[1], fb(1, n) + 1)
                    dve.wait_ge(b_ready[b], fb(b, n, c // 2) + 1)
                    dve.tensor_tensor(hp[c][:, :, 1:P + 1], four(pb(b)), four(inv_rows), ALU.mult).then_inc(b_free[b], 1)
                if 0 <= k + CB < NSEQ:
                    n1, c1 = (k + CB) // CB, (k + CB) % CB
                    t = four(hc[c1 % 2])
                    dve.wait_ge(tap_made, FC * n1 + c1 + 1)
                    link(dve.scalar_tensor_tensor(t, hp[c1][:, :, 1:P + 1], conv_w[:, c1, 1:2], t, ALU.mult, ALU.add))
                    dve.scalar_tensor_tensor(t, hp[c1][:, :, 2:P + 2], conv_w[:, c1, 2:3], t, ALU.mult,
                                             ALU.add).then_inc(conv_made, 1)
                if 0 <= k < NSEQ:
                    dve.wait_ge(b_free[4 + k % 2], fb(4 + k % 2, k // CB, k % CB // 2) + 1)
                    dve.tensor_scalar(hq_b[k % 2], q_f[k % 2], MAGIC, 127.0, ALU.subtract, ALU.min).then_inc(hq_made, 1)
                if c == CB - 2 and n + 1 < NCH:
                    quantise(n + 1)
                if c == CB - 1 and n + 1 < NCH:
                    rounded(n + 1)

        @block.sync
        def _(sp):
            prep_sp(sp)
            attn_sp(sp, 0, NCH)
            xattn_sp(sp)
            moe_sp(sp)
            sp.wait_ge(x_normed, 2 * NCH + 1)
            sp.dma_start(mask_int.rearrange("q (b k) -> q b k", b=NSEQ),
                         a["mask_Bx1xSxS2_if1"].rearrange("b o q k -> q (b o) k")).then_inc(mask_loaded, 16)
            attn_sp(sp, NCH, 3 * NCH)
            ffn_sp(sp)

        @block.tensor
        def _(pe):
            prep_pe(pe)
            pe.wait_ge(const_made, CONSTS)
            pe.wait_ge(prep_done, 2)
            pe.wait_ge(bias_loaded, 16 * 6)
            attn_pe(pe, 0, NCH)
            xattn_pe(pe)
            with pe.Fori(0, NL, 1) as l:
                moe_pe(pe, l)
            build_first(NCH, lambda *b: build_pe(pe, *b))
            attn_pe(pe, NCH, 3 * NCH)
            ffn_pe(pe)

        @block.scalar
        def _(act):
            prep_act(act)
            act.wait_ge(prep_done, 2)
            attn_act(act, 0, NCH)
            xattn_act(act)
            with act.Fori(0, NL, 1) as l:
                moe_act(act, l)
            act.wait_ge(y_ready, NB * NL)
            act.copy(big[:, 8192:16384].rearrange("p (n d) -> p n d", d=D), over(zero_t[:, :], 64)).then_inc(
                zeroed_1, 1)
            build_first(NCH, lambda *b: build_act(act, *b))
            attn_act(act, NCH, 3 * NCH)
            ffn_act(act)

        @block.gpsimd
        def _(pool):
            prep_pool(pool)
            pool.wait_ge(front_loaded, 16 * FRONT)
            attn_pool(pool, 0, NCH)
            moe_pool(pool)
            pool.memset(big[:, 0:8192], 0.0).then_inc(zeroed_0, 1)
            attn_pool(pool, NCH, 3 * NCH)

        @block.vector
        def _(dve):
            link = Chain(dve)
            prep_dve(dve, link)
            dve.wait_ge(const_made, CONSTS)
            attn_dve(dve, link, 0, NCH)
            xattn_dve(dve, link)
            link(dve.memset(small[:, WSEL, :], 1.0))
            dve.wait_ge(pool_step, pool_steps[0] + 8)
            looped(dve, link, lambda l: moe_dve(dve, link, l), NL, MOE_STEPS)
            moe_end_dve(dve, link)
            build_first(NCH, lambda *b: build_dve(dve, *b))
            dve.wait_ge(mask_loaded, 16)
            dve.tensor_scalar(mask_neg.rearrange("p b k -> p (b k)"), mask_int, 0.0, NEG, ALU.is_equal,
                              ALU.mult).then_inc(mask_made, 1)
            attn_dve(dve, link, NCH, 3 * NCH)
            link(dve.memset(scratch_b[:, 0:2112], 0.0))
            link(dve.memset(magic_t, MAGIC))
            ffn_dve(dve, link)


_INS = ["x", "mask_Bx1xSxS2_if1",
        "L0_attn_Wq", "L0_attn_bq", "L0_attn_Wk", "L0_attn_bk", "L0_attn_Wv", "L0_attn_bv", "L0_attn_Wp", "L0_attn_bp",
        "L0_attn_bias_table", "L0_attn_temperature",
        "L0_xattn_bq", "L0_xattn_bk", "L0_xattn_bv", "L0_xattn_be", "L0_ffn_routers", "L0_ffn_W1", "L0_ffn_W2",
        "L1_xattn_bo", "L1_ffn_conv_w", "L1_ffn_conv_b"]
_TURNED = {"x_T": "x", "ctx_T": "ctx_1024"}
for _name in ("L0_xattn_Wq", "L0_xattn_Wk", "L0_xattn_Wv", "L0_xattn_We", "L1_attn_Wq", "L1_attn_Wk", "L1_attn_Wv",
              "L1_attn_Wo", "L1_xattn_Wq", "L1_xattn_Wk", "L1_xattn_Wv", "L1_xattn_Wo", "L1_ffn_w1", "L1_ffn_w2"):
    _TURNED[_name + "_T"] = _name



def kernel(**inputs):
    import numpy as _np
    import concourse.bacc as _bacc
    from concourse import mybir as _mybir
    from concourse.bass_utils import run_bass_kernel_spmd as _run

    nc = _bacc.Bacc("TRN2", target_bir_lowering=False, num_devices=1)
    arrays, args = {}, {}
    laid_out = {name: inputs[name] for name in _INS}
    laid_out.update({new: inputs[name].reshape(-1, inputs[name].shape[-1]).T for new, name in _TURNED.items()})
    for name, arr in laid_out.items():
        arr = _np.ascontiguousarray(arr)
        arrays[f"in_{name}"] = arr
        args[name] = nc.dram_tensor(f"in_{name}", arr.shape, _mybir.dt.from_np(arr.dtype), kind="ExternalInput").ap()
    out = nc.dram_tensor("out_0", (NSEQ, P, D), F32, kind="ExternalOutput").ap()
    decoder(nc, args, out)
    r = _run(nc, [arrays], core_ids=[0])
    return r.results[0]["out_0"]
```

```python
from contextlib import ExitStack

import concourse.bass as bass
from concourse import mybir

F32 = mybir.dt.float32
BF16 = mybir.dt.bfloat16
I32 = mybir.dt.int32
ALU = mybir.AluOpType
ACT = mybir.ActivationFunctionType
AX = mybir.AxisListType

P = 128
D = 128
NSEQ = 16
H = 16
HD = D // H
CB = 4
CT = CB * P
NCH = NSEQ // CB
NIT = NCH // 2
QUADS = H // 4
E = 16
FF = 512
FC = FF // P
NL = 4
HT = NSEQ // 2
NB = HT + E - 1
EPS = 1e-5
MAGIC = 1.5 * 2.0 ** 23
NEG = -2.0 ** 66
RSQRT_SEED = 0x5F3759DF
Q_TERMS = (0, 0, 0, 1, 1, 2)
K_TERMS = (0, 1, 2, 0, 1, 0)


def decoder(nc, a, out):
    ctx = ExitStack()
    with ctx:
        def sb(name, shape, dt=F32):
            return ctx.enter_context(nc.sbuf_tensor(name, shape, dt))

        def sem(name):
            return ctx.enter_context(nc.semaphore(name))

        def sem2(name):
            return [sem(f"{name}{p}") for p in range(2)]

        parts_dram = [[nc.dram_tensor(f"parts_{w}{p}", [3, D, CT], BF16) for w in "qk"] for p in range(2)]
        bias_dram = nc.dram_tensor("bias_rows", [2, 3, 2 * P, H], BF16)
        slots_x = [nc.dram_tensor(f"slots_x{h}", [NB * P, D], F32).ap() for h in range(2)]
        slots_y = [nc.dram_tensor(f"slots_y{h}", [NB * P, D], F32).ap() for h in range(2)]

        big = sb("big", [P, 16384])
        stack = big[:, :].bitcast(BF16).rearrange("p (c w h t) -> p c w h t", c=2, w=2, h=H)
        w1_sb = big[:, 0:8192]
        w2_sb = big[:, 8192:16384]
        scratch_b = sb("scratch_b", [P, 6144])
        scratch_e = sb("scratch_e", [P, 4096])
        bias_sb = scratch_b[:, :].bitcast(BF16).rearrange("p (w n k h) -> p w n h k", w=2, n=3, k=P)
        mask_int = scratch_b[:, 0:2048].bitcast(I32)
        mask_neg = scratch_b[:, 2048:3072].bitcast(BF16).rearrange("p (b k) -> p b k", b=NSEQ)
        tok_x = scratch_b[:, 0:1024].rearrange("p (b d) -> p b d", d=D)
        tok_y = [scratch_b[:, 4096 + 1024 * h:5120 + 1024 * h].rearrange("p (b d) -> p b d", d=D) for h in range(2)]
        probs = [scratch_e[:, 2048 * e:2048 * e + 2048] for e in range(2)]
        mx = sb("mx", [P, 1024])
        mexp = mx[:, :].bitcast(BF16).rearrange("p (h q) -> p h q", h=H)
        vpad = sb("vpad", [P, 2, CB, H, 32])
        chunks = sb("chunks", [P, 8, CT])
        x_all = sb("x_all", [P, NSEQ, D])
        xc = [x_all[:, CB * c:CB * c + CB, :] for c in range(NCH)]
        xt = [chunks[:, p, :] for p in range(2)]
        ct = [chunks[:, 2 + p, :] for p in range(2)]
        f1nat, f2nat = chunks[:, 4, :], chunks[:, 5, :]
        qkp_all = sb("qkp", [P, 2 * 2 * 3 * CT], BF16)
        qkp = qkp_all[:, :].rearrange("p (c w n t) -> p c w n t", c=2, w=2, n=3)
        qkp32 = qkp_all[:, :].bitcast(F32)
        rest = [[sb(f"rest{p}{w}", [P, CT]) for w in range(2)] for p in range(2)]
        osb = [sb(f"osb{e}", [P, CT]) for e in range(2)]
        rden = sb("rden", [P, H])
        onorm = sb("onorm", [P, D])
        oh = sb("oh", [P, D])
        p_t = sb("p_t", [P, CT])
        m_rows = sb("m_rows", [P, H, P], BF16)
        wt = sb("wt", [P, 13, D])
        w0 = sb("w0", [P, 4, D])
        row_bias = sb("row_bias", [P, 3, D])
        f1t = sb("f1t", [P, FF], BF16)
        f2t = sb("f2t", [P, FC, D], BF16)
        ident = sb("ident", [P, P])
        ident_b = sb("ident_b", [P, P], BF16)
        anti_b = sb("anti_b", [P, P], BF16)
        ones = sb("ones", [P, P])
        ones_b = sb("ones_b", [P, P], BF16)
        tri_b = sb("tri_b", [P, P], BF16)
        causal_b = sb("causal_b", [P, P], BF16)
        abias = sb("abias", [P, 6])
        xbias = sb("xbias", [P, 4])
        score_scale = sb("score_scale", [P, 3])
        router_sb = sb("router_sb", [P, NL * E])
        conv_w = sb("conv_w", [P, FC, 3])
        conv_b = sb("conv_b", [P, FC])
        wsc = sb("wsc", [P, 8])
        zero_t = sb("zero_t", [P, D])
        nmax = sb("nmax", [P, H])
        nparts = sb("nparts", [P, P], BF16)
        mt_sb = sb("mt_sb", [P, P], BF16)
        stats = sb("stats", [P, NSEQ, 6])
        lnv = sb("lnv", [P, 4, NSEQ])
        tab = sb("tab", [P, 2, H])
        small = sb("small", [P, 16, NSEQ])
        WT_X, WT_A1, WT_A2 = 0, 5, 9

        bank = [ctx.enter_context(nc.psum_tensor(f"bank{n}", [P, 1024], F32)) for n in range(4)]

        def pb(n):
            return bank[n // 2][:, 512 * (n % 2):512 * (n % 2) + 512]

        table_loaded = sem("table_loaded")
        front_loaded = sem("front_loaded")
        late_loaded = sem("late_loaded")
        const_made = sem("const_made")
        table_ready = sem("table_ready")
        rows_made = sem("rows_made")
        rows_stored = sem("rows_stored")
        bias_loaded = sem("bias_loaded")
        abs_made = sem("abs_made")
        abs_total = sem("abs_total")
        slots_zero = sem("slots_zero")
        zeroed_0 = sem("zeroed_0")
        zeroed_1 = sem("zeroed_1")
        pool_step = sem("pool_step")
        chain = sem("dve_chain")
        x_loaded = sem("x_loaded")
        x_normed = sem("x_normed")
        t_loaded = sem2("t_loaded")
        build_ready = sem("build_ready")
        build_free = sem("build_free")
        part1_made = sem("part1_made")
        part2_made = sem("part2_made")
        parts_made = sem2("parts_made")
        parts_stored = [sem2(f"parts_stored{p}_") for p in range(2)]
        stacked = sem2("stacked")
        bias_added = sem("bias_added")
        s_ready = sem("scores_ready")
        s_free = sem("scores_free")
        nm_ready = sem("nmax_ready")
        mt_ready = sem("mt_ready")
        mt_free = sem("mt_free")
        mexp_ready = sem("mexp_ready")
        st_ready = sem("scores_t_ready")
        exp_done = sem("exp_done")
        av_done = sem("av_done")
        o_copied = sem("o_copied")
        ot_ready = sem("o_turned")
        on_ready = sem("onorm_ready")
        oh_ready = sem("oh_ready")
        oh_made = sem("oh_made")
        proj_ready = sem("proj_ready")
        z_made = sem("z_made")
        mask_loaded = sem("mask_loaded")
        mask_made = sem("mask_made")
        b_ready = [sem(f"bank{b}_filled") for b in range(8)]
        b_free = [sem(f"bank{b}_read") for b in range(8)]
        g_c_loaded = sem2("g_c_loaded")
        out_stored = sem("out_stored")
        nbias_ready = sem("nbias_ready")
        xscale_made = sem("xscale_made")
        xq_scaled = sem("xq_scaled")
        diag_made = sem("diag_made")
        xq_made = sem("xq_made")
        tap_made = sem("tap_made")
        conv_made = sem("conv_made")
        silu_made = sem("silu_made")
        qscale_made = sem("qscale_made")
        hq_made = sem("hq_made")
        w1_loaded = sem("w1_loaded")
        w2_loaded = sem("w2_loaded")
        xturn_ready = sem("xturn_ready")
        xturn_a = sem("xturn_a")
        xturn_d = sem("xturn_d")
        logits_ready = sem("logits_ready")
        shifted = sem("shifted")
        expd = sem("expd")
        onehot_ready = sem("onehot_ready")
        counts_ready = sem("counts_ready")
        pos_ready = sem("pos_ready")
        block_ready = sem("block_ready")
        scattered = sem2("scattered")
        xs_loaded = sem("xs_loaded")
        xsT_ready = sem("xsT_ready")
        xsT_made = sem("xsT_made")
        h_ready = sem("h_ready")
        h_made = sem("h_made")
        w1_copied = sem("w1_copied")
        y_ready = sem("y_ready")
        y_made = sem("y_made")
        y_stored = sem2("y_stored")
        gathered = [sem2(f"gathered{h}_") for h in range(2)]
        tok_made = sem("tok_made")

        block = ctx.enter_context(nc.Block())

        class Chain:

            def __init__(self, eng):
                self.eng, self.base, self.n = eng, 0, 0

            def __call__(self, ins):
                self.n += 1
                ins.then_inc(chain, 1)
                self.eng.wait_ge(chain, self.base + self.n)

        def looped(eng, link, body, count, steps):
            start = link.base + link.n
            with eng.Fori(0, count, 1) as i:
                link.base, link.n = start + i * steps, 0
                body(i)
                assert link.n == steps, (body, link.n, steps)
            link.base, link.n = start + count * steps, 0

        UB = [[1, 1, 2, 1, 1, 1, 1, 1], [1, 1, 2, 2, 2, 2, 4, 4]]

        def ub(b, n, k=0):
            return n * UB[0][b] + k

        def heads(ap):
            return ap.rearrange("p (h q) -> p h q", q=P)

        def four(ap):
            return ap.rearrange("p (b d) -> p b d", b=4)

        def over(ap, n):
            return ap.unsqueeze(1).broadcast_to([P, n, ap.shape[1]])

        def along(ap, n):
            return ap.unsqueeze(2).broadcast_to([P, ap.shape[1], n])

        def weights_of(s):
            base = (0, WT_A1, WT_A2)[s]
            src = w0 if s == 0 else wt
            return [src[:, base + n, :] for n in range(4)]

        BUILD = (("q", "k", "v"), ("x", "q", "k", "v"), ("x", "q", "k", "v"))
        WHEN = {"x": (0, 0), "q": (0, 1), "k": (1, 0), "v": (2, 0)}
        NORMED = (0, 2 * NCH, 3 * NCH)

        def nbuild(n, what):
            s = n // NCH
            return sum(NCH * len(BUILD[k]) for k in range(s)) + len(BUILD[s]) * (n % NCH) + BUILD[s].index(what)

        def build_at(last, g, half, build):
            n, m = g // CB + 1, g % CB
            if n < last:
                for what in BUILD[n // NCH]:
                    if WHEN[what] == (m, half):
                        build(n, what)

        def build_first(n, build):
            for what in BUILD[n // NCH]:
                build(n, what)

        def attn_sp(sp, first, last):
            def load(n):
                s, c, p = n // NCH, n % NCH, n % 2
                if n < last and s != 1:
                    if c >= 2:
                        sp.wait_ge(build_ready, nbuild(n - 2, "v") + 1)
                    sp.dma_start((xt if s == 0 else ct)[p],
                                 a["x_T" if s == 0 else "ctx_T"][:, CT * c:CT * c + CT]).then_inc(t_loaded[p], 16)

            def restack(n):
                p = n % 2
                if n >= 2:
                    sp.wait_ge(stacked[p], 192 * (n // 2))
                for w in range(2):
                    sp.wait_ge(parts_made[p], 2 * (n // 2) + w + 1)
                    sp.dma_start(parts_dram[p][w].ap().rearrange("n d t -> d n t"), qkp[:, p, w, :, :]).then_inc(
                        parts_stored[p][w], 16)
                if n in (0, 1, NCH, NCH + 1):
                    sp.wait_ge((zeroed_0, zeroed_1)[p], 1 if n < NCH else 3)
                if n >= 2:
                    sp.wait_ge(st_ready, 2 * CB * (n - 1))
                for w, terms in ((0, Q_TERMS), (1, K_TERMS)):
                    sp.wait_ge(parts_stored[p][w], 16 * (n // 2) + 16)
                    for r, part in enumerate(terms):
                        sp.dma_start(stack[HD * r:HD * r + HD, p, w, :, :],
                                     parts_dram[p][w].ap()[part].rearrange("(h d) t -> d h t", h=H)).then_inc(
                                         stacked[p], 16)

            if first:
                load(first)
                load(first + 1)
            restack(first)
            if not first:
                sp.dma_start(xt[1], a["x_T"][:, CT:2 * CT]).then_inc(t_loaded[1], 16)
                sp.dma_start(x_all[:, :, :], a["x"].rearrange("b t d -> t b d")).then_inc(x_loaded, 16)
                late_loads(sp)
            for n in range(first + 1, last):
                restack(n)
                load(n + 1)

        def build_pe(pe, n, what):
            s, c, p = n // NCH, n % NCH, n % 2
            wq, wk, wv, _ = weights_of(s)
            if nbuild(n, what):
                pe.wait_ge(build_free, nbuild(n, what))
            if what == "x":
                pe.wait_ge(x_normed, NORMED[s] + c + 1)
                for j in range(CB):
                    mm = pe.transpose(pb(6)[:, P * j:P * j + P], xc[c][:, j, :], ident[:, :])
            elif what == "q":
                if s == 0:
                    pe.wait_ge(t_loaded[p], 16 * (c // 2) + 16)
                mm = pe.matmul(pb(6), wq, xt[p], start=True, stop=True)
            elif what == "k":
                if s == 2:
                    pe.wait_ge(t_loaded[p], 16 * (NIT + c // 2) + 16)
                mm = pe.matmul(pb(6), wk, ct[p] if s == 2 else xt[p], start=True, stop=True)
            else:
                for j in range(CB):
                    mm = pe.matmul(pb(6)[:, P * j:P * j + P], (ct[p] if s == 2 else xt[p])[:, P * j:P * j + P], wv,
                                   start=True, stop=True, skip_group_check=True)
            mm.then_inc(build_ready, 1)

        def build_act(act, n, what):
            s, p = n // NCH, n % 2
            if what == "x":
                act.wait_ge(build_ready, nbuild(n, what) + 1)
                act.copy(xt[p], pb(6)).then_inc(build_free, 1)
            elif what != "v":
                w = "qk".index(what)
                if n >= 2:
                    act.wait_ge(parts_stored[p][w], 16 * (n // 2))
                act.wait_ge(build_ready, nbuild(n, what) + 1)
                act.activation(qkp[:, p, w, 0, :], pb(6), ACT.Identity, bias=abias[:, 2 * s + w:2 * s + w + 1]).then_inc(
                    part1_made, 1)

        def build_dve(dve, n, what):
            s, p = n // NCH, n % 2
            if what == "v":
                dve.wait_ge(build_ready, nbuild(n, what) + 1)
                v = pb(6).rearrange("p (b h d) -> p b h d", b=CB, h=H)
                if n >= 2:
                    dve.wait_ge(av_done, CB * (n - 1))
                if s == 0:
                    for j in range(CB):
                        ins = dve.tensor_tensor(vpad[:, p, j, :, 0:HD], v[:, j],
                                                row_bias[:, 1, :].rearrange("p (h d) -> p h d", h=H), ALU.add)
                else:
                    ins = dve.tensor_copy(vpad[:, p, :, :, 0:HD], v)
                ins.then_inc(build_free, 1)
            elif what != "x":
                w = "qk".index(what)
                dve.wait_ge(part1_made, 2 * n + w + 1)
                if n >= 2:
                    dve.wait_ge(parts_made[p], 2 * (n // 2))
                dve.scalar_tensor_tensor(rest[p][w][:, :], pb(6), abias[:, 2 * s + w:2 * s + w + 1],
                                         qkp[:, p, w, 0, :], ALU.add, ALU.subtract).then_inc(build_free, 1)

        def attn_pool(pool, first, last):
            for n in range(first, last):
                s, c, p = n // NCH, n % NCH, n % 2
                for w in range(2):
                    pool.wait_ge(build_free, nbuild(n, "qk"[w]) + 1)
                    if n >= 2:
                        pool.wait_ge(parts_stored[p][w], 16 * (n // 2))
                    pool.tensor_copy(qkp[:, p, w, 1, :], rest[p][w][:, :]).then_inc(part2_made, 1)
                    pool.wait_ge(part2_made, 2 * n + w + 1)
                    pool.tensor_tensor(qkp[:, p, w, 2, :], rest[p][w][:, :], qkp[:, p, w, 1, :],
                                       ALU.subtract).then_inc(parts_made[p], 1)
                if s != 1:
                    if n == 0:
                        pool.wait_ge(x_loaded, 16)
                    pool.tensor_tensor(xc[c], xc[c], over(row_bias[:, s, :], CB), ALU.add).then_inc(bias_added, 1)

        def attn_pe(pe, first, last, beside=lambda step: None):
            g0, g1 = CB * first, CB * last

            def scores(g, half):
                s, p, j = g // NSEQ, g // CB % 2, g % CB
                if g + half:
                    pe.wait_ge(s_free, 2 * g + half)
                for b in range(2):
                    dst = bank[0][:, 512 * b:512 * b + 512]
                    if s == 0:
                        for n in range(2):
                            m0 = 8 * half + 4 * b
                            pe.matmul(heads(dst), anti_b[:, :], bias_sb[:, 0, n, m0:m0 + 4, :], start=(n == 0),
                                      stop=False, skip_group_check=True)
                    else:
                        row = causal_b[:, :] if s == 1 else mask_neg[:, g % NSEQ, :]
                        pe.matmul(heads(dst), ident_b[:, :], over(row, 4), start=True, stop=False,
                                  skip_group_check=True)
                    for k in range(4):
                        h = 8 * half + 4 * b + k
                        mm = pe.matmul(dst[:, P * k:P * k + P], stack[:, p, 0, h, P * j:P * j + P],
                                       stack[:, p, 1, h, P * j:P * j + P], start=False, stop=(k == 3),
                                       skip_group_check=True)
                mm.then_inc(s_ready, 1)

            def scores_t(g, half):
                s, p, j = g // NSEQ, g // CB % 2, g % CB
                if g + half:
                    pe.wait_ge(exp_done, 2 * g + half)
                for b in range(2):
                    dst = bank[1][:, 512 * b:512 * b + 512]
                    m0 = 8 * half + 4 * b
                    pe.matmul(heads(dst), ones_b[:, :], mexp[:, m0:m0 + 4, :], start=True, stop=False,
                              skip_group_check=True)
                    for k in range(4):
                        h = m0 + k
                        pe.matmul(dst[:, P * k:P * k + P], stack[:, p, 1, h, P * j:P * j + P],
                                  stack[:, p, 0, h, P * j:P * j + P], start=False, stop=False,
                                  skip_group_check=True)
                    if s == 0:
                        for n in range(3):
                            mm = pe.matmul(heads(dst), anti_b[:, :], bias_sb[:, 1, n, m0:m0 + 4, :], start=False,
                                           stop=(n == 2), skip_group_check=True)
                    else:
                        row = causal_b[:, :] if s == 1 else mask_neg[:, g % NSEQ, :]
                        mm = pe.matmul(heads(dst), row, over(ident_b[:, :], 4), start=False, stop=True,
                                       skip_group_check=True)
                mm.then_inc(st_ready, 1)

            for t in range(g0, g1 + 4):
                if t < g1:
                    if t % CB == 0:
                        n = t // CB
                        pe.wait_ge(stacked[n % 2], 192 * (n // 2) + 192)
                        if n == 2 * NCH:
                            pe.wait_ge(mask_made, 1)
                    scores(t, 0)
                if g0 <= t - 1 < g1:
                    pe.wait_ge(mexp_ready, t)
                    scores_t(t - 1, 0)
                build_at(last, t, 0, lambda *b: build_pe(pe, *b))
                if g0 <= t - 4 < g1:
                    g = t - 4
                    pe.wait_ge(on_ready, g + 1)
                    pe.wait_ge(mt_free, min(t, g1))
                    if g:
                        pe.wait_ge(z_made, g)
                    pe.transpose(pb(7)[:, 0:P], onorm[:, :], ident[:, :]).then_inc(oh_ready, 1)
                if t < g1:
                    scores(t, 1)
                if g0 <= t - 1 < g1:
                    scores_t(t - 1, 1)
                if g0 <= t - 4 < g1:
                    g = t - 4
                    pe.wait_ge(oh_made, g + 1)
                    pe.matmul(pb(7)[:, 0:D], oh[:, :], weights_of(g // NSEQ)[3], start=True, stop=True).then_inc(
                        proj_ready, 1)
                if g0 <= t - 3 < g1:
                    g = t - 3
                    pe.wait_ge(o_copied, g + 1)
                    if g:
                        pe.wait_ge(on_ready, g)
                    for q in range(QUADS):
                        mm = pe.transpose(pb(5)[:, P * q:P * q + P], osb[g % 2][:, P * q:P * q + P], ident[:, :])
                    mm.then_inc(ot_ready, 1)
                build_at(last, t, 1, lambda *b: build_pe(pe, *b))
                if t < g1:
                    pe.wait_ge(nm_ready, t + 1)
                    if t >= g0 + 4:
                        pe.wait_ge(z_made, t - 3)
                    elif t:
                        pe.wait_ge(mt_free, t)
                    pe.transpose(pb(7).bitcast(BF16)[:, 0:P], nparts[:, :], ident_b[:, :]).then_inc(mt_ready, 1)
                if g0 <= t - 2 < g1:
                    g = t - 2
                    p, j = g // CB % 2, g % CB
                    pe.wait_ge(exp_done, 2 * g + 2)
                    if g:
                        pe.wait_ge(o_copied, g)
                    pe.wait_ge(build_free, nbuild(g // CB, "v") + 1)
                    for h in range(H):
                        r, q = 32 * (h % 4), h // 4
                        mm = pe.matmul(pb(4)[r:r + 32, P * q:P * q + P], vpad[:, p, j, h, :],
                                       probs[g % 2][:, P * h:P * h + P], start=True, stop=True,
                                       skip_group_check=True)
                    mm.then_inc(av_done, 1)
                beside(t - g0)

        def attn_act(act, first, last, beside=lambda step: None):
            g0, g1 = CB * first, CB * last

            def exp_of(g, half):
                s = g // NSEQ
                act.wait_ge(st_ready, 2 * g + half + 1)
                if g >= 2:
                    act.wait_ge(av_done, g - 1)
                act.activation(probs[g % 2][:, 1024 * half:1024 * half + 1024], bank[1][:, :], ACT.Exp,
                               scale=score_scale[:, s:s + 1]).then_inc(exp_done, 1)

            for t in range(g0, g1 + 4):
                if g0 <= t - 1 < g1:
                    exp_of(t - 1, 0)
                build_at(last, t, 0, lambda *b: build_act(act, *b))
                if g0 <= t - 4 < g1:
                    g = t - 4
                    act.wait_ge(oh_ready, g + 1)
                    if g:
                        act.wait_ge(proj_ready, g)
                    act.copy(oh[:, :], pb(7)[:, 0:P]).then_inc(oh_made, 1)
                if g0 <= t - 1 < g1:
                    exp_of(t - 1, 1)
                build_at(last, t, 1, lambda *b: build_act(act, *b))
                if g0 <= t - 2 < g1:
                    g = t - 2
                    act.wait_ge(av_done, g + 1)
                    if g >= 2:
                        act.wait_ge(ot_ready, g - 1)
                    act.copy(osb[g % 2][:, :], pb(4)).then_inc(o_copied, 1)
                beside(t - g0)

        def ln_begin(dve, link, n):
            v, y, t, m = (lnv[:, k, 0:n] for k in range(4))
            mean_e, mean_o = stats[:, 0:n, 1], stats[:, 0:n, 4]
            link(dve.tensor_tensor(m, mean_e, mean_o, ALU.add))
            link(dve.tensor_scalar(m, m, 0.5, None, ALU.mult))
            link(dve.tensor_tensor(t, mean_e, mean_o, ALU.subtract))
            link(dve.scalar_tensor_tensor(t, t, 0.25, t, ALU.mult, ALU.mult))
            link(dve.tensor_tensor(v, stats[:, 0:n, 2], stats[:, 0:n, 5], ALU.add))
            link(dve.scalar_tensor_tensor(v, v, 1.0 / D, t, ALU.mult, ALU.add))
            link(dve.tensor_scalar(v, v, EPS, None, ALU.add))
            link(dve.tensor_scalar(y.bitcast(I32), v.bitcast(I32), 1, None, ALU.logical_shift_right))
            link(dve.tensor_scalar(y.bitcast(I32), y.bitcast(I32), -1.0, float(RSQRT_SEED), ALU.mult, ALU.add))
            link(dve.tensor_scalar(v, v, -0.5, None, ALU.mult))

        def ln_newton(dve, link, n):
            v, y, t = (lnv[:, k, 0:n] for k in range(3))
            for _ in range(3):
                link(dve.tensor_tensor(t, y, y, ALU.mult))
                link(dve.tensor_tensor(t, t, v, ALU.mult))
                link(dve.scalar_tensor_tensor(y, t, 1.5, y, ALU.add, ALU.mult))

        def ln_scale(dve, link, z, n, dst, m=0):
            for k in range(n):
                ins = dve.tensor_scalar(dst[:, k, :], z[:, k, :], lnv[:, 3, m + k:m + k + 1],
                                        lnv[:, 1, m + k:m + k + 1], ALU.subtract, ALU.mult)
                if k < n - 1:
                    link(ins)
            return ins

        def layernorm(dve, link, z, n, dst):
            ln_begin(dve, link, n)
            ln_newton(dve, link, n)
            return ln_scale(dve, link, z, n, dst)

        def attn_dve(dve, link, first, last, beside=lambda step: None):
            g0, g1 = CB * first, CB * last

            def maximum(g, half):
                dve.wait_ge(s_ready, 2 * g + half + 1)
                dve.tensor_reduce(nmax[:, 8 * half:8 * half + 8], heads(bank[0][:, :]), AX.X, ALU.max,
                                  negate=True).then_inc(s_free, 1)

            def scale_chunk(c):
                ln_scale(dve, link, xc[c], CB, xc[c]).then_inc(x_normed, 1)

            for t in range(g0, g1 + 4):
                if t < g1:
                    maximum(t, 0)
                build_at(last, t, 0, lambda *b: build_dve(dve, *b))
                if t >= g0 + 2 * CB and t % CB == 0:
                    ln_newton(dve, link, CB)
                if t < g1:
                    maximum(t, 1)
                    dve.wait_ge(s_free, 2 * t + 2)
                    link(dve.tensor_copy(nparts[:, 0:H], nmax[:, :]))
                    dve.tensor_tensor(nparts[:, H:2 * H], nmax[:, :], nparts[:, 0:H], ALU.subtract).then_inc(
                        nm_ready, 1)
                if g0 <= t - 4 < g1:
                    g, s, c, j = t - 4, (t - 4) // NSEQ, (t - 4) // CB % NCH, (t - 4) % CB
                    dve.wait_ge(proj_ready, g + 1)
                    if s != 1 and j == 0:
                        dve.wait_ge(bias_added, NCH * (1 if s == 2 else 0) + c + 1)
                    dve.tensor_tensor(xc[c][:, j, :], pb(7)[:, 0:D], xc[c][:, j, :], ALU.add).then_inc(z_made, 1)
                    dve.wait_ge(z_made, g + 1)
                    link(dve.bn_stats(stats[:, j, :], xc[c][:, j, :]))
                if g0 <= t - 3 < g1:
                    g = t - 3
                    ot = pb(5).rearrange("p (h d) -> p h d", d=32)
                    dve.wait_ge(ot_ready, g + 1)
                    link(dve.reciprocal(rden[:, :], ot[:, :, HD]))
                    if g:
                        dve.wait_ge(oh_ready, g)
                    dve.tensor_tensor(onorm[:, :].rearrange("p (h d) -> p h d", h=H), ot[:, :, 0:HD],
                                      along(rden[:, :], HD), ALU.mult).then_inc(on_ready, 1)
                if t < g1:
                    dve.wait_ge(mt_ready, t + 1)
                    dve.tensor_copy(mt_sb[:, :], pb(7).bitcast(BF16)[:, 0:P]).then_inc(mt_free, 1)
                    dve.wait_ge(mt_free, t + 1)
                    if t:
                        dve.wait_ge(st_ready, 2 * t)
                    dve.tensor_tensor(mexp, over(mt_sb[:, :], H), m_rows[:, :, :], ALU.mult).then_inc(mexp_ready, 1)
                build_at(last, t, 1, lambda *b: build_dve(dve, *b))
                if t >= g0 + CB + 3 and (t - 4) % CB == CB - 1:
                    ln_begin(dve, link, CB)
                if t >= g0 + 2 * CB and t % CB == 0:
                    scale_chunk((t // CB - 2) % NCH)
                beside(t - g0)
            ln_newton(dve, link, CB)
            scale_chunk(NCH - 1)

        sel = mx[:, :].rearrange("p (w n j) -> p w n j", w=2, n=2)
        rows32 = p_t[:, 0:4 * H].rearrange("p (w n h) -> p w n h", w=2, n=2)
        rowsr = osb[0][:, 0:4 * H].rearrange("p (w n h) -> p w n h", w=2, n=2)
        rows_b = [p_t[:, 64 + 32 * k:96 + 32 * k].bitcast(BF16).rearrange("p (w n h) -> p w n h", w=2, n=2)
                  for k in range(3)]
        TABLE = 2 * P - 1
        TR = 249

        def prep_sp(sp):
            def load(dst, src, arrived=front_loaded):
                sp.dma_start(dst, src).then_inc(arrived, 16)

            sp.wait_ge(const_made, 2)
            table = a["L0_attn_bias_table"]
            load(tab[:, 0, :], table[0:P, :], table_loaded)
            load(tab[0:TR - P, 1, :], table[P:TR, :], table_loaded)
            load(tab[TR - P:TABLE - P, 1, :], bass.AP(table.tensor, (TR - 1) * H, [[0, TABLE - TR], [1, H]]),
                 table_loaded)
            sp.dma_start(xt[0], a["x_T"][:, 0:CT]).then_inc(t_loaded[0], 16)
            for n, name in enumerate(("Wq", "Wk", "Wv", "Wp")):
                load(w0[:, n, :], a["L0_attn_" + name])
            for n, name in enumerate(("bq", "bk")):
                load(abias[:, n:n + 1], a["L0_attn_" + name].rearrange("(d o) -> d o", o=1))
            for n, name in enumerate(("L0_attn_bp", "L0_attn_bv", "L1_xattn_bo")):
                load(row_bias[:, n, :], bass.AP(a[name].tensor, 0, [[0, P], [1, D]]))
            load(score_scale[:, 0:1], bass.AP(a["L0_attn_temperature"].tensor, 0, [[0, P], [1, 1]]))
            for k in range(3):
                sp.wait_ge(rows_made, k + 1)
                for w in range(2):
                    sp.dma_start(bias_dram.ap()[w, k].rearrange("(n p) h -> p n h", p=P), rows_b[k][:, w]).then_inc(
                        rows_stored, 16)
            sp.wait_ge(rows_stored, 16 * 6)
            for k in range(3):
                for w in range(2):
                    sp.dma_start(scratch_b[:, :].bitcast(BF16)[:, P * H * (3 * w + k):P * H * (3 * w + k + 1)],
                                 bass.AP(bias_dram, (w * 3 + k) * 2 * P * H, [[H, P], [1, P * H]])).then_inc(
                                     bias_loaded, 16)

        def late_loads(sp):
            late_n = [0]

            def late(dst, src):
                late_n[0] += 1
                sp.dma_start(dst, src).then_inc(late_loaded, 16)

            late(f1nat, a["L1_ffn_w1_T"])
            late(f2nat.rearrange("p (c d) -> p c d", c=FC), a["L1_ffn_w2_T"].rearrange("(c p) d -> p c d", p=P))
            for n, name in enumerate(("L0_xattn_Wq", "L0_xattn_Wk", "L0_xattn_Wv")):
                late(wt[:, WT_X + n, :], a[name + "_T"])
            late(wt[:, WT_X + 3:WT_X + 5, :], a["L0_xattn_We_T"].rearrange("(n e) d -> e n d", n=2))
            for n, name in enumerate(("L1_attn_Wq", "L1_attn_Wk", "L1_attn_Wv", "L1_attn_Wo")):
                late(wt[:, WT_A1 + n, :], a[name + "_T"])
            for n, name in enumerate(("L1_xattn_Wq", "L1_xattn_Wk", "L1_xattn_Wv", "L1_xattn_Wo")):
                late(wt[:, WT_A2 + n, :], a[name + "_T"])
            for n, name in enumerate(("bq", "bk", "bv", "be")):
                late(xbias[:, n:n + 1], a["L0_xattn_" + name].rearrange("(d o) -> d o", o=1))
            late(router_sb[:, :].rearrange("d (l e) -> d l e", l=NL), a["L0_ffn_routers"].rearrange("l d e -> d l e"))
            late(conv_w[:, :, :], a["L1_ffn_conv_w"].rearrange("(c p) o k -> p c (o k)", p=P))
            for c in range(FC):
                late(conv_b[:, c:c + 1], a["L1_ffn_conv_b"][P * c:P * c + P].rearrange("(p o) -> p o", o=1))
            assert late_n[0] == LATE

        def prep_act(act):
            build_first(0, lambda *b: build_act(act, *b))
            act.wait_ge(const_made, CONSTS)
            act.copy(big[:, 8192:16384].rearrange("p (n d) -> p n d", d=D), over(zero_t[:, :], 64)).then_inc(
                zeroed_1, 1)

        LATE = 2 + 3 + 1 + 4 + 4 + 4 + 1 + 1 + FC
        FRONT = 4 + 2 + 3 + 1
        CONSTS = 2 + 4 + 4 + 1 + 4

        def prep_pool(pool):
            made = [0]

            def step(ins):
                made[0] += 1
                ins.then_inc(pool_step, 1)
                pool.wait_ge(pool_step, made[0])
                assert made[0] <= PREP_STEPS

            pool.memset(abias[:, :], 0.0).then_inc(const_made, 1)
            pool.memset(tab[:, :, :], 0.0).then_inc(const_made, 1)

            def diagonal(t, pattern, base, cm, fill=1.0, cmp=ALU.not_equal, first=0.0):
                step(pool.memset(t, first))
                return pool.affine_select(out=t, in_=t, compare_op=cmp, fill=fill, base=base, pattern=pattern,
                                          channel_multiplier=cm)

            for n in range(2):
                diagonal(sel[:, 0, n, :], [[1, 256]], P * n - (TABLE - 1), 1).then_inc(const_made, 1)
                diagonal(sel[:, 1, n, :], [[-1, 256]], P * n, 1).then_inc(const_made, 1)
            diagonal(ident[:, :], [[-1, P]], 0, 1).then_inc(const_made, 1)
            pool.memset(ones[:, :], 1.0).then_inc(const_made, 1)
            diagonal(ident_b[:, :], [[-1, P]], 0, 1).then_inc(const_made, 1)
            diagonal(anti_b[:, :], [[1, P]], -(P - 1), 1).then_inc(const_made, 1)
            pool.memset(ones_b[:, :], 1.0).then_inc(const_made, 1)
            step(pool.memset(m_rows[:, :, :], 0.0))
            for n in range(2):
                step(pool.affine_select(out=m_rows[:, :, :], in_=m_rows[:, :, :], compare_op=ALU.not_equal, fill=1.0,
                                        base=-H * n, pattern=[[-1, H], [0, P]], channel_multiplier=1))
            pool.memset(big[:, 0:8192], 0.0).then_inc(zeroed_0, 1)
            diagonal(causal_b[:, :], [[-1, P]], 0, 1, NEG, ALU.is_ge).then_inc(const_made, 1)
            diagonal(tri_b[:, :], [[1, P]], 0, -1, 0.0, ALU.is_gt, 1.0).then_inc(const_made, 1)
            pool.memset(score_scale[:, 1:3], HD ** -0.5).then_inc(const_made, 1)
            pool.memset(zero_t[:, :], 0.0).then_inc(const_made, 1)

        def prep_pe(pe):
            pe.wait_ge(const_made, 6)
            pe.wait_ge(table_loaded, 16 * 3)
            for w in range(2):
                for b in range(2):
                    for n in range(2):
                        m0 = H * (2 * w + b)
                        mm = pe.matmul(pb(0)[:, m0:m0 + H], sel[:, w, n, P * b:P * b + P], tab[:, n, :],
                                       start=(n == 0), stop=(n == 1), skip_group_check=True)
            mm.then_inc(table_ready, 1)
            pe.wait_ge(front_loaded, 16 * FRONT)
            build_first(0, lambda *b: build_pe(pe, *b))

        def ternary_pe(pe, step):
            if step == TERNARY_STEP:
                pe.wait_ge(abs_made, 2)
                pe.wait_ge(build_free, nbuild(NCH, "x"))
                pe.matmul(pb(6)[:, 0:2], ones[:, :], wsc[:, 0:2], start=True, stop=True).then_inc(abs_total, 1)

        def prep_dve(dve, link):
            link(dve.memset(nparts[:, :], 0.0))
            link(dve.memset(vpad[:, :, :, :, :], 0.0))
            link(dve.memset(vpad[:, :, :, :, HD:HD + 1], 1.0))
            dve.wait_ge(table_ready, 1)
            link(dve.tensor_copy(rows32, pb(0)[:, 0:4 * H].rearrange("p (w n h) -> p w n h", w=2, n=2)))
            dve.tensor_copy(rows_b[0], rows32).then_inc(rows_made, 1)
            dve.wait_ge(rows_made, 1)
            link(dve.tensor_tensor(rowsr, rows32, rows_b[0], ALU.subtract))
            dve.tensor_copy(rows_b[1], rowsr).then_inc(rows_made, 1)
            dve.wait_ge(rows_made, 2)
            dve.tensor_tensor(rows_b[2], rowsr, rows_b[1], ALU.subtract).then_inc(rows_made, 1)
            dve.wait_ge(front_loaded, 16 * FRONT)
            build_first(0, lambda *b: build_dve(dve, *b))
            link(dve.tensor_scalar(score_scale[:, 0:1], score_scale[:, 0:1], 0.1, 10.0, ALU.max, ALU.min))
            link(dve.tensor_scalar(score_scale[:, 0:1], score_scale[:, 0:1], float(D) ** 0.5, None, ALU.mult))
            link(dve.reciprocal(score_scale[:, 0:1], score_scale[:, 0:1]))

        TERNARY_STEP = 3 * CB

        def ternary_dve(dve, link, step):
            if step == TERNARY_STEP - 1:
                dve.wait_ge(late_loaded, 16 * LATE)
                for n, f in enumerate((f1nat, f2nat)):
                    dve.tensor_reduce(wsc[:, n:n + 1], f, AX.X, ALU.add, apply_absolute_value=True).then_inc(abs_made, 1)
            if step == TERNARY_STEP:
                dve.wait_ge(abs_total, 1)
                link(dve.tensor_scalar(wsc[:, 2:4], pb(6)[:, 0:2], 1.0 / (D * FF), 1e-5, ALU.mult, ALU.max))
                link(dve.reciprocal(wsc[:, 4:6], wsc[:, 2:4]))
            if step in (TERNARY_STEP + 1, TERNARY_STEP + 2):
                n = step - TERNARY_STEP - 1
                f, t = ((f1nat, f1t[:, :]), (f2nat, f2t[:, :, :].rearrange("p c d -> p (c d)")))[n]
                link(dve.tensor_scalar(f, f, wsc[:, 4 + n:5 + n], MAGIC, ALU.mult, ALU.add))
                link(dve.tensor_scalar(f, f, MAGIC, 1.0, ALU.subtract, ALU.min))
                link(dve.tensor_scalar(t, f, -1.0, None, ALU.max))

        q_t, k_t, v_t, ent_t = rest[0][0][:, :], rest[0][1][:, :], rest[1][1][:, :], rest[1][0][:, :]
        v_tok = [osb[p][:, :] for p in range(2)]
        p_tok, p_turned = p_t[:, :], scratch_e[:, 1024:1536]
        xmax, xsum, xrec = (small[:, 15, CB * k:CB * k + CB] for k in range(3))
        XSCALE = float(D) ** -0.5

        def xattn_sp(sp):
            for n in range(NCH):
                if n >= 2:
                    sp.wait_ge(b_ready[6], ub(6, n - 2) + 1)
                sp.dma_start(ct[n % 2], a["ctx_T"][:, CT * n:CT * n + CT]).then_inc(g_c_loaded[n % 2], 16)
            for h in range(2):
                sp.dma_start(slots_x[h].rearrange("(b p) d -> p b d", p=P), over(zero_t[:, :], NB)).then_inc(
                    slots_zero, 16)

        def xattn_pe(pe, route):
            def fill(b, n, k=0):
                if ub(b, n, k):
                    pe.wait_ge(b_free[b], ub(b, n, k))

            def tokens(n):
                p = n % 2
                pe.wait_ge(x_normed, n + 1)
                fill(2, n)
                for j in range(CB):
                    mm = pe.transpose(pb(2)[:, P * j:P * j + P], xc[n][:, j, :], ident[:, :])
                mm.then_inc(b_ready[2], 1)
                pe.wait_ge(g_c_loaded[p], 16 * (n // 2) + 16)
                fill(3, n)
                pe.matmul(pb(3), wt[:, WT_X + 1, :], ct[p], start=True, stop=True).then_inc(b_ready[3], 1)
                pe.wait_ge(b_free[2], ub(2, n) + 1)
                pe.matmul(pb(2), wt[:, WT_X, :], xt[p], start=True, stop=True).then_inc(b_ready[2], 1)

            def values(n):
                p = n % 2
                fill(4, n)
                pe.matmul(pb(4), wt[:, WT_X + 2, :], ct[p], start=True, stop=True).then_inc(b_ready[4], 1)
                fill(6, n)
                pe.wait_ge(b_free[4], ub(4, n) + 1)
                for j in range(CB):
                    mm = pe.transpose(pb(6)[:, P * j:P * j + P], v_t[:, P * j:P * j + P], ident[:, :])
                mm.then_inc(b_ready[6], 1)

            def entangle(n):
                pe.wait_ge(b_free[3], ub(3, n) + 1)
                fill(5, n)
                pe.matmul(pb(5), wt[:, WT_X + 4, :], k_t, start=True, stop=False)
                pe.wait_ge(b_free[2], ub(2, n, 1) + 1)
                pe.matmul(pb(5), wt[:, WT_X + 3, :], q_t, start=False, stop=True).then_inc(b_ready[5], 1)

            def scores(n):
                pe.wait_ge(b_free[5], ub(5, n) + 1)
                fill(7, n)
                for j in range(CB):
                    mm = pe.matmul(pb(7)[:, P * j:P * j + P], ent_t[:, P * j:P * j + P], v_t[:, P * j:P * j + P],
                                   start=True, stop=True, skip_group_check=True)
                mm.then_inc(b_ready[7], 1)

            def turn_probs(n):
                pe.wait_ge(b_free[7], ub(7, n) + 1)
                fill(1, n)
                for j in range(CB):
                    mm = pe.transpose(pb(1)[:, P * j:P * j + P], p_tok[:, P * j:P * j + P], ident[:, :])
                mm.then_inc(b_ready[1], 1)

            def weigh(n):
                pe.wait_ge(b_free[1], ub(1, n) + 1)
                pe.wait_ge(b_free[6], ub(6, n) + 1)
                fill(0, n)
                for j in range(CB):
                    mm = pe.matmul(pb(0)[:, P * j:P * j + P], p_turned[:, P * j:P * j + P],
                                   v_tok[n % 2][:, P * j:P * j + P], start=True, stop=True, skip_group_check=True)
                mm.then_inc(b_ready[0], 1)

            pe.wait_ge(x_normed, NCH)
            pe.wait_ge(late_loaded, 16 * LATE)
            for n in range(NCH + 1):
                if n < NCH:
                    tokens(n)
                else:
                    for b in (4, 5):
                        pe.wait_ge(b_free[b], ub(b, NCH))
                    route("turn0", "turn1")
                if n >= 1:
                    turn_probs(n - 1)
                if n < NCH:
                    values(n)
                else:
                    route("logits0", "logits1")
                if n >= 1:
                    weigh(n - 1)
                if n < NCH:
                    entangle(n)
                    scores(n)
                else:
                    route("count")

        def xattn_act(act, route):
            for n in range(NCH + 1):
                if n < NCH:
                    act.wait_ge(b_ready[2], ub(2, n) + 1)
                    act.copy(xt[n % 2], pb(2)).then_inc(b_free[2], 1)
                else:
                    route("turn0")
                if n >= 1:
                    act.wait_ge(nbias_ready, n)
                    for j in range(CB):
                        ins = act.activation(p_tok[:, P * j:P * j + P], pb(7)[:, P * j:P * j + P], ACT.Exp,
                                             bias=xmax[:, j:j + 1], scale=XSCALE, accum_out=xsum[:, j:j + 1])
                    ins.then_inc(b_free[7], 1)
                if n < NCH:
                    act.wait_ge(b_ready[2], ub(2, n, 1) + 1)
                    act.activation(q_t, pb(2), ACT.Identity, bias=xbias[:, 0:1]).then_inc(b_free[2], 1)
                    act.wait_ge(b_ready[4], ub(4, n) + 1)
                    act.activation(v_t, pb(4), ACT.Identity, bias=xbias[:, 2:3]).then_inc(b_free[4], 1)
                    act.wait_ge(b_ready[5], ub(5, n) + 1)
                    act.activation(ent_t, pb(5), ACT.Tanh, bias=xbias[:, 3:4]).then_inc(b_free[5], 1)
            route("shift")

        def xattn_dve(dve, link, route):
            for n in range(NCH + 1):
                if n < NCH:
                    dve.wait_ge(b_ready[3], ub(3, n) + 1)
                    dve.tensor_scalar(k_t, pb(3), xbias[:, 1:2], None, ALU.add).then_inc(b_free[3], 1)
                else:
                    route("weigh0", "weigh1", "turn1")
                if n >= 1:
                    dve.wait_ge(b_ready[1], ub(1, n - 1) + 1)
                    dve.tensor_copy(p_turned, pb(1)).then_inc(b_free[1], 1)
                    link(dve.reciprocal(xrec, xsum))
                if n < NCH:
                    dve.wait_ge(b_ready[6], ub(6, n) + 1)
                    dve.tensor_copy(v_tok[n % 2], pb(6)).then_inc(b_free[6], 1)
                if n >= 1:
                    dve.wait_ge(b_ready[0], ub(0, n - 1) + 1)
                    for j in range(CB):
                        ins = dve.scalar_tensor_tensor(xc[n - 1][:, j, :], pb(0)[:, P * j:P * j + P],
                                                       xrec[:, j:j + 1], xc[n - 1][:, j, :], ALU.mult, ALU.add)
                        if j < CB - 1:
                            link(ins)
                    ins.then_inc(b_free[0], 1)
                if n < NCH:
                    dve.wait_ge(b_ready[7], ub(7, n) + 1)
                    link(dve.tensor_reduce(xmax, four(pb(7)), AX.X, ALU.max, negate=True))
                    dve.tensor_scalar(xmax, xmax, XSCALE, None, ALU.mult).then_inc(nbias_ready, 1)
                else:
                    route("shift", "choose", "onehot", "sum", "starts", "slots", "positions", "weight", "compare",
                          "blocks")
                if n >= 1:
                    dve.wait_ge(b_free[0], ub(0, n - 1) + 1)
                    for j in range(CB):
                        link(dve.bn_stats(stats[:, j, :], xc[n - 1][:, j, :]))
                    layernorm(dve, link, xc[n - 1], CB, xc[n - 1]).then_inc(x_normed, 1)

        xt_half = scratch_e[:, 0:HT * P]
        tmps = scratch_e[:, 2048:4096].rearrange("p (n m) -> p n m", n=16)
        shift_sb, exp_sb, cand_sb, cnt_sb, cum_sb, base_sb, rank_sb, iota_e, iota_e64, seg, iota_i = (
            tmps[:, n, :] for n in range(11))
        onehot_b = tmps[:, 11, 0:HT * E // 2].bitcast(BF16)
        w1_block = [qkp32[:, FF * u:FF * u + FF] for u in range(2)]
        hT_sb = [qkp32[:, 2 * FF + FF * u:2 * FF + FF * u + FF] for u in range(2)]
        xs_sb = [rest[g][0][:, :] for g in range(2)]
        xsT_sb = [qkp32[:, 4 * FF + 2 * D + D * u:4 * FF + 2 * D + D * u + D] for u in range(2)]
        ys_sb = [scratch_b[:, 1024:1024 + NB * D], chunks[:, :, :].rearrange("p a b -> p (a b)")]

        def te(ap):
            return ap.rearrange("p (t e) -> p t e", e=E)

        def et(ap):
            return ap.rearrange("p (e t) -> p e t", e=E)

        (LMAX, EMAX, ESUM, EREC, IDX, NEXP, BLK, BEND, BSTART, POS, SEG1, WSEL, _, POSI, _) = range(15)
        GRP = 4
        GROUPS = [(j, min(j + GRP, NB)) for j in range(0, NB, GRP)]
        NG = len(GROUPS)
        assert NG % 2 == 0
        SECTIONS = 2 * NL
        posi = [small[:, POSI + h, 0:HT].bitcast(I32) for h in range(2)]
        blk_tab = sb("blk_tab", [P, 5, NB])
        blocks_i = blk_tab[:, 0, :].bitcast(I32)
        blocks_f = blk_tab[:, 1, :]
        bexp = blk_tab[:, 2, :]
        boff = [blk_tab[:, 3 + h, :].bitcast(I32) for h in range(2)]
        cmp_sb = sb("cmp_sb", [P, NB * E])
        PREP_STEPS = 8 + 2 + 2

        ROUTE = {5: ["weigh0"], 6: ["turn0"], 7: ["weigh1"], 8: ["turn1", "logits0"], 9: ["logits1"], 10: ["shift"],
                 11: ["choose", "onehot"], 12: ["count"], 13: ["sum", "starts"], 14: ["slots"], 15: ["positions"],
                 17: ["weight"], 18: ["compare"], 19: ["blocks"]}
        FINISH = {7: [0], 8: [1], 9: [2], 11: [3], 12: ["begin"], 14: ["newton"], 15: ["scale0"], 16: ["scale1"]}

        def wait_for(eng, semaphore, count):
            if not isinstance(count, int) or count > 0:
                eng.wait_ge(semaphore, count)

        def sections(eng, section):
            section(0, 0, 0)
            with eng.Fori(0, NL - 1, 1) as k:
                section(2 * k + 1, k, 1)
                section(2 * k + 2, k + 1, 0)
            section(SECTIONS - 1, NL - 1, 1)

        def parts_at(s, t):
            return [] if isinstance(s, int) and s == SECTIONS - 1 else ROUTE.get(t, [])

        def moe_sp(sp):
            sp.wait_ge(st_ready, 2 * NSEQ)
            sp.dma_start(w1_sb.rearrange("p (e f) -> p e f", e=E), a["L0_ffn_W1"].rearrange("e d f -> d e f")).then_inc(
                w1_loaded, 16)
            sp.dma_start(w2_sb.rearrange("p (e c d) -> p e c d", e=E, c=FC),
                         a["L0_ffn_W2"].rearrange("e (c p) d -> p e c d", p=P)).then_inc(w2_loaded, 16)

            def store(s, g):
                j0, j1 = GROUPS[g]
                sp.wait_ge(y_made, NB * s + j1)
                sp.dma_start(slots_y[s % 2][P * j0:P * j1, :].rearrange("(b p) d -> p b d", p=P),
                             ys_sb[s % 2][:, D * j0:D * j1].rearrange("p (b d) -> p b d", d=D)).then_inc(y_stored[s % 2], 16)

            def load(s, g):
                j0, j1 = GROUPS[g]
                if g == 0:
                    sp.wait_ge(scattered[s % 2], 16 * HT * (s // 2 + 1))
                if g >= 2:
                    sp.wait_ge(xsT_ready, NB * s + GROUPS[g - 2][1])
                elif s:
                    sp.wait_ge(xsT_ready, NB * (s - 1) + GROUPS[g - 2][1])
                if NG * s + g:
                    sp.wait_ge(xs_loaded, 16 * (NG * s + g))
                sp.dma_start(xs_sb[g % 2][:, 0:D * (j1 - j0)].rearrange("p (b d) -> p b d", d=D),
                             slots_x[s % 2][P * j0:P * j1, :].rearrange("(b p) d -> p b d", p=P)).then_inc(xs_loaded, 16)

            load(0, 0)
            load(0, 1)
            for s in range(SECTIONS):
                for g in range(NG):
                    if g + 2 < NG:
                        load(s, g + 2)
                    elif s + 1 < SECTIONS:
                        load(s + 1, g + 2 - NG)
                    store(s, g)

        def moe_pool(pool):
            def first_x(h):
                for g in range(2):
                    pool.wait_ge(x_normed, NCH + 2 * h + g + 1)
                    pool.dma_start(tok_y[h][:, 4 * g:4 * g + 4, :], xc[2 * h + g]).then_inc(gathered[h][g], 16)

            def scatter(s):
                pool.wait_ge(pos_ready, s + 1)
                for t in range(HT):
                    pool.indirect_dma_start(out=slots_x[s % 2], out_offset=bass.IndirectOffsetOnAxis(
                        ap=posi[s % 2][:, t:t + 1], axis=0), in_=tok_x[:, t, :], in_offset=None).then_inc(
                            scattered[s % 2], 16)

            def gather(s):
                h = s % 2
                pool.wait_ge(y_stored[h], 16 * NG * (s // 2 + 1))
                for t in range(HT):
                    pool.indirect_dma_start(out=tok_y[h][:, t, :], out_offset=None, in_=slots_y[h],
                                            in_offset=bass.IndirectOffsetOnAxis(ap=posi[h][:, t:t + 1], axis=0)).then_inc(
                                                gathered[h][t // 4], 16)

            first_x(0)
            ii = iota_i.bitcast(I32)
            base = PREP_STEPS
            pool.iota(ii, pattern=[[0, HT], [1, E]], base=0, channel_multiplier=0).then_inc(pool_step, 1)
            pool.wait_ge(pool_step, base + 1)
            pool.tensor_copy(iota_e, ii).then_inc(pool_step, 1)
            pool.wait_ge(pool_step, base + 2)
            pool.tensor_scalar(iota_e64, iota_e, 64.0, None, ALU.add).then_inc(pool_step, 1)
            pool.memset(seg, 1.0).then_inc(pool_step, 1)
            pool.wait_ge(pool_step, base + 4)
            pool.memset(et(seg)[:, :, 0:1], 0.0).then_inc(pool_step, 1)
            pool.memset(small[:, SEG1, :], 1.0).then_inc(pool_step, 1)
            pool.wait_ge(pool_step, base + 6)
            pool.iota(blocks_i, pattern=[[1, NB]], base=0, channel_multiplier=0).then_inc(pool_step, 1)
            pool.wait_ge(pool_step, base + 7)
            pool.tensor_copy(blocks_f, blocks_i).then_inc(pool_step, 1)
            pool.wait_ge(slots_zero, 16 * 2)
            scatter(0)
            first_x(1)
            for s in range(SECTIONS):
                if s:
                    gather(s - 1)
                if s + 1 < SECTIONS:
                    scatter(s + 1)
            attn_pool(pool, NCH, NCH + 1)
            gather(SECTIONS - 1)

        def route_pe(pe, s, l, h, part):
            if part in ("turn0", "turn1"):
                g = int(part[-1])
                pe.wait_ge(tok_made, 2 * s + g + 1)
                if g == 0:
                    wait_for(pe, xturn_d, s)
                else:
                    pe.wait_ge(xturn_a, s + 1)
                for j in range(4):
                    mm = pe.transpose(pb(4)[:, P * j:P * j + P], tok_x[:, 4 * g + j, :], ident[:, :])
                mm.then_inc(xturn_ready, 1)
            if part in ("logits0", "logits1"):
                g = int(part[-1])
                pe.wait_ge((xturn_a, xturn_d)[g], s + 1)
                wait_for(pe, pos_ready, s)
                for j in range(4 * g, 4 * g + 4):
                    mm = pe.matmul(pb(5)[:, E * j:E * j + E], xt_half[:, P * j:P * j + P],
                                   router_sb[:, bass.ds(E * l, E)], start=True, stop=True, skip_group_check=True)
                if g == 1:
                    mm.then_inc(logits_ready, 1)
            if part == "count":
                pe.wait_ge(onehot_ready, s + 1)
                pe.matmul(pb(5)[:, 0:HT * E], tri_b[:, :], onehot_b, start=True, stop=True, skip_group_check=True)
                pe.matmul(pb(5)[:, HT * E:2 * HT * E], ones_b[:, :], onehot_b, start=True, stop=True,
                          skip_group_check=True).then_inc(counts_ready, 1)

        def route_act(act, s, part):
            if part == "turn0":
                act.wait_ge(xturn_ready, 2 * s + 1)
                act.copy(xt_half[:, 0:512], pb(4)).then_inc(xturn_a, 1)
            if part == "shift":
                act.wait_ge(shifted, s + 1)
                act.activation(exp_sb, shift_sb, ACT.Exp).then_inc(expd, 1)

        def route_dve(dve, link, s, l, h, part):
            sm = small[:, :, 0:HT]
            se = small
            if part in ("weigh0", "weigh1"):
                g = int(part[-1])
                dve.wait_ge(gathered[h][g], l * (16 * 4) + 16)
                dve.tensor_tensor(tok_x[:, 4 * g:4 * g + 4, :], tok_y[h][:, 4 * g:4 * g + 4, :],
                                  along(sm[:, WSEL + h, 4 * g:4 * g + 4], D), ALU.mult).then_inc(tok_made, 1)
            if part == "turn1":
                dve.wait_ge(xturn_ready, 2 * s + 2)
                dve.tensor_copy(xt_half[:, 512:1024], pb(4)).then_inc(xturn_d, 1)
            if part == "shift":
                dve.wait_ge(logits_ready, s + 1)
                logits = te(pb(5)[:, 0:HT * E])
                link(dve.tensor_reduce(sm[:, LMAX, :], logits, AX.X, ALU.max))
                dve.tensor_tensor(te(shift_sb), logits, along(sm[:, LMAX, :], E), ALU.subtract).then_inc(shifted, 1)
            if part == "choose":
                dve.wait_ge(expd, s + 1)
                link(dve.tensor_reduce(sm[:, EMAX, :], te(exp_sb), AX.X, ALU.max))
                link(dve.tensor_tensor(te(cand_sb), te(exp_sb), along(sm[:, EMAX, :], E), ALU.is_equal))
                link(dve.scalar_tensor_tensor(cand_sb, cand_sb, -64.0, iota_e64, ALU.mult, ALU.add))
            if part == "onehot":
                link(dve.tensor_reduce(sm[:, IDX, :], te(cand_sb), AX.X, ALU.min))
                dve.tensor_tensor(te(onehot_b), te(iota_e), along(sm[:, IDX, :], E), ALU.is_equal).then_inc(
                    onehot_ready, 1)
            if part == "sum":
                dve.wait_ge(counts_ready, s + 1)
                link(dve.tensor_copy(et(cnt_sb), te(pb(5)[:, HT * E:2 * HT * E]).rearrange("p t e -> p e t")))
                link(dve.tensor_tensor_scan(cum_sb, seg, cnt_sb, 0.0, ALU.mult, ALU.add))
            if part == "starts":
                link(dve.tensor_scalar(se[:, NEXP, :], et(cum_sb)[:, :, HT - 1], 1.0 / P,
                                       (P - 1) / P - 0.5 + 0.5 / P, ALU.mult, ALU.add))
                link(dve.tensor_scalar(se[:, NEXP, :], se[:, NEXP, :], MAGIC, None, ALU.add))
                link(dve.tensor_scalar(se[:, BLK, :], se[:, NEXP, :], MAGIC, None, ALU.subtract))
                link(dve.tensor_tensor_scan(se[:, BEND, :], se[:, SEG1, :], se[:, BLK, :], 0.0, ALU.mult, ALU.add))
                link(dve.tensor_tensor(se[:, BSTART, :], se[:, BEND, :], se[:, BLK, :], ALU.subtract))
            if part == "slots":
                link(dve.tensor_tensor(base_sb, cum_sb, cnt_sb, ALU.subtract))
                link(dve.scalar_tensor_tensor(et(base_sb), along(se[:, BSTART, :], HT), float(P), et(base_sb),
                                              ALU.mult, ALU.add))
                link(dve.tensor_tensor(te(rank_sb), te(pb(5)[:, 0:HT * E]), et(base_sb).rearrange("p e t -> p t e"),
                                       ALU.add))
            if part == "positions":
                link(dve.tensor_tensor(rank_sb, rank_sb, onehot_b, ALU.mult))
                link(dve.tensor_reduce(sm[:, POS, :], te(rank_sb), AX.X, ALU.add))
                dve.tensor_copy(posi[h], sm[:, POS, :]).then_inc(pos_ready, 1)
            if part == "weight":
                link(dve.tensor_reduce(sm[:, ESUM, :], te(exp_sb), AX.X, ALU.add))
                link(dve.reciprocal(sm[:, EREC, :], sm[:, ESUM, :]))
                link(dve.tensor_tensor(sm[:, WSEL + h, :], sm[:, EMAX, :], sm[:, EREC, :], ALU.mult))
            if part == "compare":
                link(dve.tensor_tensor(te(cmp_sb[:, :]), over(se[:, BEND, :], NB), along(blocks_f, E), ALU.is_le))
                link(dve.tensor_reduce(bexp, te(cmp_sb[:, :]), AX.X, ALU.add))
            if part == "blocks":
                link(dve.tensor_scalar(bexp, bexp, float(E - 1), float(FF), ALU.min, ALU.mult))
                dve.tensor_copy(boff[h], bexp).then_inc(block_ready, 1)

        ROUTE_STEPS = 1 + 3 + 1 + 2 + 5 + 3 + 2 + 3 + 2 + 1

        def in_flight(s, t, half, lag):
            if isinstance(s, int) and (s == 0 and t < lag or s == SECTIONS - 1 and t - lag >= NB):
                return None
            return NB * s + (t - lag), (t - lag) % NB, half if t >= lag else 1 - half

        def last_steps(s):
            return NB + 2 if isinstance(s, int) and s == SECTIONS - 1 else NB

        def before(b, j):
            return b - min(j, 1)

        def moe_pe(pe, s, l, half):
            pe.wait_ge(block_ready, s + 1)
            for t in range(last_steps(s)):
                if t < NB:
                    b, j, _ = in_flight(s, t, half, 0)
                    if j % GRP == 0:
                        pe.wait_ge(xs_loaded, 16 * (NG * s + j // GRP + 1))
                    wait_for(pe, xsT_made, before(b, j))
                    pe.transpose(pb(j % 2)[:, 0:P], xs_sb[j // GRP % 2][:, D * (j % GRP):D * (j % GRP) + D],
                                 ident[:, :]).then_inc(xsT_ready, 1)
                if in_flight(s, t, half, 1):
                    b, j, _ = in_flight(s, t, half, 1)
                    pe.wait_ge(w1_copied, b + 1)
                    pe.wait_ge(xsT_made, b + 1)
                    wait_for(pe, h_made, before(b, j))
                    for c in range(FC):
                        mm = pe.matmul(pb(2 + j % 2)[:, P * c:P * c + P], w1_block[j % 2][:, P * c:P * c + P],
                                       xsT_sb[j % 2], start=True, stop=True, skip_group_check=True)
                    mm.then_inc(h_ready, 1)
                if in_flight(s, t, half, 2):
                    b, j, h = in_flight(s, t, half, 2)
                    e = pe.value_load(boff[h][0:1, j:j + 1], min_val=0, max_val=(E - 1) * FF)
                    pe.wait_ge(h_made, b + 1)
                    wait_for(pe, y_made, before(b, j))
                    for c in range(FC):
                        mm = pe.matmul(pb(6 + j % 2)[:, 0:D], hT_sb[j % 2][:, P * c:P * c + P],
                                       w2_sb[:, bass.ds(e + P * c, D)], start=(c == 0), stop=(c == FC - 1))
                    mm.then_inc(y_ready, 1)
                for part in parts_at(s, t):
                    route_pe(pe, s + 1, l + half, 1 - half, part)

        def moe_act(act, s, l, half):
            if isinstance(s, int) and s == 0:
                act.wait_ge(w1_loaded, 16)
                act.wait_ge(block_ready, 1)
            for t in range(last_steps(s)):
                if t < NB:
                    b, j, _ = in_flight(s, t, half, 0)
                    e = act.value_load(boff[half][0:1, j:j + 1], min_val=0, max_val=(E - 1) * FF)
                    wait_for(act, h_ready, before(b, j))
                    act.copy(w1_block[j % 2], w1_sb[:, bass.ds(e, FF)]).then_inc(w1_copied, 1)
                if in_flight(s, t, half, 1):
                    b, j, _ = in_flight(s, t, half, 1)
                    if j == 0:
                        wait_for(act, y_ready, b)
                    act.wait_ge(h_ready, b + 1)
                    act.activation(hT_sb[j % 2], pb(2 + j % 2), ACT.Silu).then_inc(h_made, 1)
                if in_flight(s, t, half, 2):
                    b, j, h = in_flight(s, t, half, 2)
                    if t == NB - 1 and parts_at(s, 3):
                        act.wait_ge(block_ready, s + 2)
                    act.wait_ge(y_ready, b + 1)
                    act.copy(ys_sb[h][:, D * j:D * j + D], pb(6 + j % 2)[:, 0:D]).then_inc(y_made, 1)
                for part in parts_at(s, t):
                    route_act(act, s + 1, part)

        def moe_dve(dve, link, s, l, half):
            for t in range(last_steps(s)):
                if t < NB:
                    b, j, _ = in_flight(s, t, half, 0)
                    if j == 0:
                        wait_for(dve, h_ready, b)
                    dve.wait_ge(xsT_ready, b + 1)
                    dve.tensor_copy(xsT_sb[j % 2], pb(j % 2)[:, 0:P]).then_inc(xsT_made, 1)
                for part in parts_at(s, t):
                    route_dve(dve, link, s + 1, l + half, 1 - half, part)
                if isinstance(s, int) and s == SECTIONS - 1:
                    for part in FINISH.get(t, []):
                        finish(dve, link, 0, part)

        def finish(dve, link, h, part):
            if isinstance(part, int):
                dve.wait_ge(gathered[h][part // 2], 16 * 4 * NL + 16)
                for t in (2 * part, 2 * part + 1):
                    row = x_all[:, HT * h + t, :]
                    link(dve.scalar_tensor_tensor(row, tok_y[h][:, t, :], small[:, WSEL + h, t:t + 1], row, ALU.mult,
                                                  ALU.add))
                    link(dve.bn_stats(stats[:, t, :], row))
            elif part == "begin":
                ln_begin(dve, link, HT)
            elif part == "newton":
                ln_newton(dve, link, HT)
            else:
                c = int(part[-1])
                ln_scale(dve, link, xc[2 * h + c], CB, xc[2 * h + c], CB * c).then_inc(x_normed, 1)

        hp = [scratch_b[:, 528 * c:528 * c + 520].rearrange("p (b t) -> p b t", b=CB) for c in range(FC)]
        xq_f, diag = chunks[:, 6, :], chunks[:, 7, :]
        inv_rows = scratch_b[:, 3136:3648]
        hc = [scratch_b[:, 3648 + 512 * n:4160 + 512 * n] for n in range(2)]
        q_f = [scratch_b[:, 4672 + 512 * n:5184 + 512 * n] for n in range(2)]
        magic_t = scratch_b[:, 5700:5701]
        hs = [big[:, 2048 * n:2048 * n + 2048].rearrange("p (c t) -> p c t", c=FC) for n in range(2)]
        xq_b, xqT_b = (chunks[:, 5, 256 * k:256 * k + 256].bitcast(BF16) for k in range(2))
        hq_b = [scratch_e[:, 2560 + 256 * n:2816 + 256 * n].bitcast(BF16) for n in range(2)]
        hqT_b = [scratch_e[:, 3072 + 256 * n:3328 + 256 * n].bitcast(BF16) for n in range(2)]

        FFN_FIRST = -CB - 1
        FFN_PE_ACT, FFN_DVE = NSEQ + 1, NSEQ + 2
        FFN_BESIDE = {2 * NSEQ + 1 + i: FFN_FIRST + i for i in range(2)}
        CLEAR_AT, SCALE_AT, ROUND_AT = 2 * NSEQ - 6, 2 * NSEQ - 4, 2 * NSEQ - 2

        def fb(b, n, k=0):
            return NCH * UB[0][b] + n * UB[1][b] + k

        def ffn_sp(sp):
            for c in range(NCH):
                sp.wait_ge(x_normed, 5 * NCH + c + 1)
                sp.dma_start(out.rearrange("b t d -> t b d")[:, CB * c:CB * c + CB, :], xc[c]).then_inc(out_stored, 16)
            sp.wait_ge(out_stored, 16 * NCH)

        def ffn_pe(pe, steps):
            def turn(k):
                n, j = k // CB, k % CB
                b = 4 + j % 2
                pe.wait_ge(silu_made, FC * n + FC)
                pe.wait_ge(b_free[b], fb(b, n, j // 2))
                for c in range(FC):
                    mm = pe.transpose(pb(b)[:, P * c:P * c + P], hs[n % 2][:, c, P * j:P * j + P], ident[:, :])
                mm.then_inc(b_ready[b], 1)

            def turn_rounded(k):
                n, j = k // CB, k % CB
                pe.wait_ge(hq_made, k + 1)
                pe.wait_ge(b_free[6], fb(6, n, j))
                for c in range(FC):
                    mm = pe.transpose(pb(6).bitcast(BF16)[:, P * c:P * c + P], hq_b[j % 2][:, P * c:P * c + P],
                                      ident_b[:, :])
                mm.then_inc(b_ready[6], 1)

            def bring_down(k):
                n, j = k // CB, k % CB
                pe.wait_ge(b_free[6], fb(6, n, j) + 1)
                pe.wait_ge(b_free[7], fb(7, n, j))
                for c in range(FC):
                    mm = pe.matmul(pb(7)[:, 0:D], hqT_b[j % 2][:, P * c:P * c + P], f2t[:, c, :], start=(c == 0),
                                   stop=(c == FC - 1))
                mm.then_inc(b_ready[7], 1)

            def up_first(n):
                pe.wait_ge(xq_made, n + 1)
                pe.wait_ge(b_free[0], fb(0, n))
                for j in range(CB):
                    mm = pe.transpose(pb(0).bitcast(BF16)[:, P * j:P * j + P], xq_b[:, P * j:P * j + P], ident_b[:, :])
                mm.then_inc(b_ready[0], 1)
                pe.wait_ge(diag_made, n + 1)
                pe.wait_ge(b_free[1], fb(1, n))
                pe.matmul(pb(1), ones[:, :], diag, start=True, stop=True).then_inc(b_ready[1], 1)
                pe.wait_ge(b_free[0], fb(0, n) + 1)

            def up(n, c):
                b = 2 + c % 2
                pe.wait_ge(b_free[b], fb(b, n, c // 2))
                pe.matmul(pb(b), f1t[:, P * c:P * c + P], xqT_b, start=True, stop=True).then_inc(b_ready[b], 1)

            for k in steps:
                n, c = (k + CB + 1) // CB, (k + CB + 1) % CB
                if k == FFN_FIRST:
                    pe.wait_ge(s_free, 2 * 3 * NSEQ)
                    pe.wait_ge(exp_done, 2 * 3 * NSEQ)
                if k == -1:
                    pe.wait_ge(build_free, nbuild(3 * NCH - 1, "v") + 1)
                    pe.wait_ge(o_copied, 3 * NSEQ)
                    pe.wait_ge(on_ready, 3 * NSEQ)
                    pe.wait_ge(z_made, 3 * NSEQ)
                if 0 <= k - 1 < NSEQ:
                    turn_rounded(k - 1)
                if n < NCH and c == 0:
                    up_first(n)
                if n < NCH:
                    up(n, c)
                if 0 <= k + 1 < NSEQ:
                    turn(k + 1)
                if 0 <= k - 1 < NSEQ:
                    bring_down(k - 1)

        def ffn_act_quantise(act, n):
            act.wait_ge(xscale_made, n + 1)
            for j in range(CB):
                ins = act.activation(xq_f[:, P * j:P * j + P], xc[n][:, j, :], ACT.Identity, bias=magic_t,
                                     scale=small[:, 1, j:j + 1])
            ins.then_inc(xq_scaled, 1)
            if n:
                act.wait_ge(b_ready[1], fb(1, n))
            for j in range(CB):
                ins = act.activation(diag[:, P * j:P * j + P], ident[:, :], ACT.Copy, scale=small[:, 2, j:j + 1])
            ins.then_inc(diag_made, 1)

        def ffn_act(act, steps):
            def scaled(k):
                b = 4 + k % 2
                act.wait_ge(qscale_made, k + 1)
                act.activation(q_f[k % 2], pb(b), ACT.Identity, bias=magic_t, scale=small[:, 4 + k % CB, 0:1]).then_inc(
                    b_free[b], 1)

            def turned(k):
                act.wait_ge(b_ready[6], fb(6, 0, k) + 1)
                act.copy(hqT_b[k % 2], pb(6).bitcast(BF16)[:, 0:512]).then_inc(b_free[6], 1)

            for k in steps:
                n, c = (k + CB + 1) // CB, (k + CB + 1) % CB
                if n < NCH and c == 0:
                    act.wait_ge(b_ready[0], fb(0, n) + 1)
                    act.copy(xqT_b, pb(0).bitcast(BF16)[:, 0:512]).then_inc(b_free[0], 1)
                    act.wait_ge(b_ready[1], fb(1, n) + 1)
                    for b in (2, 3):
                        act.wait_ge(b_free[b], fb(b, n))
                    act.copy(inv_rows, pb(1)).then_inc(b_free[1], 1)
                if 0 <= k < NSEQ:
                    scaled(k)
                if 0 <= k - 1 < NSEQ:
                    turned(k - 1)
                if n < NCH:
                    act.wait_ge(b_free[2 + c % 2], fb(2 + c % 2, n, c // 2) + 1)
                    if FC * n + c >= 2:
                        act.wait_ge(silu_made, FC * n + c - 1)
                    act.activation(four(hc[c % 2]), hp[c][:, :, 0:P], ACT.Identity, bias=conv_b[:, c:c + 1],
                                   scale=conv_w[:, c, 0:1]).then_inc(tap_made, 1)
                if 0 <= k + CB < NSEQ:
                    n1, c1 = (k + CB) // CB, (k + CB) % CB
                    act.wait_ge(conv_made, FC * n1 + c1 + 1)
                    act.activation(hs[n1 % 2][:, c1, :], hc[c1 % 2], ACT.Silu).then_inc(silu_made, 1)
                if c == CB - 2 and n + 1 < NCH:
                    ffn_act_quantise(act, n + 1)

        def ffn_dve_quantise(dve, link, n):
            am, sc, inv = small[:, 0, 0:CB], small[:, 1, 0:CB], small[:, 2, 0:CB]
            x = xc[n]
            dve.wait_ge(x_normed, 4 * NCH + n + 1)
            link(dve.tensor_reduce(am, x, AX.X, ALU.max, apply_absolute_value=True))
            link(dve.tensor_scalar(am, am, 1e-5, None, ALU.max))
            link(dve.reciprocal(sc, am))
            link(dve.tensor_scalar(sc, sc, 127.0, None, ALU.mult))
            dve.tensor_scalar(inv, am, 1.0 / 127.0, wsc[:, 2:3], ALU.mult, ALU.mult).then_inc(xscale_made, 1)

        def ffn_dve_rounded(dve, n):
            dve.wait_ge(xq_scaled, n + 1)
            if n:
                dve.wait_ge(b_ready[0], fb(0, n))
            dve.tensor_scalar(xq_b, xq_f, MAGIC, 127.0, ALU.subtract, ALU.min).then_inc(xq_made, 1)

        def ffn_dve(dve, link, steps):
            def residual(k):
                n, j = k // CB, k % CB
                dve.wait_ge(b_ready[7], fb(7, n, j) + 1)
                dve.scalar_tensor_tensor(xc[n][:, j, :], pb(7)[:, 0:D], small[:, 4 + j, 1:2], xc[n][:, j, :],
                                         ALU.mult, ALU.add).then_inc(b_free[7], 1)
                dve.wait_ge(b_free[7], fb(7, n, j) + 1)
                link(dve.bn_stats(stats[:, j, :], xc[n][:, j, :]))
                if j == CB - 1:
                    layernorm(dve, link, xc[n], CB, xc[n]).then_inc(x_normed, 1)

            for k in steps:
                n, c = (k + CB + 1) // CB, (k + CB + 1) % CB
                if 0 <= k < NSEQ:
                    b = 4 + k % 2
                    q = small[:, 4 + k % CB, :]
                    dve.wait_ge(b_ready[b], fb(b, k // CB, k % CB // 2) + 1)
                    link(dve.tensor_reduce(q[:, 2:3], pb(b), AX.X, ALU.max, apply_absolute_value=True))
                    link(dve.tensor_scalar(q[:, 2:3], q[:, 2:3], 1e-5, None, ALU.max))
                    link(dve.reciprocal(q[:, 3:4], q[:, 2:3]))
                    dve.tensor_scalar(q[:, 0:1], q[:, 3:4], 127.0, None, ALU.mult).then_inc(qscale_made, 1)
                    link(dve.tensor_scalar(q[:, 1:2], q[:, 2:3], 1.0 / 127.0, wsc[:, 3:4], ALU.mult, ALU.mult))
                if n < NCH:
                    b = 2 + c % 2
                    if c == 0:
                        dve.wait_ge(b_free[1], fb(1, n) + 1)
                    dve.wait_ge(b_ready[b], fb(b, n, c // 2) + 1)
                    dve.tensor_tensor(hp[c][:, :, 1:P + 1], four(pb(b)), four(inv_rows), ALU.mult).then_inc(b_free[b], 1)
                if 0 <= k + CB < NSEQ:
                    n1, c1 = (k + CB) // CB, (k + CB) % CB
                    t = four(hc[c1 % 2])
                    dve.wait_ge(tap_made, FC * n1 + c1 + 1)
                    link(dve.scalar_tensor_tensor(t, hp[c1][:, :, 1:P + 1], conv_w[:, c1, 1:2], t, ALU.mult, ALU.add))
                    dve.scalar_tensor_tensor(t, hp[c1][:, :, 2:P + 2], conv_w[:, c1, 2:3], t, ALU.mult,
                                             ALU.add).then_inc(conv_made, 1)
                if 0 <= k - 2 < NSEQ:
                    residual(k - 2)
                if 0 <= k < NSEQ:
                    dve.wait_ge(b_free[4 + k % 2], fb(4 + k % 2, k // CB, k % CB // 2) + 1)
                    dve.tensor_scalar(hq_b[k % 2], q_f[k % 2], MAGIC, 127.0, ALU.subtract, ALU.min).then_inc(hq_made, 1)
                if c == CB - 3 and n + 1 < NCH:
                    ffn_dve_quantise(dve, link, n + 1)
                if c == CB - 1 and n + 1 < NCH:
                    ffn_dve_rounded(dve, n + 1)

        @block.sync
        def _(sp):
            prep_sp(sp)
            attn_sp(sp, 0, NCH)
            xattn_sp(sp)
            moe_sp(sp)
            sp.wait_ge(x_normed, 2 * NCH + 1)
            sp.dma_start(mask_int.rearrange("q (b k) -> q b k", b=NSEQ),
                         a["mask_Bx1xSxS2_if1"].rearrange("b o q k -> q (b o) k")).then_inc(mask_loaded, 16)
            attn_sp(sp, NCH, 3 * NCH)
            ffn_sp(sp)

        @block.tensor
        def _(pe):
            prep_pe(pe)
            pe.wait_ge(const_made, CONSTS)
            pe.wait_ge(bias_loaded, 16 * 6)
            attn_pe(pe, 0, NCH, lambda step: ternary_pe(pe, step))
            xattn_pe(pe, lambda *parts: [route_pe(pe, 0, 0, 0, part) for part in parts])
            pe.wait_ge(w1_loaded, 16)
            pe.wait_ge(w2_loaded, 16)
            sections(pe, lambda *at: moe_pe(pe, *at))
            pe.wait_ge(y_made, NB * SECTIONS)
            build_first(NCH, lambda *b: build_pe(pe, *b))

            def beside(step):
                if step in FFN_BESIDE:
                    ffn_pe(pe, [FFN_BESIDE[step]])

            attn_pe(pe, NCH, 3 * NCH, beside)
            ffn_pe(pe, range(max(FFN_BESIDE.values()) + 1, FFN_PE_ACT))

        @block.scalar
        def _(act):
            prep_act(act)
            attn_act(act, 0, NCH)
            xattn_act(act, lambda *parts: [route_act(act, 0, part) for part in parts])
            sections(act, lambda *at: moe_act(act, *at))
            build_first(NCH, lambda *b: build_act(act, *b))
            act.wait_ge(w1_copied, NB * SECTIONS)
            act.copy(big[:, 4096:8192].rearrange("p (n d) -> p n d", d=D), over(zero_t[:, :], 32)).then_inc(zeroed_0, 1)
            act.wait_ge(y_ready, NB * SECTIONS)
            act.copy(big[:, 12288:16384].rearrange("p (n d) -> p n d", d=D), over(zero_t[:, :], 32)).then_inc(
                zeroed_1, 1)

            def beside(step):
                if step == ROUND_AT - 1:
                    ffn_act_quantise(act, 0)
                if step in FFN_BESIDE:
                    ffn_act(act, [FFN_BESIDE[step]])

            attn_act(act, NCH, 3 * NCH, beside)
            ffn_act(act, range(max(FFN_BESIDE.values()) + 1, FFN_PE_ACT))

        @block.gpsimd
        def _(pool):
            prep_pool(pool)
            pool.wait_ge(front_loaded, 16 * FRONT)
            attn_pool(pool, 0, NCH)
            moe_pool(pool)
            attn_pool(pool, NCH + 1, 3 * NCH)

        @block.vector
        def _(dve):
            link = Chain(dve)
            prep_dve(dve, link)
            dve.wait_ge(const_made, CONSTS)
            attn_dve(dve, link, 0, NCH, lambda step: ternary_dve(dve, link, step))
            link(dve.memset(small[:, WSEL:WSEL + 2, :], 1.0))

            def route_first(*parts):
                if "weigh0" in parts:
                    dve.wait_ge(pool_step, PREP_STEPS + 8)
                for part in parts:
                    route_dve(dve, link, 0, 0, 0, part)

            xattn_dve(dve, link, route_first)
            moe_dve(dve, link, 0, 0, 0)

            def two_sections(k):
                moe_dve(dve, link, 2 * k + 1, k, 1)
                moe_dve(dve, link, 2 * k + 2, k + 1, 0)

            looped(dve, link, two_sections, NL - 1, 2 * ROUTE_STEPS)
            moe_dve(dve, link, SECTIONS - 1, NL - 1, 1)
            dve.wait_ge(w1_copied, NB * SECTIONS)
            dve.memset(big[:, 0:4096], 0.0).then_inc(zeroed_0, 1)
            build_first(NCH, lambda *b: build_dve(dve, *b))
            dve.wait_ge(y_ready, NB * SECTIONS)
            dve.memset(big[:, 8192:12288], 0.0).then_inc(zeroed_1, 1)

            def beside(step):
                for part in {1: [0, 1], 2: [2, 3, "begin"], 3: ["newton", "scale0"], 4: ["scale1"]}.get(step, []):
                    finish(dve, link, 1, part)
                if step == 6:
                    dve.wait_ge(mask_loaded, 16)
                    dve.tensor_scalar(mask_neg.rearrange("p b k -> p (b k)"), mask_int, 0.0, NEG, ALU.is_equal,
                                      ALU.mult).then_inc(mask_made, 1)
                if step == CLEAR_AT:
                    dve.wait_ge(st_ready, 2 * (2 * NSEQ + 1))
                    link(dve.memset(scratch_b[:, 0:2112], 0.0))
                    link(dve.memset(magic_t, MAGIC))
                if step == SCALE_AT:
                    ffn_dve_quantise(dve, link, 0)
                if step == ROUND_AT:
                    ffn_dve_rounded(dve, 0)
                if step in FFN_BESIDE:
                    ffn_dve(dve, link, [FFN_BESIDE[step]])

            attn_dve(dve, link, NCH, 3 * NCH, beside)
            ffn_dve(dve, link, range(max(FFN_BESIDE.values()) + 1, FFN_DVE))


_INS = ["x", "mask_Bx1xSxS2_if1",
        "L0_attn_Wq", "L0_attn_bq", "L0_attn_Wk", "L0_attn_bk", "L0_attn_Wv", "L0_attn_bv", "L0_attn_Wp", "L0_attn_bp",
        "L0_attn_bias_table", "L0_attn_temperature",
        "L0_xattn_bq", "L0_xattn_bk", "L0_xattn_bv", "L0_xattn_be", "L0_ffn_routers", "L0_ffn_W1", "L0_ffn_W2",
        "L1_xattn_bo", "L1_ffn_conv_w", "L1_ffn_conv_b"]
_TURNED = {"x_T": "x", "ctx_T": "ctx_1024"}
for _name in ("L0_xattn_Wq", "L0_xattn_Wk", "L0_xattn_Wv", "L0_xattn_We", "L1_attn_Wq", "L1_attn_Wk", "L1_attn_Wv",
              "L1_attn_Wo", "L1_xattn_Wq", "L1_xattn_Wk", "L1_xattn_Wv", "L1_xattn_Wo", "L1_ffn_w1", "L1_ffn_w2"):
    _TURNED[_name + "_T"] = _name


def kernel(**inputs):
    import numpy as _np
    import concourse.bacc as _bacc
    from concourse import mybir as _mybir
    from concourse.bass_utils import run_bass_kernel_spmd as _run

    nc = _bacc.Bacc("TRN2", target_bir_lowering=False, num_devices=1)
    arrays, args = {}, {}
    laid_out = {name: inputs[name] for name in _INS}
    laid_out.update({new: inputs[name].reshape(-1, inputs[name].shape[-1]).T for new, name in _TURNED.items()})
    for name, arr in laid_out.items():
        arr = _np.ascontiguousarray(arr)
        arrays[f"in_{name}"] = arr
        args[name] = nc.dram_tensor(f"in_{name}", arr.shape, _mybir.dt.from_np(arr.dtype), kind="ExternalInput").ap()
    out = nc.dram_tensor("out_0", (NSEQ, P, D), F32, kind="ExternalOutput").ap()
    decoder(nc, args, out)
    r = _run(nc, [arrays], core_ids=[0])
    return r.results[0]["out_0"]
```
